# Optimizing a Trainium2 kernel written in Bass

```python
import numpy as np
import jax
import jax.numpy as jnp

def _softmax(x, axis=-1):
    return jax.nn.softmax(x, axis=axis)

def _gelu(x):
    return jax.nn.gelu(x, approximate=True)

def _silu(x):
    return jax.nn.silu(x)

def _sigmoid(x):
    return jax.nn.sigmoid(x)

def _layernorm(x, axis=-1, eps=1e-05):
    m = jnp.mean(x, axis=axis, keepdims=True)
    v = jnp.var(x, axis=axis, keepdims=True)
    return (x - m) / jnp.sqrt(v + eps)

def _scatter_add(tgt, idx, src, axis=0):
    return tgt.at[idx].add(src)

def _segment_sum(src, seg, n):
    return jax.ops.segment_sum(src, seg, n)
kernel_name = 'mk_adaln_d1_jaxref_r8_dc4506'

def setup_inputs(seed: int=0):
    np.random.seed(seed)
    _w = jnp.asarray

    def _L0_attn_setup():
        import jax, jax.numpy as jnp
        import numpy as np
        HEADS = 16
        KV_HEADS = 4
        DIM_HEAD = 128
        DIM = 256
        ROPE_BASE = 10000.0

        def rotate_half(t):
            t1, t2 = jnp.split(t, 2, axis=-1)
            return jnp.concatenate((-t2, t1), axis=-1)

        def apply_rotary(t, cos, sin):
            return t * cos + rotate_half(t) * sin
        key = jax.random.key(seed)
        ks = jax.random.split(key, 6)
        b, n = (4, 128)
        s = 1.0 / np.sqrt(DIM)
        x = jax.random.normal(ks[0], (b, n, DIM), dtype=jnp.float32)
        Wq = jax.random.normal(ks[1], (DIM, HEADS * DIM_HEAD), dtype=jnp.float32) * s
        Wk = jax.random.normal(ks[2], (DIM, KV_HEADS * DIM_HEAD), dtype=jnp.float32) * s
        Wv = jax.random.normal(ks[3], (DIM, KV_HEADS * DIM_HEAD), dtype=jnp.float32) * s
        Wo = jax.random.normal(ks[4], (HEADS * DIM_HEAD, DIM), dtype=jnp.float32) * s
        head_scale = 1.0 + 0.02 * jax.random.normal(ks[5], (1, HEADS, 1, 1), dtype=jnp.float32)
        return {'x': x, 'Wq': Wq, 'Wk': Wk, 'Wv': Wv, 'Wo': Wo, 'head_scale': head_scale}
    _L0_attn_in = _L0_attn_setup()

    def _L0_ffn_setup():
        import jax, jax.numpy as jnp
        import numpy as np
        TOP_K = 4
        key = jax.random.key(seed)
        ks = jax.random.split(key, 5)
        H, I, E = (256, 96, 32)
        s = 0.02
        return {'hidden_states': jax.random.normal(ks[0], (1, 128, H), jnp.float32), 'router_w': jax.random.normal(ks[1], (E, H), jnp.float32) * s, 'gate_w': jax.random.normal(ks[2], (E, I, H), jnp.float32) * s, 'up_w': jax.random.normal(ks[3], (E, I, H), jnp.float32) * s, 'down_w': jax.random.normal(ks[4], (E, H, I), jnp.float32) * s}
    _L0_ffn_in = _L0_ffn_setup()
    _L0_c = _w((lambda *s: np.random.randn(*s).astype(np.float32) * 0.05)(4, 256))
    _L0_wmod = _w((lambda *s: np.random.randn(*s).astype(np.float32) * 0.05)(256, 6 * 256) * 256 ** (-0.5))
    _d = {'L0_attn_x': _L0_attn_in['x'], 'L0_attn_Wq': _L0_attn_in['Wq'], 'L0_attn_Wk': _L0_attn_in['Wk'], 'L0_attn_Wv': _L0_attn_in['Wv'], 'L0_attn_Wo': _L0_attn_in['Wo'], 'L0_attn_head_scale': _L0_attn_in['head_scale'], 'L0_ffn_router_w': _L0_ffn_in['router_w'], 'L0_ffn_gate_w': _L0_ffn_in['gate_w'], 'L0_ffn_up_w': _L0_ffn_in['up_w'], 'L0_ffn_down_w': _L0_ffn_in['down_w'], 'L0_c': _L0_c, 'L0_wmod': _L0_wmod}
    _x0 = _d['L0_attn_x']
    _d['L0_attn_x'] = jax.random.normal(jax.random.fold_in(jax.random.key(seed), 1), (4, 1024, 256), dtype=_x0.dtype)
    del _x0
    return _d

def reference(L0_attn_x, L0_attn_Wq, L0_attn_Wk, L0_attn_Wv, L0_attn_Wo, L0_attn_head_scale, L0_ffn_router_w, L0_ffn_gate_w, L0_ffn_up_w, L0_ffn_down_w, L0_c, L0_wmod):

    def _L0_attn_ref(x, Wq, Wk, Wv, Wo, head_scale):
        import jax, jax.numpy as jnp
        import numpy as np
        HEADS = 16
        KV_HEADS = 4
        DIM_HEAD = 128
        DIM = 256
        ROPE_BASE = 10000.0

        def rotate_half(t):
            t1, t2 = jnp.split(t, 2, axis=-1)
            return jnp.concatenate((-t2, t1), axis=-1)

        def apply_rotary(t, cos, sin):
            return t * cos + rotate_half(t) * sin
        b, n, _ = x.shape
        q = (x @ Wq).reshape(b, n, HEADS, DIM_HEAD).transpose(0, 2, 1, 3)
        k = (x @ Wk).reshape(b, n, KV_HEADS, DIM_HEAD).transpose(0, 2, 1, 3)
        v = (x @ Wv).reshape(b, n, KV_HEADS, DIM_HEAD).transpose(0, 2, 1, 3)
        inv_freq = 1.0 / ROPE_BASE ** (jnp.arange(0, DIM_HEAD, 2, dtype=jnp.float32) / DIM_HEAD)
        freqs = jnp.arange(n, dtype=jnp.float32)[:, None] * inv_freq[None, :]
        emb = jnp.concatenate((freqs, freqs), axis=-1)
        cos, sin = (jnp.cos(emb), jnp.sin(emb))
        q = apply_rotary(q, cos, sin)
        k = apply_rotary(k, cos, sin)
        rep = HEADS // KV_HEADS
        k = jnp.repeat(k, rep, axis=1)
        v = jnp.repeat(v, rep, axis=1)
        scale = 1.0 / jnp.sqrt(jnp.array(DIM_HEAD, dtype=x.dtype))
        scores = jnp.einsum('bhid,bhjd->bhij', q, k) * scale
        causal = jnp.tril(jnp.ones((n, n), dtype=bool))
        scores = jnp.where(causal, scores, jnp.finfo(scores.dtype).min)
        attn = jax.nn.softmax(scores, axis=-1)
        out = jnp.einsum('bhij,bhjd->bhid', attn, v)
        out = out * head_scale
        out = out.transpose(0, 2, 1, 3).reshape(b, n, HEADS * DIM_HEAD)
        return out @ Wo

    def _L0_ffn_ref(hidden_states, router_w, gate_w, up_w, down_w):
        import jax, jax.numpy as jnp
        import numpy as np
        TOP_K = 4
        B, S, H = hidden_states.shape
        E = router_w.shape[0]
        x = hidden_states.reshape(-1, H)
        logits = x @ router_w.T
        probs = jax.nn.softmax(logits.astype(jnp.float32), axis=-1)
        rw, sel = jax.lax.top_k(probs, TOP_K)
        rw = rw / jnp.sum(rw, axis=-1, keepdims=True)
        rw = rw.astype(x.dtype)

        def body(acc, expert):
            gw, uw, dw, e = expert
            w_tok = jnp.sum(jnp.where(sel == e, rw, 0.0), axis=-1)
            h = jax.nn.silu(x @ gw.T) * (x @ uw.T)
            y = h @ dw.T
            return (acc + w_tok[:, None] * y, None)
        acc0 = jnp.zeros_like(x)
        out, _ = jax.lax.scan(body, acc0, (gate_w, up_w, down_w, jnp.arange(E)))
        return out.reshape(B, S, H)
    x = L0_attn_x
    mod = (_silu(L0_c) @ L0_wmod).reshape(L0_c.shape[0], 6, 1, -1)
    sa, ca, ga, sb, cb, gb = (mod[:, 0], mod[:, 1], mod[:, 2], mod[:, 3], mod[:, 4], mod[:, 5])
    ga = (2 * (ga >= 0) - 1) * jnp.maximum(jnp.abs(ga), 0.25)
    gb = (2 * (gb >= 0) - 1) * jnp.maximum(jnp.abs(gb), 0.25)
    h = _layernorm(x, axis=-1) * (1 + ca) + sa
    x = x + ga * _L0_attn_ref(h, L0_attn_Wq, L0_attn_Wk, L0_attn_Wv, L0_attn_Wo, L0_attn_head_scale)
    h = _layernorm(x, axis=-1) * (1 + cb) + sb
    x = x + gb * _L0_ffn_ref(h, L0_ffn_router_w, L0_ffn_gate_w, L0_ffn_up_w, L0_ffn_down_w)
    return x

_drawn_inputs = setup_inputs


def setup_inputs(seed=0):
    import zlib

    import numpy as np

    out = dict(_drawn_inputs(seed))
    spreads = {}
    factors = {'L0_attn_head_scale': 8.0,
     'L0_ffn_router_w': 8.0,
     'L0_ffn_gate_w': 8.0,
     'L0_ffn_up_w': 8.0,
     'L0_ffn_down_w': 8.0}
    for name, (base, spread) in spreads.items():
        noise = np.random.default_rng([zlib.crc32(name.encode()), seed]).standard_normal(out[name].shape)
        drawn = base * np.exp(spread * noise) if base else spread * noise
        out[name] = jnp.asarray(drawn.astype(out[name].dtype))
    for name, factor in factors.items():
        out[name] = (out[name] * factor).astype(out[name].dtype)
    return out
```

```python
from contextlib import ExitStack

import concourse.bass as bass
from concourse import mybir

ALU = mybir.AluOpType
ACT = mybir.ActivationFunctionType
AX_X = mybir.AxisListType.X
F32 = mybir.dt.float32
F32R = mybir.dt.float32r
BF16 = mybir.dt.bfloat16
U32 = mybir.dt.uint32

P = 128
B, N, D = 4, 1024, 256
H, KV, DH = 16, 4, 128
G = H // KV
T = N // P
KD = D // P
CH = 4
CW = CH * P
NTILE = KV * T
UNITS = KV * (T // CH)
WQ = (G + 2) * DH
WG = KD * WQ + G * D
KCOL, VCOL = G * DH, (G + 1) * DH
EPS = 1e-5
ONE = 1

PROJ = ["K", "V", "Q0", "Q1", "Q2", "Q3"]


def misc_order():
    order = [(p, 0) for p in PROJ]
    for n in range(NTILE):
        if n:
            order.append(("Y", n - 1))
        order += [(p, n // CH + 1) for p in projected_in(n)]
        order.append(("R", n))
    order.append(("Y", NTILE - 1))
    return {what: k for k, what in enumerate(order)}


def projected_in(n):
    if n // CH + 1 >= UNITS or n % CH == CH - 1:
        return []
    return PROJ[2 * (n % CH):2 * (n % CH) + 2]


MISC = misc_order()
NMISC = len(MISC)
NROT = UNITS * (G + 1)
NPT = T + KV * T * (T + 1) // 2
NPV = NPT - T
NS = NTILE * G


def rot_index(p, unit):
    return unit * (G + 1) + (0 if p == "K" else 1 + int(p[1]))


def pt_index(n, j):
    kv, i = divmod(n, T)
    return T + kv * T * (T + 1) // 2 + i * (i + 1) // 2 + j


def scores_at(n, j):
    nj = n % T + 1
    return [h for h in range(G) if h * nj // G == j] if n + 1 < NTILE else []


def attention(nc, x, wq, wk, wv, wo, hscale, c, wmod, cos, sin, ident, causal, rows_dram, modp, wsplit, x1, ident_sb):
    with ExitStack() as ctx:
        def sb(name, shape, dt=F32):
            return ctx.enter_context(nc.sbuf_tensor(name, shape, dt))

        def sem(name):
            return ctx.enter_context(nc.semaphore(name))

        wbuf = sb("wbuf", [P, 2, 2, WG], F32R)
        kbuf = sb("kbuf", [P, 2, 2, N], F32R)
        vbuf = sb("vbuf", [P, 2, 2, T, DH], F32R)
        qbuf = sb("qbuf", [P, 2, 2, G, CW], F32R)
        ht = sb("ht", [P, 2, KD, N], F32R)
        probs = sb("probs", [P, 2, G, N])
        pt = sb("pt", [P, 2, 2, G * P], F32R)
        cos_sb = sb("cos_sb", [P, N])
        sin_sb = sb("sin_sb", [P, N])
        raw = sb("raw", [P, 2, CW])
        swapped = sb("swapped", [P, 2, CW])
        rot = sb("rot", [P, 2, CW])
        r_sb = sb("r_sb", [P, G * P])
        o_f = sb("o_f", [P, G * P])
        o_r = sb("o_r", [P, 2, G * P], F32R)
        xacc = sb("xacc", [P, T, D])
        ytmp = sb("ytmp", [P, 2, D])
        z = ytmp
        hf = r_sb[:].rearrange("p (s k t) -> p s k t", s=2, k=KD)
        ga = sb("ga", [P, B, D])
        causal_sb = sb("causal_sb", [P, P], BF16)
        identb_sb = sb("identb_sb", [P, P], BF16)
        hs_sb = sb("hs_sb", [P, H])
        stats = sb("stats", [P, T, 6])
        mv = sb("mv", [P, T, 2])
        rstd = sb("rstd", [P, 2, T])
        mhalf = sb("mhalf", [P, T])
        eps = sb("eps", [P, T])
        mark = sb("mark", [P, 1])
        negmax = sb("negmax", [P, 4])
        lsum = sb("lsum", [P, 2, G])
        linv = sb("linv", [P, 2, G])
        rrow = sb("rrow", [P, 2, G])

        s_ps = ctx.enter_context(nc.psum_tensor("s_ps", [P, 2, N], F32))
        pt_ps = ctx.enter_context(nc.psum_tensor("pt_ps", [P, 2, 512], F32))
        o_ps = ctx.enter_context(nc.psum_tensor("o_ps", [P, 512], F32))
        misc = ctx.enter_context(nc.psum_tensor("misc", [P, 512], F32))

        prepare(nc, ctx, sb, sem, wq, wk, wv, wo, hscale, c, wmod, cos, sin, ident, causal, wsplit,
                probs, wbuf, cos_sb, sin_sb, causal_sb, identb_sb, hs_sb, mhalf, eps, ident_sb, ga, rows_dram, modp,
                xacc, raw, swapped, rot, o_f, o_ps, misc)

        w_loaded = [sem("w_loaded0"), sem("w_loaded1")]
        x_loaded = sem("x_loaded")
        x1_stored = sem("x1_stored")
        stats_done = sem("stats_done")
        mean_done = sem("mean_done")
        var_eps = sem("var_eps")
        rstd_done = sem("rstd_done")
        z_done = sem("z_done")
        pt_filled = sem("pt_filled")
        pt_emptied = sem("pt_emptied")
        pthi_done = sem("pthi_done")
        hhi_done = sem("hhi_done")
        hlo_done = sem("hlo_done")
        misc_filled = sem("misc_filled")
        misc_emptied = sem("misc_emptied")
        swap_done = [sem("swap_done0"), sem("swap_done1")]
        cos_done = sem("cos_done")
        sin_done = sem("sin_done")
        rot_done = sem("rot_done")
        rothi_done = sem("rothi_done")
        rotlo_done = sem("rotlo_done")
        vhi_done = sem("vhi_done")
        scores_done = sem("scores_done")
        max_done = sem("max_done")
        probs_done = sem("probs_done")
        pv_done = sem("pv_done")
        linv_done = sem("linv_done")
        rrow_done = sem("rrow_done")
        o_done = sem("o_done")
        ohi_done = sem("ohi_done")
        olo_done = sem("olo_done")
        y_done = sem("y_done")
        acc_done = sem("acc_done")

        f32 = lambda ap: ap.bitcast(F32)

        def wqkv(par, half, k, col, width):
            return wbuf[:, par, half, k * WQ + col:k * WQ + col + width]

        def wo_part(par, half, h):
            return wbuf[:, par, half, KD * WQ + h * D:KD * WQ + (h + 1) * D]

        def rot_dest(p, unit, half):
            kv, c = divmod(unit, T // CH)
            if p == "K":
                return kbuf[:, kv % 2, half, c * CW:(c + 1) * CW]
            return qbuf[:, unit % 2, half, int(p[1]), :]

        block = ctx.enter_context(nc.Block())

        @block.sync
        def _(sp):
            for started in (x1_stored,):
                sp.sem_inc(started, ONE)
            for g in range(2):
                sp.dma_start(wbuf[:, g].rearrange("p s w -> p (s w)").bitcast(F32), wsplit[g]).then_inc(w_loaded[g], 16)
            with sp.Fori(0, B) as b:
                sp.wait_ge(x1_stored, ONE + b * 16)
                sp.dma_start(xacc[:], x[bass.ds(b, 1), :, :].rearrange("o (t p) d -> p (o t) d", p=P)).then_inc(x_loaded, 16)

                def swap(p, unit):
                    r = rot_index(p, unit)
                    sp.wait_ge(misc_emptied, ONE + b * NMISC + MISC[(p, unit)] + 1)
                    sp.dma_start(swapped[0:64, r % 2, :], raw[64:128, r % 2, :]).then_inc(swap_done[r % 2], 16)
                    sp.dma_start(swapped[64:128, r % 2, :], raw[0:64, r % 2, :]).then_inc(swap_done[r % 2], 16)

                for p in PROJ:
                    if p != "V":
                        swap(p, 0)
                for n in range(NTILE):
                    if n and n % T == 0:
                        reload(sp, b, n // T - 1, misc_filled, w_loaded, wbuf, wsplit)
                    for p in projected_in(n):
                        if p != "V":
                            swap(p, n // CH + 1)
                reload(sp, b, KV - 1, misc_filled, w_loaded, wbuf, wsplit)
                sp.wait_ge(acc_done, ONE + b * NTILE + NTILE)
                sp.dma_start(x1[bass.ds(b, 1), :, :].rearrange("o (t p) d -> p (o t) d", p=P), xacc[:]).then_inc(x1_stored, 16)
            sp.wait_ge(x1_stored, ONE + 16 * B)
            for g in range(2):
                sp.wait_ge(w_loaded[g], 16 * (1 + 2 * B))

        @block.tensor
        def _(pe):
            for started in (pv_done, pt_filled,):
                pe.sem_inc(started, ONE)
            def three(out, a, w, start, stop):
                pe.matmul(out, a(0), w(0), start=start, stop=False)
                pe.matmul(out, a(0), w(1), start=False, stop=False)
                return pe.matmul(out, a(1), w(0), start=False, stop=stop)

            with pe.Fori(0, B) as b:
                def fill_misc(what, unit):
                    m = MISC[(what, unit)]
                    pe.wait_ge(misc_emptied, ONE + b * NMISC + m)

                def project(p, unit):
                    kv, c = divmod(unit, T // CH)
                    fill_misc(p, unit)
                    pe.wait_ge(w_loaded[kv % 2], b * 32 + 16 * (kv // 2 + 1))
                    pe.wait_ge(hlo_done, ONE + b * T + CH * (c + 1))
                    if p == "V":
                        for t in range(CH):
                            tok = (c * CH + t) * P
                            for k in range(KD):
                                last = three(misc[:, t * DH:(t + 1) * DH], lambda s: ht[:, s, k, tok:tok + P],
                                             lambda s: wqkv(kv % 2, s, k, VCOL, DH), k == 0, k == KD - 1)
                    else:
                        col = KCOL if p == "K" else int(p[1]) * DH
                        for k in range(KD):
                            last = three(misc[:, :], lambda s: wqkv(kv % 2, s, k, col, DH),
                                         lambda s: ht[:, s, k, c * CW:(c + 1) * CW], k == 0, k == KD - 1)
                    last.then_inc(misc_filled, 1)

                def scores(n, h):
                    kv, i = divmod(n, T)
                    s, w, unit = n * G + h, (i + 1) * P, n // CH
                    pe.wait_ge(rotlo_done, ONE + b * NROT + (unit + 1) * (G + 1))
                    pe.wait_ge(probs_done, ONE + b * NS + max(s - 1, 0))
                    tok = (i % CH) * P
                    for lo in range(0, w, 512):
                        hi = min(lo + 512, w)
                        diag = hi == w
                        last = three(s_ps[:, s % 2, lo:hi], lambda f: qbuf[:, unit % 2, f, h, tok:tok + P],
                                     lambda f: kbuf[:, kv % 2, f, lo:hi], True, not diag)
                    last = pe.matmul(s_ps[:, s % 2, w - P:w], identb_sb[:], causal_sb[:], start=False, stop=True)
                    last.then_inc(scores_done, 1)

                def turn(n, j):
                    a = pt_index(n, j)
                    if j == 0:
                        pe.wait_ge(probs_done, ONE + b * NS + (n + 1) * G)
                    pe.wait_ge(pt_emptied, ONE + b * NPT + a - 1)
                    for h in range(G):
                        last = pe.transpose(pt_ps[:, a % 2, h * P:(h + 1) * P],
                                            probs[:, n % 2, h, j * P:(j + 1) * P], ident_sb[:])
                    last.then_inc(pt_filled, 1)

                def values(n, j):
                    a, kv = pt_index(n, j), n // T
                    if j == 0:
                        pe.wait_ge(o_done, ONE + b * NTILE + n)
                        pe.wait_ge(misc_emptied, ONE + b * NMISC + MISC[("V", n // CH)] + 1)
                    pe.wait_ge(pt_emptied, ONE + b * NPT + a + 1)
                    three(o_ps[:, :], lambda f: vbuf[:, kv % 2, f, j, :], lambda f: pt[:, a % 2, f, :],
                          j == 0, j == n % T).then_inc(pv_done, 1)

                def spread_norm(n):
                    fill_misc("R", n)
                    pe.wait_ge(rrow_done, b * NTILE + n + 1)
                    for h in range(G):
                        last = pe.transpose(misc[:, h * P:(h + 1) * P],
                                            rrow[:, n % 2, h:h + 1].broadcast_to([P, P]), ident_sb[:])
                    last.then_inc(misc_filled, 1)

                def project_out(n):
                    fill_misc("Y", n)
                    pe.wait_ge(olo_done, ONE + b * NTILE + n + 1)
                    for h in range(G):
                        last = three(misc[:, 0:D], lambda f: o_r[:, f, h * P:(h + 1) * P],
                                     lambda f: wo_part(n // T % 2, f, h), h == 0, h == G - 1)
                    last.then_inc(misc_filled, 1)

                for t in range(T):
                    pe.wait_ge(z_done, b * T + t + 1)
                    pe.wait_ge(pt_emptied, ONE + b * NPT + max(t - 1, 0))
                    for k in range(KD):
                        last = pe.transpose(pt_ps[:, t % 2, k * P:(k + 1) * P], z[:, t % 2, k * P:(k + 1) * P], ident_sb[:])
                    last.then_inc(pt_filled, 1)
                for p in PROJ:
                    project(p, 0)
                for h in range(G):
                    scores(0, h)
                for n in range(NTILE):
                    nj, proj = n % T + 1, projected_in(n)
                    for j in range(nj):
                        turn(n, j)
                        if j == 0 and n:
                            project_out(n - 1)
                        if j == 0 and proj:
                            project(proj[0], n // CH + 1)
                        if j == nj - 1:
                            if proj:
                                project(proj[1], n // CH + 1)
                            spread_norm(n)
                        for h in scores_at(n, j):
                            scores(n + 1, h)
                        if j:
                            values(n, j - 1)
                    values(n, nj - 1)
                project_out(NTILE - 1)

        @block.scalar
        def _(act):
            for started in (misc_emptied, probs_done,):
                act.sem_inc(started, ONE)
            with act.Fori(0, B) as b:
                def empty_proj(p, unit):
                    act.wait_ge(misc_filled, b * NMISC + MISC[(p, unit)] + 1)
                    kv, c = divmod(unit, T // CH)
                    if p == "V":
                        act.copy(vbuf[:, kv % 2, 0, c * CH:(c + 1) * CH, :].rearrange("p t d -> p (t d)"),
                                 misc[:, :]).then_inc(vhi_done, 1)
                    else:
                        r = rot_index(p, unit)
                        act.wait_ge(rot_done, ONE + b * NROT + max(r - 1, 0))
                        act.copy(raw[:, r % 2, :], misc[:, :]).then_inc(misc_emptied, 1)

                def rot_high(p, unit):
                    if p == "V":
                        return
                    r = rot_index(p, unit)
                    act.wait_ge(rot_done, ONE + b * NROT + r + 1)
                    act.copy(rot_dest(p, unit, 0), rot[:, r % 2, :]).then_inc(rothi_done, 1)

                def exps(n, h):
                    s, w = n * G + h, (n % T + 1) * P
                    act.wait_ge(max_done, b * NS + s + 1)
                    act.wait_ge(linv_done, ONE + b * NTILE + max(n - 1, 0))
                    act.activation(probs[:, n % 2, h, 0:w], s_ps[:, s % 2, 0:w], ACT.Exp, bias=negmax[:, s % 4:s % 4 + 1],
                                   scale=1.0, accum_out=lsum[:, n % 2, h:h + 1]).then_inc(probs_done, 1)

                def o_high(n):
                    act.wait_ge(o_done, ONE + b * NTILE + n + 1)
                    if n:
                        act.wait_ge(misc_filled, b * NMISC + MISC[("Y", n - 1)] + 1)
                    act.copy(o_r[:, 0, :], o_f[:, :]).then_inc(ohi_done, 1)

                for t in range(T):
                    act.wait_ge(pt_emptied, ONE + b * NPT + t + 1)
                    act.copy(ht[:, 0, :, t * P:(t + 1) * P], hf[:, t % 2]).then_inc(hhi_done, 1)
                for q, p in enumerate(PROJ):
                    empty_proj(p, 0)
                    if q:
                        rot_high(PROJ[q - 1], 0)
                rot_high(PROJ[-1], 0)
                for h in range(G):
                    exps(0, h)
                for n in range(NTILE):
                    nj, proj = n % T + 1, projected_in(n)
                    for j in range(nj):
                        a = pt_index(n, j)
                        act.wait_ge(pt_filled, ONE + b * NPT + a + 1)
                        act.wait_ge(pv_done, ONE + b * NPV + max(a - T - 1, 0))
                        act.copy(pt[:, a % 2, 0, :], pt_ps[:, a % 2, :]).then_inc(pthi_done, 1)
                        if j == 0 and proj:
                            empty_proj(proj[0], n // CH + 1)
                        if j == nj - 1:
                            if proj:
                                empty_proj(proj[1], n // CH + 1)
                                rot_high(proj[0], n // CH + 1)
                            act.wait_ge(misc_filled, b * NMISC + MISC[("R", n)] + 1)
                            act.wait_ge(o_done, ONE + b * NTILE + n)
                            act.copy(r_sb[:, :], misc[:, :]).then_inc(misc_emptied, 1)
                        for h in scores_at(n, j):
                            exps(n + 1, h)
                    if proj:
                        rot_high(proj[1], n // CH + 1)
                    o_high(n)

        @block.vector
        def _(dve):
            for started in (pt_emptied, linv_done, o_done, rot_done,):
                dve.sem_inc(started, ONE)
            with dve.Fori(0, B) as b:
                def rot_cos(p, unit):
                    if p == "V":
                        kv, c = divmod(unit, T // CH)
                        dve.wait_ge(vhi_done, b * UNITS + unit + 1)
                        dve.tensor_tensor(vbuf[:, kv % 2, 1, c * CH:(c + 1) * CH, :].rearrange("p t d -> p (t d)"),
                                          misc[:, :],
                                          f32(vbuf[:, kv % 2, 0, c * CH:(c + 1) * CH, :].rearrange("p t d -> p (t d)")),
                                          ALU.subtract).then_inc(misc_emptied, 1)
                        return
                    r, c = rot_index(p, unit), unit % (T // CH)
                    dve.wait_ge(misc_emptied, ONE + b * NMISC + MISC[(p, unit)] + 1)
                    dve.wait_ge(rotlo_done, ONE + b * NROT + max(r - 1, 0))
                    dve.tensor_tensor(rot[:, r % 2, :], raw[:, r % 2, :], cos_sb[:, c * CW:(c + 1) * CW],
                                      ALU.mult).then_inc(cos_done, 1)

                def rot_sum(p, unit):
                    if p == "V":
                        return
                    r = rot_index(p, unit)
                    dve.wait_ge(cos_done, b * NROT + r + 1)
                    dve.wait_ge(sin_done, b * NROT + r + 1)
                    dve.tensor_tensor(rot[:, r % 2, :], rot[:, r % 2, :], swapped[:, r % 2, :],
                                      ALU.add).then_inc(rot_done, 1)

                def row_max(n, h):
                    s, w = n * G + h, (n % T + 1) * P
                    dve.wait_ge(scores_done, b * NS + s + 1)
                    dve.tensor_reduce(negmax[:, s % 4:s % 4 + 1], s_ps[:, s % 2, 0:w], AX_X, ALU.max,
                                      negate=True).then_inc(max_done, 1)

                def invert_sums(n):
                    dve.wait_ge(probs_done, ONE + b * NS + (n + 1) * G)
                    dve.reciprocal(linv[:, n % 2, :], lsum[:, n % 2, :]).then_inc(linv_done, 1)

                def gate(n):
                    dve.wait_ge(misc_filled, b * NMISC + MISC[("Y", n)] + 1)
                    dve.wait_ge(acc_done, ONE + b * NTILE + max(n - 1, 0))
                    dve.tensor_tensor(ytmp[:, n % 2, :], misc[:, 0:D],
                                      ga[:, bass.ds(b, 1), :].rearrange("p o d -> p (o d)"),
                                      ALU.mult).then_inc(misc_emptied, 1)

                dve.wait_ge(x_loaded, b * 16 + 16)
                for t in range(T):
                    dve.bn_stats(stats[:, t, :], xacc[:, t, :]).then_inc(stats_done, 1)
                dve.wait_ge(stats_done, b * T + T)
                dve.memset(mark[:], 0.0)
                for t in range(T):
                    dve.bn_aggr(mv[:, t, :], stats[:, t, :]).then_inc(mean_done, 1)
                dve.wait_ge(rstd_done, b + 1)

                def shift(t):
                    dve.wait_ge(pt_filled, ONE + b * NPT + t + 1)
                    dve.wait_ge(hlo_done, ONE + b * T + max(t - 1, 0))
                    for k in range(KD):
                        last = dve.tensor_scalar(hf[:, t % 2, k, :], pt_ps[:, t % 2, k * P:(k + 1) * P],
                                                 modp[:, 1, k, bass.ds(b, 1)], modp[:, 0, k, bass.ds(b, 1)],
                                                 ALU.mult, ALU.add)
                    last.then_inc(pt_emptied, 1)

                for t in range(T):
                    dve.wait_ge(pt_filled, ONE + b * NPT + max(t - 1, 0))
                    dve.tensor_scalar(z[:, t % 2, :], xacc[:, t, :], mv[:, t, 0:1], rstd[:, 1, t:t + 1],
                                      ALU.subtract, ALU.mult).then_inc(z_done, 1)
                    if t:
                        shift(t - 1)
                shift(T - 1)
                for q, p in enumerate(PROJ):
                    rot_cos(p, 0)
                    if q:
                        rot_sum(PROJ[q - 1], 0)
                rot_sum(PROJ[-1], 0)
                for h in range(G):
                    row_max(0, h)
                for n in range(NTILE):
                    nj, proj = n % T + 1, projected_in(n)
                    invert_sums(n)
                    for j in range(nj):
                        a = pt_index(n, j)
                        dve.wait_ge(pthi_done, b * NPV + a - T + 1)
                        dve.tensor_tensor(pt[:, a % 2, 1, :], pt_ps[:, a % 2, :], f32(pt[:, a % 2, 0, :]),
                                          ALU.subtract).then_inc(pt_emptied, 1)
                        if j == 0 and n:
                            gate(n - 1)
                        if j == 0 and proj:
                            rot_cos(proj[0], n // CH + 1)
                        if j == nj - 1 and proj:
                            rot_cos(proj[1], n // CH + 1)
                            rot_sum(proj[0], n // CH + 1)
                        for h in scores_at(n, j):
                            row_max(n + 1, h)
                    if proj:
                        rot_sum(proj[1], n // CH + 1)
                    dve.wait_ge(misc_emptied, ONE + b * NMISC + MISC[("R", n)] + 1)
                    dve.wait_ge(pv_done, ONE + b * NPV + pt_index(n, nj - 1) - T + 1)
                    dve.wait_ge(olo_done, ONE + b * NTILE + n)
                    dve.tensor_tensor(o_f[:, :], o_ps[:, :], r_sb[:, :], ALU.mult).then_inc(o_done, 1)
                gate(NTILE - 1)

        @block.gpsimd
        def _(pool):
            for started in (olo_done, acc_done, hlo_done, rotlo_done,):
                pool.sem_inc(started, ONE)
            with pool.Fori(0, B) as b:
                def rot_sin(p, unit):
                    if p == "V":
                        return
                    r, c = rot_index(p, unit), unit % (T // CH)
                    per = NROT // 2 * 32
                    pool.wait_ge(swap_done[r % 2], b * per + 32 * (r // 2 + 1))
                    pool.tensor_tensor(swapped[:, r % 2, :], swapped[:, r % 2, :], sin_sb[:, c * CW:(c + 1) * CW],
                                       ALU.mult).then_inc(sin_done, 1)

                def rot_low(p, unit):
                    if p == "V":
                        return
                    r = rot_index(p, unit)
                    pool.wait_ge(rothi_done, b * NROT + r + 1)
                    pool.tensor_tensor(rot_dest(p, unit, 1), rot[:, r % 2, :], f32(rot_dest(p, unit, 0)),
                                       ALU.subtract).then_inc(rotlo_done, 1)

                def accumulate(n):
                    pool.wait_ge(misc_emptied, ONE + b * NMISC + MISC[("Y", n)] + 1)
                    pool.wait_ge(acc_done, ONE + b * NTILE + n)
                    pool.tensor_tensor(xacc[:, n % T, :], xacc[:, n % T, :], ytmp[:, n % 2, :],
                                       ALU.add).then_inc(acc_done, 1)

                pool.wait_ge(x_loaded, b * 16 + 16)
                pool.wait_ge(mean_done, b * T + T)
                pool.tensor_tensor(rstd[:, 0, :], mv[:, :, 1], eps[:], ALU.add).then_inc(var_eps, 1)
                pool.wait_ge(var_eps, b + 1)
                pool.tensor_tensor(rstd[:, 1, :], rstd[:, 0, :], mhalf[:], ALU.pow).then_inc(rstd_done, 1)
                for t in range(T):
                    pool.wait_ge(hhi_done, b * T + t + 1)
                    pool.tensor_tensor(ht[:, 1, :, t * P:(t + 1) * P], hf[:, t % 2], f32(ht[:, 0, :, t * P:(t + 1) * P]),
                                       ALU.subtract).then_inc(hlo_done, 1)
                for q, p in enumerate(PROJ):
                    rot_sin(p, 0)
                    if q:
                        rot_low(PROJ[q - 1], 0)
                rot_low(PROJ[-1], 0)
                for n in range(NTILE):
                    nj, proj = n % T + 1, projected_in(n)
                    kv = n // T
                    pool.wait_ge(linv_done, ONE + b * NTILE + n + 1)
                    pool.tensor_tensor(rrow[:, n % 2, :], linv[:, n % 2, :], hs_sb[:, kv * G:(kv + 1) * G],
                                       ALU.mult).then_inc(rrow_done, 1)
                    if n:
                        accumulate(n - 1)
                    if proj:
                        rot_sin(proj[0], n // CH + 1)
                        rot_sin(proj[1], n // CH + 1)
                        rot_low(proj[0], n // CH + 1)
                        rot_low(proj[1], n // CH + 1)
                    pool.wait_ge(ohi_done, b * NTILE + n + 1)
                    pool.tensor_tensor(o_r[:, 1, :], o_f[:, :], f32(o_r[:, 0, :]), ALU.subtract).then_inc(olo_done, 1)
                accumulate(NTILE - 1)


def reload(sp, b, kv, misc_filled, w_loaded, wbuf, wsplit):
    sp.wait_ge(misc_filled, b * NMISC + MISC[("Y", kv * T + T - 1)] + 1)
    sp.dma_start(wbuf[:, kv % 2].rearrange("p s w -> p (s w)").bitcast(F32), wsplit[(kv + 2) % KV]).then_inc(w_loaded[kv % 2], 16)


def prepare(nc, ctx, sb, sem, wq, wk, wv, wo, hscale, c, wmod, cos, sin, ident, causal, wsplit,
            probs, wbuf, cos_sb, sin_sb, causal_sb, identb_sb, hs_sb, mhalf, eps, ident_sb, ga, rows_dram, modp,
            xacc, raw, swapped, rot, o_f, ps_a, ps_b):
    flat = probs[:].rearrange("p a h n -> p (a h n)")
    wraw = [flat[:, g * WG:(g + 1) * WG] for g in range(2)]
    wm = flat[:, 2 * WG:2 * WG + KD * 6 * D].rearrange("p (k n) -> p k n", k=KD)
    c_sb = sb("c_sb", [P, KD, B])
    c_act = sb("c_act", [P, 3, KD, B])
    c_wide = xacc[:].rearrange("p t d -> p (t d)")[:, 0:KD * B * P].rearrange("p (k b c) -> p k b c", k=KD, b=B)
    gates = raw[:].rearrange("p s w -> p (s w)")[:, 0:3 * D].rearrange("p (s d) -> p s d", s=3)
    gb = swapped[:].rearrange("p s w -> p (s w)").rearrange("p (b d) -> p b d", b=B)
    shift_row = rot[:].rearrange("p s w -> p (s w)").rearrange("p (b d) -> p b d", b=B)
    scale_row = xacc[:].rearrange("p t d -> p (t d)")[:, KD * B * P:].rearrange("p (b d) -> p b d", b=B)

    const_loaded = sem("const_loaded")
    mod_loaded = sem("mod_loaded")
    wraw_loaded = [sem("wraw_loaded0"), sem("wraw_loaded1")]
    whi_done = sem("whi_done")
    wlo_done = sem("wlo_done")
    wsplit_stored = [sem("wsplit_stored0"), sem("wsplit_stored1")]
    exp_done = sem("exp_done")
    silu_steps = sem("silu_steps")
    wide_done = sem("wide_done")
    modp_filled = sem("modp_filled")
    gate_filled = sem("gate_filled")
    gate_steps = sem("gate_steps")
    mhalf_set = sem("mhalf_set")

    block_cm = nc.Block()
    with block_cm as block:
        @block.sync
        def _(sp):
            for k in range(KD):
                for bb in range(B):
                    sp.dma_start(c_sb[:, k, bb:bb + 1], c[bb:bb + 1, k * P:(k + 1) * P].rearrange("b p -> p b")).then_inc(mod_loaded, 16)
            sp.dma_start(wm, wmod.rearrange("(k p) n -> p k n", p=P)).then_inc(mod_loaded, 16)
            sp.dma_start(cos_sb[:], cos).then_inc(const_loaded, 16)
            sp.dma_start(sin_sb[:], sin).then_inc(const_loaded, 16)
            sp.dma_start(ident_sb[:], ident).then_inc(const_loaded, 16)
            sp.dma_start(o_f[:, 0:P], causal).then_inc(const_loaded, 16)
            sp.dma_start(hs_sb[:], hscale.rearrange("a h b c -> a (h b c)").broadcast_to([P, H])).then_inc(const_loaded, 16)
            for kv in range(KV):
                g = kv % 2
                if kv >= 2:
                    sp.wait_ge(wlo_done, kv - 1)
                for k in range(KD):
                    dst = wraw[g][:, k * WQ:(k + 1) * WQ]
                    rows = slice(k * P, (k + 1) * P)
                    sp.dma_start(dst[:, 0:KCOL], wq[rows, kv * KCOL:(kv + 1) * KCOL]).then_inc(wraw_loaded[g], 16)
                    sp.dma_start(dst[:, KCOL:VCOL], wk[rows, kv * DH:(kv + 1) * DH]).then_inc(wraw_loaded[g], 16)
                    sp.dma_start(dst[:, VCOL:WQ], wv[rows, kv * DH:(kv + 1) * DH]).then_inc(wraw_loaded[g], 16)
                sp.dma_start(wraw[g][:, KD * WQ:].rearrange("p (h n) -> p h n", h=G),
                             wo[kv * G * DH:(kv + 1) * G * DH, :].rearrange("(h p) n -> p h n", p=P)).then_inc(wraw_loaded[g], 16)
            for kv in range(KV):
                sp.wait_ge(wlo_done, kv + 1)
                sp.dma_start(wsplit[kv], wbuf[:, kv % 2].rearrange("p s w -> p (s w)").bitcast(F32)).then_inc(wsplit_stored[kv % 2], 16)
            for g in range(2):
                sp.wait_ge(wsplit_stored[g], 32)
            sp.wait_ge(gate_steps, 2 + 10 * B)
            for k, row in enumerate((gb, shift_row, scale_row)):
                sp.dma_start(rows_dram[k:k + 1], row[0:1]).then_inc(const_loaded, 16)
            sp.wait_ge(const_loaded, 16 * 8)

        @block.scalar
        def _(act):
            act.wait_ge(mod_loaded, 16 * (KD * B + 1))
            act.activation(c_act[:, 0], c_sb[:], ACT.Exp, scale=-1.0).then_inc(exp_done, 1)
            for kv in range(KV):
                act.wait_ge(wraw_loaded[kv % 2], 16 * (3 * KD + 1) * (kv // 2 + 1))
                if kv >= 2:
                    act.wait_ge(wsplit_stored[kv % 2], 16)
                act.copy(wbuf[:, kv % 2, 0, :], wraw[kv % 2]).then_inc(whi_done, 1)

        @block.vector
        def _(dve):
            dve.memset(mhalf[:], -0.5)
            dve.memset(eps[:], EPS).then_inc(mhalf_set, 1)
            dve.wait_ge(exp_done, 1)
            dve.tensor_scalar(c_act[:, 1], c_act[:, 0], 1.0, None, ALU.add).then_inc(silu_steps, 1)
            dve.wait_ge(silu_steps, 1)
            dve.reciprocal(c_act[:, 2], c_act[:, 1]).then_inc(silu_steps, 1)
            dve.wait_ge(silu_steps, 2)
            dve.tensor_tensor(c_act[:, 0], c_act[:, 2], c_sb[:], ALU.mult).then_inc(silu_steps, 1)
            dve.wait_ge(silu_steps, 3)
            for k in range(KD):
                last = dve.tensor_copy(c_wide[:, k], c_act[:, 0, k, :].rearrange("p (b o) -> p b o", o=1).broadcast_to([P, B, P]))
            last.then_inc(wide_done, 1)
            dve.wait_ge(modp_filled, 1)
            last = dve.tensor_copy(modp[:].rearrange("p s k b -> p (s k b)"), ps_a[:, 0:6 * KD * B])
            last.then_inc(gate_steps, 1)
            dve.wait_ge(gate_steps, 1)
            for sec in (1, 4):
                last = dve.tensor_scalar(modp[:, sec], modp[:, sec], 1.0, None, ALU.add)
            last.then_inc(gate_steps, 1)
            steps = 2
            for bb in range(B):
                for half, dest in enumerate((ga, gb)):
                    n = 2 * bb + half
                    src = ps_b[:, half * D:(half + 1) * D]
                    dve.wait_ge(gate_filled, n + 1)
                    dve.tensor_scalar(gates[:, 0], src, 0.0, 2.0, ALU.is_ge, ALU.mult).then_inc(gate_steps, 1)
                    dve.wait_ge(gate_steps, steps + 1)
                    dve.tensor_scalar(gates[:, 2], gates[:, 0], -1.0, None, ALU.add).then_inc(gate_steps, 1)
                    dve.wait_ge(gate_steps, steps + 2)
                    dve.tensor_tensor(gates[:, 1], src, gates[:, 2], ALU.mult).then_inc(gate_steps, 1)
                    dve.wait_ge(gate_steps, steps + 3)
                    dve.scalar_tensor_tensor(out=dest[:, bb, :], in0=gates[:, 1], scalar=0.25, in1=gates[:, 2],
                                             op0=ALU.max, op1=ALU.mult).then_inc(gate_steps, 1)
                    dve.wait_ge(gate_steps, steps + 4)
                    steps += 4
            for bb in range(B):
                dve.wait_ge(gate_filled, 2 * B + bb + 1)
                dve.tensor_copy(shift_row[:, bb, :], ps_b[:, 0:D]).then_inc(gate_steps, 1)
                dve.tensor_scalar(scale_row[:, bb, :], ps_b[:, D:2 * D], 1.0, None, ALU.add).then_inc(gate_steps, 1)
            for kv in range(KV):
                dve.wait_ge(whi_done, kv + 1)
                dve.tensor_tensor(wbuf[:, kv % 2, 1, :], wraw[kv % 2], wbuf[:, kv % 2, 0, :].bitcast(F32),
                                  ALU.subtract).then_inc(wlo_done, 1)

        @block.gpsimd
        def _(pool):
            pool.wait_ge(const_loaded, 16 * 5)
            pool.tensor_copy(causal_sb[:], o_f[:, 0:P])
            pool.tensor_copy(identb_sb[:], ident_sb[:]).then_inc(mhalf_set, 1)
            pool.wait_ge(mhalf_set, 2)

        @block.tensor
        def _(pe):
            pe.wait_ge(silu_steps, 3)
            pe.wait_ge(mod_loaded, 16 * (KD * B + 1))
            for sec in range(6):
                for half in range(KD):
                    col = (sec * KD + half) * B
                    for k in range(KD):
                        last = pe.matmul(ps_a[:, col:col + B], wm[:, k, sec * D + half * P:sec * D + (half + 1) * P],
                                         c_act[:, 0, k, :], start=(k == 0), stop=(k == KD - 1))
            last.then_inc(modp_filled, 1)
            pe.wait_ge(wide_done, 1)
            for bb in range(B):
                for half, sec in enumerate((2, 5)):
                    if bb or half:
                        pe.wait_ge(gate_steps, 2 + 4 * (2 * bb + half))
                    for k in range(KD):
                        last = pe.matmul(ps_b[:, half * D:(half + 1) * D], c_wide[:, k, bb, :],
                                         wm[:, k, sec * D:(sec + 1) * D], start=(k == 0), stop=(k == KD - 1))
                    last.then_inc(gate_filled, 1)
            for bb in range(B):
                pe.wait_ge(gate_steps, 2 + 8 * B + 2 * bb)
                for half, sec in enumerate((3, 4)):
                    for k in range(KD):
                        last = pe.matmul(ps_b[:, half * D:(half + 1) * D], c_wide[:, k, bb, :],
                                         wm[:, k, sec * D:(sec + 1) * D], start=(k == 0), stop=(k == KD - 1))
                last.then_inc(gate_filled, 1)


E, TOPK, FI = 32, 4, 96
NTOK = B * N
NSLOT_TILES = NTOK * TOPK // P + E
FU = 8
STORE_LAG = FU - 1


def route(nc, x1, rows_dram, rw, gw, uw, dw, idtab, h2, ydram, out, tri, iota_e, ebase, iota_m, tokens, ident_sb):
    with ExitStack() as ctx:
        def sb(name, shape, dt=F32):
            return ctx.enter_context(nc.sbuf_tensor(name, shape, dt))

        def sem(name):
            return ctx.enter_context(nc.semaphore(name))

        def bank(name, dt=F32):
            return ctx.enter_context(nc.psum_tensor(name, [P, 512], dt))

        banks = [bank(f"bank{i}") for i in range(8)]
        wgu = sb("wgu", [P, KD, E, 2 * FI])
        wd = sb("wd", [P, E, D])
        w4_all = sb("w4_all", [P, B * T + FU, TOPK])
        hot_all = sb("hot_all", [P, B * T, TOPK, E], BF16)
        rank_all = sb("rank_all", [P, B * T, E])
        totals = sb("totals", [P, E])
        etab = sb("etab", [P, NSLOT_TILES], mybir.dt.int32)
        offtab = sb("offtab", [P, NSLOT_TILES], mybir.dt.int32)
        pos_all = sb("pos_all", [P, B * T + FU, TOPK], U32)

        transposed_weights(nc, banks, gw, uw, dw, wgu, wd, ident_sb)
        route_tokens(nc, banks, x1, rows_dram, rw, idtab, h2, tri, iota_e, ebase, tokens, ident_sb,
                     w4_all, hot_all, rank_all, totals)
        place_tiles(nc, iota_m, hot_all, rank_all, totals, w4_all, etab, offtab, pos_all)
        experts(nc, banks, idtab, h2, ydram, wgu, wd, etab, offtab, ident_sb)
        combine(nc, x1, rows_dram, ydram, out, w4_all, pos_all)


def transposed_weights(nc, banks, gw, uw, dw, wgu, wd, ident_sb):
    EG = 4
    with ExitStack() as ctx:
        sb = lambda name, shape: ctx.enter_context(nc.sbuf_tensor(name, shape, F32))
        sem = lambda name: ctx.enter_context(nc.semaphore(name))
        graw = sb("graw", [P, 2, 2, EG, D])
        draw = sb("draw", [P, 2, EG, KD, FI])
        raw_loaded = [sem("raw_loaded0"), sem("raw_loaded1")]
        turned = sem("turned")
        turn_copied = sem("turn_copied")
        down_copied = sem("down_copied")
        steps = E // EG
        block = ctx.enter_context(nc.Block())

        @block.sync
        def _(sp):
            for g in range(steps):
                if g >= 2:
                    sp.wait_ge(turned, 6 * (g - 1))
                for k, w in enumerate((gw, uw)):
                    sp.dma_start(graw[0:FI, g % 2, k], w[g * EG:(g + 1) * EG].rearrange("e i d -> i e d")).then_inc(raw_loaded[g % 2], 16)
                for e in range(EG):
                    sp.dma_start(draw[:, g % 2, e], dw[g * EG + e].rearrange("(k p) i -> p k i", p=P)).then_inc(raw_loaded[g % 2], 16)

        @block.tensor
        def _(pe):
            for g in range(steps):
                pe.wait_ge(raw_loaded[g % 2], 16 * (2 + EG) * (g // 2 + 1))
                for e in range(EG):
                    if g:
                        pe.wait_ge(turn_copied, EG * (g - 1) + e + 1)
                    for k in range(KD):
                        for w in range(2):
                            last = pe.transpose(banks[e][:, (2 * k + w) * FI:(2 * k + w + 1) * FI],
                                                graw[0:FI, g % 2, w, e, k * P:(k + 1) * P], ident_sb[0:FI, 0:FI])
                    last.then_inc(turned, 1)
                for q in range(EG // 2):
                    if g:
                        pe.wait_ge(down_copied, (EG // 2) * (g - 1) + q + 1)
                    for e in range(2):
                        for k in range(KD):
                            last = pe.transpose(banks[4 + q][0:FI, (2 * e + k) * P:(2 * e + k + 1) * P],
                                                draw[:, g % 2, 2 * q + e, k, :], ident_sb[:])
                    last.then_inc(turned, 1)

        @block.vector
        def _(dve):
            for g in range(steps):
                for e in range(EG):
                    dve.wait_ge(turned, 6 * g + e + 1)
                    dve.tensor_copy(wgu[:, :, g * EG + e, :], banks[e][:, 0:4 * FI].rearrange("p (k c) -> p k c", k=KD)).then_inc(turn_copied, 1)

        @block.scalar
        def _(act):
            for g in range(steps):
                for q in range(EG // 2):
                    act.wait_ge(turned, 6 * g + EG + q + 1)
                    act.copy(wd[0:FI, g * EG + 2 * q:g * EG + 2 * q + 2, :].rearrange("p e d -> p (e d)"),
                             banks[4 + q][0:FI, :]).then_inc(down_copied, 1)


def route_tokens(nc, banks, x1, rows_dram, rw, idtab, h2, tri, iota_e, ebase, tokens, ident_sb,
                 w4_all, hot_all, rank_all, totals):
    with ExitStack() as ctx:
        sb = lambda name, shape, dt=F32: ctx.enter_context(nc.sbuf_tensor(name, shape, dt))
        sem = lambda name: ctx.enter_context(nc.semaphore(name))
        xb = sb("xb", [P, T, D])
        hb = sb("hb", [P, T, D])
        hbt = sb("hbt", [P, T, KD, P])
        mod = sb("mod", [P, 2, D])
        rwr = sb("rwr", [P, D])
        rwt = sb("rwt", [P, KD, E])
        st = sb("st", [P, T, 6])
        mv = sb("mv2", [P, T, 2])
        rstd = sb("rstd2", [P, 2, T])
        mhalf = sb("mhalf2", [P, T])
        eps = sb("eps2", [P, T])
        mark = sb("mark2", [P, 4])
        logits = sb("logits", [P, T, E])
        top = sb("top", [P, T, 8])
        top_at = sb("top_at", [P, T, 8], U32)
        at_f = sb("at_f", [P, T, TOPK])
        diff = sb("diff", [P, T, TOPK])
        e4 = sb("e4", [P, T, TOPK])
        esum = sb("esum", [P, 2, T])
        hot = sb("hot", [P, T, TOPK, E])
        mask = sb("mask", [P, T, E], BF16)
        runsum = sb("runsum", [P, E], BF16)
        batch_sum = sb("batch_sum", [P, E])
        rank = sb("rank", [P, T, E])
        slot = sb("slot", [P, T, E])
        slots = sb("slots", [P, T, TOPK, E])
        slot_f = sb("slot_f", [P, T, TOPK])
        slot_u = sb("slot_u", [P, T, TOPK], U32)
        tok = sb("tok", [P, B * T], U32)
        tokb = sb("tokb", [P, T], U32)
        tri_sb = sb("tri_sb", [P, P], BF16)
        tri_f = sb("tri_f", [P, P])
        ones = sb("ones", [P, P], BF16)
        iota_sb = sb("iota_sb", [P, E])
        ebase_sb = sb("ebase_sb", [P, E])
        zero = sb("zero", [P, NTOK * E // P], U32)

        names = """const2 zeroed tab_set in_loaded h2_stored rw_turned rwt_done stats2 mean2 var2 rstd2_done norm2 scaled2
                   h2_done turned2 turn2_copied logits_filled logits_copied top_done at_done diff_done atf_done hot_done
                   mask_done hotall_done bsum_done e4_done esum_done einv_done w4_done rank_filled rank_copied rankall_done
                   slot_done slots_done slotf_done slotu_done tokb_done scatter_go scattered runsum_done totals_filled""".split()
        s = {name: sem("q_" + name) for name in names}
        block = ctx.enter_context(nc.Block())

        @block.sync
        def _(sp):
            sp.dma_start(rwr[0:E, :], rw).then_inc(s["const2"], 16)
            sp.dma_start(tri_f[:], tri).then_inc(s["const2"], 16)
            sp.dma_start(iota_sb[:], iota_e).then_inc(s["const2"], 16)
            sp.dma_start(ebase_sb[:], ebase).then_inc(s["const2"], 16)
            sp.dma_start(tok[:], tokens).then_inc(s["const2"], 16)
            sp.wait_ge(s["zeroed"], 1)
            sp.dma_start(idtab.rearrange("(p n) o -> p (n o)", p=P), zero[:]).then_inc(s["tab_set"], 16)
            sp.sem_inc(s["h2_stored"], ONE)
            with sp.Fori(0, B) as b:
                sp.wait_ge(s["h2_stored"], ONE + b * 16)
                sp.dma_start(xb[:], x1[bass.ds(b, 1), :, :].rearrange("o (t p) d -> p (o t) d", p=P)).then_inc(s["in_loaded"], 16)
                for k in range(2):
                    sp.dma_start(mod[:, k, :], rows_dram[k + 1:k + 2, bass.ds(b, 1), :].rearrange("a b d -> a (b d)").broadcast_to([P, D])).then_inc(s["in_loaded"], 16)
                sp.wait_ge(s["h2_done"], b + 1)
                sp.dma_start(h2[bass.ds(b, 1), :, :].rearrange("o (t p) d -> p (o t) d", p=P), hb[:]).then_inc(s["h2_stored"], 16)
            sp.wait_ge(s["h2_stored"], ONE + 16 * B)
            sp.wait_ge(s["tab_set"], 16)

        @block.vector
        def _(dve):
            dve.memset(mhalf[:], -0.5)
            dve.memset(eps[:], EPS)
            dve.memset(ones[:], 1.0)
            dve.memset(zero[:], 0)
            dve.memset(runsum[:], 0.0).then_inc(s["zeroed"], 1)
            dve.wait_ge(s["rw_turned"], 1)
            dve.tensor_copy(rwt[:].rearrange("p k e -> p (k e)"), banks[7][:, 0:KD * E]).then_inc(s["rwt_done"], 1)
            dve.wait_ge(s["const2"], 16 * 5)
            dve.tensor_copy(tri_sb[:], tri_f[:]).then_inc(s["runsum_done"], ONE)
            with dve.Fori(0, B) as b:
                tiles = bass.ds(b * T, T)
                dve.wait_ge(s["in_loaded"], b * 48 + 48)
                dve.memset(mark[:, 0:1], 0.0)
                for t in range(T):
                    last = dve.bn_stats(st[:, t, :], xb[:, t, :])
                last.then_inc(s["stats2"], 1)
                dve.wait_ge(s["stats2"], b + 1)
                dve.memset(mark[:, 1:2], 0.0)
                for t in range(T):
                    last = dve.bn_aggr(mv[:, t, :], st[:, t, :])
                last.then_inc(s["mean2"], 1)
                dve.wait_ge(s["rstd2_done"], b + 1)
                for t in range(T):
                    last = dve.tensor_scalar(xb[:, t, :], xb[:, t, :], mv[:, t, 0:1], rstd[:, 1, t:t + 1], ALU.subtract, ALU.mult)
                last.then_inc(s["norm2"], 1)
                dve.wait_ge(s["norm2"], b + 1)
                dve.tensor_tensor(hb[:], xb[:], mod[:, 1:2, :].broadcast_to([P, T, D]), ALU.mult).then_inc(s["scaled2"], 1)
                dve.wait_ge(s["scaled2"], b + 1)
                dve.tensor_tensor(hb[:], hb[:], mod[:, 0:1, :].broadcast_to([P, T, D]), ALU.add).then_inc(s["h2_done"], 1)
                dve.wait_ge(s["logits_filled"], b + 1)
                dve.tensor_copy(logits[:].rearrange("p t e -> p (t e)"), banks[4][:, 0:T * E]).then_inc(s["logits_copied"], 1)
                dve.wait_ge(s["logits_copied"], b + 1)
                dve.memset(mark[:, 2:3], 0.0)
                for t in range(T):
                    last = dve.max(top[:, t, :], logits[:, t, :])
                last.then_inc(s["top_done"], 1)
                dve.wait_ge(s["top_done"], b + 1)
                dve.tensor_tensor(diff[:], top[:, :, 0:TOPK], top[:, :, 0:1].broadcast_to([P, T, TOPK]), ALU.subtract).then_inc(s["diff_done"], 1)
                for t in range(T):
                    last = dve.max_index(top_at[:, t, :], top[:, t, :], logits[:, t, :])
                last.then_inc(s["at_done"], 1)
                dve.wait_ge(s["at_done"], b + 1)
                dve.tensor_copy(at_f[:], top_at[:, :, 0:TOPK]).then_inc(s["atf_done"], 1)
                dve.wait_ge(s["atf_done"], b + 1)
                for j in range(TOPK):
                    last = dve.tensor_tensor(hot[:, :, j, :], at_f[:, :, j:j + 1].broadcast_to([P, T, E]),
                                             iota_sb[:].rearrange("p (o e) -> p o e", o=1).broadcast_to([P, T, E]), ALU.is_equal)
                last.then_inc(s["hot_done"], 1)
                dve.wait_ge(s["hot_done"], b + 1)
                dve.tensor_reduce(mask[:], hot[:].rearrange("p t j e -> p t e j"), AX_X, ALU.max).then_inc(s["mask_done"], 1)
                dve.tensor_copy(hot_all[:, tiles].rearrange("p t j e -> p (t j e)"), hot[:].rearrange("p t j e -> p (t j e)")).then_inc(s["hotall_done"], 1)
                dve.wait_ge(s["mask_done"], b + 1)
                dve.tensor_reduce(batch_sum[:], mask[:].rearrange("p t e -> p e t"), AX_X, ALU.add).then_inc(s["bsum_done"], 1)
                dve.wait_ge(s["e4_done"], b + 1)
                dve.tensor_reduce(esum[:, 0, :], e4[:], AX_X, ALU.add).then_inc(s["esum_done"], 1)
                dve.wait_ge(s["esum_done"], b + 1)
                dve.reciprocal(esum[:, 1, :], esum[:, 0, :]).then_inc(s["einv_done"], 1)
                dve.wait_ge(s["einv_done"], b + 1)
                dve.tensor_tensor(w4_all[:, tiles], e4[:], esum[:, 1, :].rearrange("p (t o) -> p t o", o=1).broadcast_to([P, T, TOPK]),
                                  ALU.mult).then_inc(s["w4_done"], 1)
                dve.wait_ge(s["rank_filled"], b + 1)
                dve.tensor_copy(rank[:].rearrange("p t e -> p (t e)"), banks[5][:, 0:T * E]).then_inc(s["rank_copied"], 1)
                dve.wait_ge(s["rank_copied"], b + 1)
                dve.tensor_copy(rank_all[:, tiles].rearrange("p t e -> p (t e)"), rank[:].rearrange("p t e -> p (t e)")).then_inc(s["rankall_done"], 1)
                dve.tensor_tensor(slot[:], rank[:], ebase_sb[:].rearrange("p (o e) -> p o e", o=1).broadcast_to([P, T, E]),
                                  ALU.add).then_inc(s["slot_done"], 1)
                dve.wait_ge(s["slot_done"], b + 1)
                for j in range(TOPK):
                    last = dve.tensor_tensor(slots[:, :, j, :], hot[:, :, j, :], slot[:], ALU.mult)
                last.then_inc(s["slots_done"], 1)
                dve.wait_ge(s["slots_done"], b + 1)
                dve.tensor_reduce(slot_f[:], slots[:], AX_X, ALU.add).then_inc(s["slotf_done"], 1)
                dve.wait_ge(s["slotf_done"], b + 1)
                dve.tensor_copy(slot_u[:], slot_f[:]).then_inc(s["slotu_done"], 1)
                dve.tensor_tensor(runsum[:], runsum[:], batch_sum[:], ALU.add).then_inc(s["runsum_done"], 1)
            dve.wait_ge(s["totals_filled"], 1)
            dve.tensor_copy(totals[:], banks[6][:, 0:E]).then_inc(s["totals_filled"], 1)
            dve.wait_ge(s["totals_filled"], 2)

        @block.scalar
        def _(act):
            with act.Fori(0, B) as b:
                for q in range(T // 2):
                    act.wait_ge(s["turned2"], b * (T // 2) + q + 1)
                    act.copy(hbt[:, 2 * q:2 * q + 2].rearrange("p t k c -> p (t k c)"), banks[q][:]).then_inc(s["turn2_copied"], 1)
                act.wait_ge(s["diff_done"], b + 1)
                act.activation(e4[:], diff[:], ACT.Exp).then_inc(s["e4_done"], 1)

        @block.tensor
        def _(pe):
            pe.wait_ge(s["const2"], 16 * 5)
            for k in range(KD):
                last = pe.transpose(banks[7][:, k * E:(k + 1) * E], rwr[0:E, k * P:(k + 1) * P], ident_sb[0:E, 0:E])
            last.then_inc(s["rw_turned"], 1)
            pe.wait_ge(s["rwt_done"], 1)
            pe.wait_ge(s["zeroed"], 1)
            with pe.Fori(0, B) as b:
                pe.wait_ge(s["h2_done"], b + 1)
                for q in range(T // 2):
                    for t in (2 * q, 2 * q + 1):
                        for k in range(KD):
                            c = ((t % 2) * KD + k) * P
                            last = pe.transpose(banks[q][:, c:c + P], hb[:, t, k * P:(k + 1) * P], ident_sb[:])
                    last.then_inc(s["turned2"], 1)
                pe.wait_ge(s["turn2_copied"], (b + 1) * (T // 2))
                for t in range(T):
                    for k in range(KD):
                        last = pe.matmul(banks[4][:, t * E:(t + 1) * E], hbt[:, t, k, :], rwt[:, k, :], start=(k == 0), stop=(k == KD - 1))
                last.then_inc(s["logits_filled"], 1)
                pe.wait_ge(s["runsum_done"], b + ONE)
                pe.wait_ge(s["mask_done"], b + 1)
                for t in range(T):
                    out = banks[5][:, t * E:(t + 1) * E]
                    pe.matmul(out, ones[:], runsum[:], start=True, stop=False)
                    for before in range(t):
                        pe.matmul(out, ones[:], mask[:, before, :], start=False, stop=False)
                    last = pe.matmul(out, tri_sb[:], mask[:, t, :], start=False, stop=True)
                last.then_inc(s["rank_filled"], 1)
            pe.wait_ge(s["runsum_done"], B + ONE)
            pe.matmul(banks[6][:, 0:E], ones[:], runsum[:], start=True, stop=True).then_inc(s["totals_filled"], 1)

        @block.gpsimd
        def _(pool):
            pool.wait_ge(s["tab_set"], 16)
            pool.wait_ge(s["zeroed"], 1)
            pool.wait_ge(s["const2"], 16 * 5)
            with pool.Fori(0, B) as b:
                pool.wait_ge(s["mean2"], b + 1)
                pool.tensor_tensor(rstd[:, 0, :], mv[:, :, 1], eps[:], ALU.add).then_inc(s["var2"], 1)
                pool.wait_ge(s["var2"], b + 1)
                pool.tensor_tensor(rstd[:, 1, :], rstd[:, 0, :], mhalf[:], ALU.pow).then_inc(s["rstd2_done"], 1)
                pool.tensor_copy(tokb[:], tok[:, bass.ds(b * T, T)]).then_inc(s["tokb_done"], 1)
                pool.wait_ge(s["tokb_done"], b + 1)
                pool.wait_ge(s["slotu_done"], b + 1)
                pool.sem_inc(s["scatter_go"], 1)
                for t in range(T):
                    for j in range(TOPK):
                        pool.indirect_dma_start(idtab, bass.IndirectOffsetOnAxis(ap=slot_u[:, t, j:j + 1], axis=0),
                                                tokb[:, t:t + 1], None).then_inc(s["scattered"], 16)
                pool.wait_ge(s["scattered"], (b + 1) * 16 * T * TOPK)


def place_tiles(nc, iota_m, hot_all, rank_all, totals, w4_all, etab, offtab, pos_all):
    with ExitStack() as ctx:
        sb = lambda name, shape, dt=F32: ctx.enter_context(nc.sbuf_tensor(name, shape, dt))
        M = NSLOT_TILES
        padded = sb("padded", [P, E])
        padded_i = sb("padded_i", [P, 2, E], mybir.dt.int32)
        ntiles = sb("ntiles", [P, E])
        ones = sb("ones_e", [P, E])
        upto = sb("upto", [P, E])
        base = sb("base", [P, 2, E])
        place = sb("place", [P, B * T, E])
        places = sb("places", [P, B * T, TOPK, E])
        pos_f = sb("pos_f", [P, B * T, TOPK])
        passed = sb("passed", [P, M, E])
        passed_n = sb("passed_n", [P, M, E])
        tile_e = sb("tile_e", [P, 3, M])
        off_f = sb("off_f", [P, 4, M])
        iota_sb = sb("iota_m_sb", [P, M])
        loaded = ctx.enter_context(nc.semaphore("iota_loaded"))
        step_done = ctx.enter_context(nc.semaphore("placing_step_done"))
        block = ctx.enter_context(nc.Block())

        @block.sync
        def _(sp):
            sp.dma_start(iota_sb[:], iota_m).then_inc(loaded, 16)

        @block.vector
        def _(dve):
            count = [0]

            def step(ins):
                count[0] += 1
                ins.then_inc(step_done, 1)
                dve.wait_ge(step_done, count[0])

            wide = lambda ap, n: ap.rearrange("p (o e) -> p o e", o=1).broadcast_to([P, n, E])
            dve.wait_ge(loaded, 16)
            step(dve.memset(ones[:], 1.0))
            step(dve.tensor_scalar(padded[:], totals[:], float(P - 1), None, ALU.add))
            step(dve.tensor_copy(padded_i[:, 0], padded[:]))
            step(dve.tensor_scalar(padded_i[:, 1], padded_i[:, 0], 7, None, ALU.arith_shift_right))
            step(dve.tensor_copy(ntiles[:], padded_i[:, 1]))
            step(dve.tensor_tensor_scan(upto[:], ones[:], ntiles[:], 0.0, ALU.mult, ALU.add))
            step(dve.tensor_tensor(base[:, 0], upto[:], ntiles[:], ALU.subtract))
            step(dve.tensor_scalar(base[:, 1], base[:, 0], float(P), None, ALU.mult))
            step(dve.tensor_tensor(place[:], rank_all[:], wide(base[:, 1], B * T), ALU.add))
            for j in range(TOPK):
                last = dve.tensor_tensor(places[:, :, j, :], hot_all[:, :, j, :], place[:], ALU.mult)
            step(last)
            step(dve.tensor_reduce(pos_f[:], places[:], AX_X, ALU.add))
            step(dve.tensor_copy(pos_all[:, 0:B * T], pos_f[:]))
            step(dve.memset(pos_all[:, B * T:], 0))
            step(dve.memset(w4_all[:, B * T:], 0.0))
            step(dve.tensor_tensor(passed[:], wide(upto[:], M), iota_sb[:].rearrange("p (m o) -> p m o", o=1).broadcast_to([P, M, E]), ALU.is_le))
            step(dve.tensor_tensor(passed_n[:], passed[:], wide(ntiles[:], M), ALU.mult))
            step(dve.tensor_reduce(tile_e[:, 0], passed[:], AX_X, ALU.add))
            step(dve.tensor_reduce(off_f[:, 0], passed_n[:], AX_X, ALU.add))
            step(dve.tensor_scalar(tile_e[:, 1], tile_e[:, 0], float(E - 1), None, ALU.min))
            step(dve.tensor_copy(etab[:], tile_e[:, 1]))
            step(dve.tensor_tensor(off_f[:, 1], iota_sb[:], off_f[:, 0], ALU.subtract))
            step(dve.tensor_scalar(off_f[:, 2], off_f[:, 1], float(P), None, ALU.mult))
            step(dve.scalar_tensor_tensor(out=off_f[:, 3], in0=tile_e[:, 1], scalar=float(NTOK), in1=off_f[:, 2], op0=ALU.mult, op1=ALU.add))
            step(dve.tensor_scalar(tile_e[:, 2], off_f[:, 3], float(NTOK * E - P), None, ALU.min))
            step(dve.tensor_copy(offtab[:], tile_e[:, 2]))


def experts(nc, banks, idtab, h2, ydram, wgu, wd, etab, offtab, ident_sb):
    with ExitStack() as ctx:
        sb = lambda name, shape, dt=F32: ctx.enter_context(nc.sbuf_tensor(name, shape, dt))
        sem = lambda name: ctx.enter_context(nc.semaphore(name))
        ids = [sb(f"ids{u}", [P, 1], U32) for u in range(FU)]
        xg = [sb(f"xg{u}", [P, D]) for u in range(FU)]
        xt = sb("xt", [P, FU, KD, P])
        sig = sb("sig", [P, FU, FI])
        act_out = sb("act_out", [P, FU, FI])
        at = sb("at", [P, FU, P])
        y = sb("y", [P, FU, D])
        id_loaded = [sem(f"id_loaded{u}") for u in range(FU)]
        gathered = [sem(f"gathered{u}") for u in range(FU)]
        y_stored = [sem(f"y_stored{u}") for u in range(FU)]
        gather_go = sem("gather_go")
        sp_go = sem("sp_go")
        x_turned = sem("x_turned")
        x_copied = sem("x_copied")
        gu_done = sem("gu_done")
        silu_done = sem("silu_done")
        prod_done = sem("prod_done")
        p_turned = sem("p_turned")
        p_copied = sem("p_copied")
        y_done = sem("yt_done")
        y_copied = sem("y_copied")
        M = NSLOT_TILES
        block = ctx.enter_context(nc.Block())
        h2_rows = h2.rearrange("b n d -> (b n) d")
        x_ps = banks[0:2]
        gu_ps = banks[2:4]
        p_ps = banks[4:6]
        y_ps = banks[6:8]

        def stepped(eng, step, lag=0):
            for m in range(2 * FU):
                step(m, m % FU, True)
            with eng.Fori(2, M // FU) as g:
                for u in range(FU):
                    step(g * FU + u, u, False)
            for m in range(M, M + lag):
                step(m, m % FU, True)

        @block.sync
        def _(sp):
            def step(m, u, edge):
                if not edge or m < M:
                    off = sp.value_load(offtab[0:1, bass.ds(m, 1)], min_val=0, max_val=NTOK * E - P)
                    if not edge or m >= FU:
                        sp.wait_ge(gathered[u], (m - FU - u) * (16 // FU) + 16)
                        sp.sem_inc(sp_go, 1)
                    sp.dma_start(ids[u][:], idtab[bass.ds(off, P), :]).then_inc(id_loaded[u], 16)
                if not edge or m >= STORE_LAG:
                    q, v = m - STORE_LAG, (u - STORE_LAG) % FU
                    sp.wait_ge(y_copied, q + 1)
                    sp.sem_inc(sp_go, 1)
                    sp.dma_start(ydram[bass.ds(q * P, P), :], y[:, v, :]).then_inc(y_stored[v], 16)
            stepped(sp, step, STORE_LAG)
            for u in range(FU):
                sp.wait_ge(y_stored[u], 16 * (M // FU))

        @block.gpsimd
        def _(pool):
            def step(m, u, edge):
                pool.wait_ge(id_loaded[u], (m - u) * (16 // FU) + 16)
                if not edge or m >= FU:
                    pool.wait_ge(x_turned, m - FU + 1)
                pool.sem_inc(gather_go, 1)
                pool.indirect_dma_start(xg[u][:], None, h2_rows, bass.IndirectOffsetOnAxis(ap=ids[u][:], axis=0)).then_inc(gathered[u], 16)
            stepped(pool, step)

        @block.tensor
        def _(pe):
            def step(m, u, edge):
                if not edge or m < M:
                    pe.wait_ge(gathered[u], (m - u) * (16 // FU) + 16)
                    if not edge or m >= 2:
                        pe.wait_ge(x_copied, m - 1)
                    for k in range(KD):
                        last = pe.transpose(x_ps[u % 2][:, k * P:(k + 1) * P], xg[u][:, k * P:(k + 1) * P], ident_sb[:])
                    last.then_inc(x_turned, 1)
                if not edge or 1 <= m < M + 1:
                    q, v = m - 1, (u - 1) % FU
                    e = pe.value_load(etab[0:1, bass.ds(q, 1)], min_val=0, max_val=E - 1)
                    pe.wait_ge(x_copied, q + 1)
                    if not edge or q >= 2:
                        pe.wait_ge(prod_done, q - 1)
                    for k in range(KD):
                        last = pe.matmul(gu_ps[v % 2][:, 0:2 * FI], xt[:, v, k, :], wgu[:, k, bass.ds(e, 1), :].rearrange("p o c -> p (o c)"),
                                         start=(k == 0), stop=(k == KD - 1))
                    last.then_inc(gu_done, 1)
                if not edge or 2 <= m < M + 2:
                    q, v = m - 2, (u - 2) % FU
                    pe.wait_ge(prod_done, q + 1)
                    if not edge or q >= 2:
                        pe.wait_ge(p_copied, q - 1)
                    pe.transpose(p_ps[v % 2][0:FI, 0:P], act_out[:, v, :], ident_sb[:]).then_inc(p_turned, 1)
                if not edge or 3 <= m < M + 3:
                    q, v = m - 3, (u - 3) % FU
                    e = pe.value_load(etab[0:1, bass.ds(q, 1)], min_val=0, max_val=E - 1)
                    pe.wait_ge(p_copied, q + 1)
                    if not edge or q >= 2:
                        pe.wait_ge(y_copied, q - 1)
                    pe.matmul(y_ps[v % 2][:, 0:D], at[0:FI, v, :], wd[0:FI, bass.ds(e, 1), :].rearrange("p o c -> p (o c)"),
                              start=True, stop=True).then_inc(y_done, 1)
            stepped(pe, step, 3)

        @block.scalar
        def _(act):
            def step(m, u, edge):
                if not edge or m < M:
                    act.wait_ge(x_turned, m + 1)
                    if not edge or m >= FU:
                        act.wait_ge(gu_done, m - FU + 1)
                    act.copy(xt[:, u].rearrange("p k t -> p (k t)"), x_ps[u % 2][:, 0:D]).then_inc(x_copied, 1)
                if not edge or 1 <= m < M + 1:
                    q, v = m - 1, (u - 1) % FU
                    act.wait_ge(gu_done, q + 1)
                    act.activation(sig[:, v, :], gu_ps[v % 2][:, 0:FI], ACT.Silu).then_inc(silu_done, 1)
                if not edge or 2 <= m < M + 2:
                    q, v = m - 2, (u - 2) % FU
                    act.wait_ge(p_turned, q + 1)
                    if not edge or q >= FU:
                        act.wait_ge(y_done, q - FU + 1)
                    act.copy(at[0:FI, v, :], p_ps[v % 2][0:FI, 0:P]).then_inc(p_copied, 1)
            stepped(act, step, 2)

        @block.vector
        def _(dve):
            def step(m, u, edge):
                if not edge or 1 <= m < M + 1:
                    q, v = m - 1, (u - 1) % FU
                    dve.wait_ge(silu_done, q + 1)
                    if not edge or q >= FU:
                        dve.wait_ge(p_turned, q - FU + 1)
                    dve.tensor_tensor(act_out[:, v, :], gu_ps[v % 2][:, FI:2 * FI], sig[:, v, :], ALU.mult).then_inc(prod_done, 1)
                if not edge or 3 <= m < M + 3:
                    q, v = m - 3, (u - 3) % FU
                    dve.wait_ge(y_done, q + 1)
                    if not edge or q >= FU:
                        dve.wait_ge(y_stored[v], (m - 3 - v) * (16 // FU))
                    dve.tensor_copy(y[:, v, :], y_ps[v % 2][:, 0:D]).then_inc(y_copied, 1)
            stepped(dve, step, 3)


def combine(nc, x1, rows_dram, ydram, out, w4_all, pos_all):
    with ExitStack() as ctx:
        sb = lambda name, shape, dt=F32: ctx.enter_context(nc.sbuf_tensor(name, shape, dt))
        sem = lambda name: ctx.enter_context(nc.semaphore(name))
        CU = 4
        x = [sb(f"cx{u}", [P, D]) for u in range(CU)]
        yg = [[sb(f"yg{u}_{j}", [P, D]) for j in range(TOPK)] for u in range(CU)]
        acc = sb("cacc", [P, CU, D])
        gb = sb("gb", [P, B, D])
        pos = [sb(f"pos{u}", [P, TOPK], U32) for u in range(CU)]
        w4 = sb("w4", [P, CU, TOPK])
        gb_loaded = sem("gb_loaded")
        x_loaded = [sem(f"cx_loaded{u}") for u in range(CU)]
        y_gathered = [sem(f"y_gathered{u}") for u in range(CU)]
        stored = [sem(f"out_stored{u}") for u in range(CU)]
        pos_done = sem("pos_done")
        w4_done = sem("w4c_done")
        summed = sem("summed")
        added = sem("added")
        gather_go = sem("gather_go2")
        block = ctx.enter_context(nc.Block())
        x_rows, out_rows = (a.rearrange("b n d -> (b n) d") for a in (x1, out))

        @block.sync
        def _(sp):
            sp.dma_start(gb[:].rearrange("p b d -> p (b d)"), rows_dram[0:1].rearrange("a b d -> a (b d)").broadcast_to([P, B * D])).then_inc(gb_loaded, 16)
            for u in range(CU):
                sp.sem_inc(stored[u], ONE)
            with sp.Fori(0, B) as b:
                for i in range(0, T, CU):
                    for u in range(CU):
                        sp.wait_ge(stored[u], ONE + b * (16 * T // CU) + 16 * (i // CU))
                        sp.dma_start(x[u][:], x_rows[bass.ds((b * T + i + u) * P, P), :]).then_inc(x_loaded[u], 16)
                    for u in range(CU):
                        sp.wait_ge(added, b * T + i + u + 1)
                        sp.dma_start(out_rows[bass.ds((b * T + i + u) * P, P), :], x[u][:]).then_inc(stored[u], 16)
            for u in range(CU):
                sp.wait_ge(stored[u], ONE + B * (16 * T // CU))

        @block.gpsimd
        def _(pool):
            with pool.Fori(0, B) as b:
                for i in range(T):
                    u = i % CU
                    pool.wait_ge(pos_done, b * T + i + 1)
                    pool.sem_inc(gather_go, 1)
                    for j in range(TOPK):
                        pool.indirect_dma_start(yg[u][j][:], None, ydram, bass.IndirectOffsetOnAxis(ap=pos[u][:, j:j + 1], axis=0)).then_inc(y_gathered[u], 16)

        @block.vector
        def _(dve):
            dve.wait_ge(gb_loaded, 16)

            def positions(t, u):
                dve.tensor_copy(w4[:, u, :], w4_all[:, bass.ds(t, 1), :].rearrange("p o j -> p (o j)")).then_inc(w4_done, 1)
                dve.tensor_copy(pos[u][:], pos_all[:, bass.ds(t, 1), :].rearrange("p o j -> p (o j)")).then_inc(pos_done, 1)

            for u in range(CU):
                positions(u, u)
            with dve.Fori(0, B) as b:
                for i in range(T):
                    u, t, n = i % CU, b * T + i, i * (TOPK + 1)
                    per = T * (TOPK + 1)
                    dve.wait_ge(w4_done, t + 1)
                    dve.wait_ge(y_gathered[u], b * (16 * TOPK * T // CU) + 16 * TOPK * (i // CU + 1))
                    dve.tensor_scalar(acc[:, u, :], yg[u][0][:], w4[:, u, 0:1], None, ALU.mult).then_inc(summed, 1)
                    for j in range(1, TOPK):
                        dve.wait_ge(summed, b * per + n + j)
                        dve.scalar_tensor_tensor(out=acc[:, u, :], in0=yg[u][j][:], scalar=w4[:, u, j:j + 1], in1=acc[:, u, :],
                                                 op0=ALU.mult, op1=ALU.add).then_inc(summed, 1)
                    dve.wait_ge(summed, b * per + n + TOPK)
                    dve.tensor_tensor(acc[:, u, :], acc[:, u, :], gb[:, bass.ds(b, 1), :].rearrange("p o d -> p (o d)"),
                                      ALU.mult).then_inc(summed, 1)
                    dve.wait_ge(summed, b * per + n + TOPK + 1)
                    dve.wait_ge(x_loaded[u], b * (16 * T // CU) + 16 * (i // CU + 1))
                    dve.tensor_tensor(x[u][:], x[u][:], acc[:, u, :], ALU.add).then_inc(added, 1)
                    positions(t + CU, u)


def build(nc, x, wq, wk, wv, wo, hscale, rw, gw, uw, dw, c, wmod, cos, sin, ident, causal, tri, iota_e, ebase, iota_m, tokens, out):
    dram = lambda name, shape, dt=F32: nc.dram_tensor(name, shape, dt).ap()
    wsplit = dram("wsplit", [KV, P, 2 * WG])
    rows = dram("rows", [3, B, D])
    x1 = dram("x1", [B, N, D])
    h2 = dram("h2", [B, N, D])
    idtab = dram("idtab", [NTOK * E, 1], U32)
    ydram = dram("ydram", [NSLOT_TILES * P, D])
    with ExitStack() as ctx:
        modp = ctx.enter_context(nc.sbuf_tensor("modp", [P, 6, KD, B], F32))
        ident_sb = ctx.enter_context(nc.sbuf_tensor("ident_sb", [P, P], F32))
        attention(nc, x, wq, wk, wv, wo, hscale, c, wmod, cos, sin, ident, causal, rows, modp, wsplit, x1, ident_sb)
        route(nc, x1, rows, rw, gw, uw, dw, idtab, h2, ydram, out, tri, iota_e, ebase, iota_m, tokens, ident_sb)


_INS = ['L0_attn_x', 'L0_attn_Wq', 'L0_attn_Wk', 'L0_attn_Wv', 'L0_attn_Wo', 'L0_attn_head_scale', 'L0_ffn_router_w',
        'L0_ffn_gate_w', 'L0_ffn_up_w', 'L0_ffn_down_w', 'L0_c', 'L0_wmod']


def constants():
    import numpy as np
    inv = (np.float32(1.0) / np.power(np.float32(10000.0), np.arange(0, DH, 2, dtype=np.float32) / np.float32(DH))).astype(np.float32)
    freqs = np.arange(N, dtype=np.float32)[:, None] * inv[None, :]
    emb = np.concatenate((freqs, freqs), axis=-1).T
    root = float(DH) ** -0.25
    sign = np.where(np.arange(DH) < DH // 2, -1.0, 1.0)[:, None]
    cos = (np.cos(emb.astype(np.float64)) * root).astype(np.float32)
    sin = (np.sin(emb.astype(np.float64)) * sign * root).astype(np.float32)
    causal = np.where(np.arange(P)[None, :] <= np.arange(P)[:, None], 0.0, -3e38).astype(np.float32)
    rows = lambda a: np.ascontiguousarray(np.broadcast_to(np.asarray(a, np.float32)[None, :], (P, len(a))))
    return {"cos": cos, "sin": sin, "ident": np.eye(P, dtype=np.float32), "causal": causal,
            "tri": np.triu(np.ones((P, P), np.float32), 1), "iota_e": rows(np.arange(E)),
            "ebase": rows(np.arange(E) * NTOK), "iota_m": rows(np.arange(NSLOT_TILES)),
            "tokens": (np.arange(B * T)[None, :] * P + np.arange(P)[:, None]).astype(np.uint32)}


def kernel(**inputs):
    import numpy as _np
    import concourse.bacc as _bacc
    from concourse import mybir as _mybir
    from concourse.bass_utils import run_bass_kernel_spmd as _run

    nc = _bacc.Bacc("TRN2", target_bir_lowering=False, num_devices=1)
    arrays, args = {}, []
    given = {name: _np.ascontiguousarray(inputs[name]) for name in _INS}
    given.update(constants())
    for name, a in given.items():
        arrays[f"in_{name}_dram"] = a
        args.append(nc.dram_tensor(f"in_{name}_dram", a.shape, _mybir.dt.from_np(a.dtype), kind="ExternalInput").ap())
    args.append(nc.dram_tensor("out_0_dram", (B, N, D), _mybir.dt.float32, kind="ExternalOutput").ap())
    build(nc, *args)
    r = _run(nc, [arrays], core_ids=[0])
    return r.results[0]["out_0_dram"]
```

```python
from contextlib import ExitStack

import concourse.bass as bass
from concourse import mybir

ALU = mybir.AluOpType
ACT = mybir.ActivationFunctionType
AX_X = mybir.AxisListType.X
F32 = mybir.dt.float32
F32R = mybir.dt.float32r
BF16 = mybir.dt.bfloat16
U32 = mybir.dt.uint32

P = 128
B, N, D = 4, 1024, 256
H, KV, DH = 16, 4, 128
G = H // KV
T = N // P
KD = D // P
CH = 4
CW = CH * P
NTILE = KV * T
UNITS = KV * (T // CH)
WQ = (G + 2) * DH
WG = KD * WQ + G * D
KCOL, VCOL = G * DH, (G + 1) * DH
EPS = 1e-5
ONE = 1

PROJ = ["K", "V", "Q0", "Q1", "Q2", "Q3"]


def projected_in(n):
    if n // CH + 1 >= UNITS or n % CH == CH - 1:
        return []
    return PROJ[2 * (n % CH):2 * (n % CH) + 2]


def scores_at(n, j):
    nj = n % T + 1
    return [h for h in range(G) if h * max(nj - 1, 1) // G == j] if n + 1 < NTILE else []


def tile_order(n):
    nj, proj, unit, order = n % T + 1, projected_in(n), n // CH + 1, []
    before = projected_in(n - 1) if n else []
    if n:
        order.append(("split out", n - 1))
    for j in range(nj):
        order.append(("turn", j))
        if j == 0 and before and (n - 1) % T + 1 < 3:
            order.append(("rotate", before[0], (n - 1) // CH + 1))
        if j == min(1, nj - 1) and before:
            order.append(("rotate", before[1], (n - 1) // CH + 1))
        order += [("scores", h) for h in scores_at(n, j)]
        if j == 0 and proj:
            order.append(("project", proj[0], unit))
        if n and j == min(1, nj - 1):
            order.append(("out", n - 1, 0))
        if n and j == min(2, nj - 1):
            order.append(("out", n - 1, 1))
        if j == nj - 1 and nj >= 3 and proj:
            order.append(("rotate", proj[0], unit))
        if j:
            order.append(("values", j - 1))
    if proj:
        order.append(("project", proj[1], unit))
    return order + [("values", nj - 1)]


LAST_OUT = [("out", NTILE - 1, 0), ("out", NTILE - 1, 1)]
NRING = 3


def ring_fills():
    fills = [("norm", t) for t in range(T)] + [("project", p, 0) for p in PROJ]
    for n in range(NTILE):
        for step in tile_order(n):
            if step[0] == "turn":
                fills.append(("turn", n, step[1]))
            elif step[0] in ("project", "out"):
                fills.append(step)
    return fills + LAST_OUT


FILLS = ring_fills()
FILL = {what: k for k, what in enumerate(FILLS)}
NROT = UNITS * (G + 1)
NPROJ = UNITS * len(PROJ)
NPT = T + KV * T * (T + 1) // 2
NPV = NPT - T
NS = NTILE * G


def rot_index(p, unit):
    return unit * (G + 1) + (0 if p == "K" else 1 + int(p[1]))


def proj_index(p, unit):
    return unit * len(PROJ) + PROJ.index(p)


def pt_index(n, j):
    kv, i = divmod(n, T)
    return T + kv * T * (T + 1) // 2 + i * (i + 1) // 2 + j


def attention(nc, x, wq, wk, wv, wo, hscale, c, wmod, cos, sin, ident, causal, rows_dram, modp, wsplit, x1, ident_sb):
    with ExitStack() as ctx:
        def sb(name, shape, dt=F32):
            return ctx.enter_context(nc.sbuf_tensor(name, shape, dt))

        def sem(name):
            return ctx.enter_context(nc.semaphore(name))

        wbuf = sb("wbuf", [P, 2, 2, WG], F32R)
        kbuf = sb("kbuf", [P, 2, 2, N], F32R)
        vbuf = sb("vbuf", [P, 2, 2, T, DH], F32R)
        qbuf = sb("qbuf", [P, 2, 2, G, CW], F32R)
        ht = sb("ht", [P, 2, KD, N], F32R)
        probs = sb("probs", [P, 2, G, N])
        pt = sb("pt", [P, 2, 2, G * P], F32R)
        cos_sb = sb("cos_sb", [P, N])
        sin_sb = sb("sin_sb", [P, N])
        raw = sb("raw", [P, 2, CW])
        swapped = sb("swapped", [P, 2, CW])
        rot = sb("rot", [P, 2, CW])
        o_r = sb("o_r", [P, 2, G * P], F32R)
        xacc = sb("xacc", [P, T, D])
        ysum = sb("ysum", [P, T, D])
        z = raw[:, 0, :].rearrange("p (s d) -> p s d", s=2)
        hf = raw[:, 1, :].rearrange("p (s k t) -> p s k t", s=2, k=KD)
        ga = sb("ga", [P, B, D])
        causal_sb = sb("causal_sb", [P, P], BF16)
        identb_sb = sb("identb_sb", [P, P], BF16)
        hs_sb = sb("hs_sb", [P, H])
        stats = sb("stats", [P, T, 6])
        mv = sb("mv", [P, T, 2])
        rstd = sb("rstd", [P, 2, T])
        mhalf = sb("mhalf", [P, T])
        eps = sb("eps", [P, T])
        mark = sb("mark", [P, 1])
        negmax = sb("negmax", [P, 4])
        lsum = sb("lsum", [P, 2, G])
        linv = sb("linv", [P, 2, G])
        rrow = sb("rrow", [P, 2, G])

        s_ps = ctx.enter_context(nc.psum_tensor("s_ps", [P, 2, N], F32))
        ring = ctx.enter_context(nc.psum_tensor("ring", [P, NRING, 512], F32))
        o_ps = ctx.enter_context(nc.psum_tensor("o_ps", [P, 512], F32))

        prepare(nc, ctx, sb, sem, wq, wk, wv, wo, hscale, c, wmod, cos, sin, ident, causal, wsplit,
                probs, wbuf, cos_sb, sin_sb, causal_sb, identb_sb, hs_sb, mhalf, eps, ident_sb, ga, rows_dram, modp,
                xacc, raw, swapped, rot, ysum[:, 0], ring[:, 0], ring[:, 1])

        w_loaded = [sem("w_loaded0"), sem("w_loaded1")]
        x_loaded = sem("x_loaded")
        x1_stored = sem("x1_stored")
        stats_done = sem("stats_done")
        mean_done = sem("mean_done")
        var_eps = sem("var_eps")
        rstd_done = sem("rstd_done")
        z_done = sem("z_done")
        pt_filled = sem("pt_filled")
        pt_emptied = sem("pt_emptied")
        pthi_done = sem("pthi_done")
        hhi_done = sem("hhi_done")
        hlo_done = sem("hlo_done")
        proj_filled = sem("proj_filled")
        raw_done = sem("raw_done")
        vlo_done = sem("vlo_done")
        out_filled = sem("out_filled")
        sum_done = sem("sum_done")
        swap_done = [sem("swap_done0"), sem("swap_done1")]
        cos_done = sem("cos_done")
        sin_done = sem("sin_done")
        rot_done = sem("rot_done")
        rothi_done = sem("rothi_done")
        rotlo_done = sem("rotlo_done")
        vhi_done = sem("vhi_done")
        scores_done = sem("scores_done")
        max_done = sem("max_done")
        probs_done = sem("probs_done")
        pv_done = sem("pv_done")
        linv_done = sem("linv_done")
        rrow_done = sem("rrow_done")
        ohi_done = sem("ohi_done")
        olo_done = sem("olo_done")
        gate_go = sem("gate_go")
        gated = sem("gated")
        acc_done = sem("acc_done")

        f32 = lambda ap: ap.bitcast(F32)

        def wqkv(par, half, k, col, width):
            return wbuf[:, par, half, k * WQ + col:k * WQ + col + width]

        def wo_part(par, half, h):
            return wbuf[:, par, half, KD * WQ + h * D:KD * WQ + (h + 1) * D]

        def bank(*what):
            return ring[:, FILL[what] % NRING]

        def rot_dest(p, unit, half):
            kv, c = divmod(unit, T // CH)
            if p == "K":
                return kbuf[:, kv % 2, half, c * CW:(c + 1) * CW]
            return qbuf[:, unit % 2, half, int(p[1]), :]

        block = ctx.enter_context(nc.Block())

        @block.sync
        def _(sp):
            sp.sem_inc(x1_stored, ONE)
            for g in range(2):
                sp.dma_start(wbuf[:, g].rearrange("p s w -> p (s w)").bitcast(F32), wsplit[g]).then_inc(w_loaded[g], 16)
            with sp.Fori(0, B) as b:
                sp.wait_ge(x1_stored, ONE + b * 16)
                sp.dma_start(xacc[:], x[bass.ds(b, 1), :, :].rearrange("o (t p) d -> p (o t) d", p=P)).then_inc(x_loaded, 16)

                def swap(p, unit):
                    r = rot_index(p, unit)
                    sp.wait_ge(raw_done, ONE + b * NROT + r + 1)
                    sp.dma_start(swapped[0:64, r % 2, :], raw[64:128, r % 2, :]).then_inc(swap_done[r % 2], 16)
                    sp.dma_start(swapped[64:128, r % 2, :], raw[0:64, r % 2, :]).then_inc(swap_done[r % 2], 16)

                def reload(kv):
                    sp.wait_ge(out_filled, b * 2 * NTILE + 2 * (kv + 1) * T)
                    sp.dma_start(wbuf[:, kv % 2].rearrange("p s w -> p (s w)").bitcast(F32),
                                 wsplit[(kv + 2) % KV]).then_inc(w_loaded[kv % 2], 16)

                for p in PROJ:
                    if p != "V":
                        swap(p, 0)
                for n in range(NTILE):
                    for p in projected_in(n):
                        if p != "V":
                            swap(p, n // CH + 1)
                    if n and n % T == 0:
                        reload(n // T - 1)
                reload(KV - 1)
                sp.wait_ge(acc_done, ONE + b * T + T)
                sp.dma_start(x1[bass.ds(b, 1), :, :].rearrange("o (t p) d -> p (o t) d", p=P), xacc[:]).then_inc(x1_stored, 16)
            sp.wait_ge(x1_stored, ONE + 16 * B)
            for g in range(2):
                sp.wait_ge(w_loaded[g], 16 * (1 + 2 * B))

        @block.tensor
        def _(pe):
            for started in (pv_done, pt_filled):
                pe.sem_inc(started, ONE)

            def three(out, a, w, start, stop):
                pe.matmul(out, a(0), w(0), start=start, stop=False)
                pe.matmul(out, a(0), w(1), start=False, stop=False)
                return pe.matmul(out, a(1), w(0), start=False, stop=stop)

            with pe.Fori(0, B) as b:
                def bank_free(*what):
                    k = FILL[what] - NRING
                    if k < 0:
                        return
                    kind, *which = FILLS[k]
                    if kind == "norm":
                        pe.wait_ge(pt_emptied, ONE + b * NPT + which[0] + 1)
                    elif kind == "turn":
                        pe.wait_ge(pt_emptied, ONE + b * NPT + pt_index(*which) + 1)
                    elif kind == "out":
                        pe.wait_ge(sum_done, ONE + b * NTILE * G + which[0] * G + (which[1] + 1) * G // 2)
                    elif which[0] == "V":
                        pe.wait_ge(vlo_done, b * UNITS + which[1] + 1)
                    else:
                        pe.wait_ge(raw_done, ONE + b * NROT + rot_index(*which) + 1)

                def project(p, unit):
                    kv, c = divmod(unit, T // CH)
                    into = bank("project", p, unit)
                    bank_free("project", p, unit)
                    pe.wait_ge(w_loaded[kv % 2], b * 32 + 16 * (kv // 2 + 1))
                    pe.wait_ge(hlo_done, ONE + b * T + CH * (c + 1))
                    if p == "V":
                        for t in range(CH):
                            tok = (c * CH + t) * P
                            for k in range(KD):
                                last = three(into[:, t * DH:(t + 1) * DH], lambda s: ht[:, s, k, tok:tok + P],
                                             lambda s: wqkv(kv % 2, s, k, VCOL, DH), k == 0, k == KD - 1)
                    else:
                        col = KCOL if p == "K" else int(p[1]) * DH
                        for k in range(KD):
                            last = three(into, lambda s: wqkv(kv % 2, s, k, col, DH),
                                         lambda s: ht[:, s, k, c * CW:(c + 1) * CW], k == 0, k == KD - 1)
                    last.then_inc(proj_filled, 1)

                def scores(n, h):
                    kv, i = divmod(n, T)
                    s, w, unit = n * G + h, (i + 1) * P, n // CH
                    pe.wait_ge(rotlo_done, ONE + b * NROT + unit * (G + 1) + h + 2)
                    pe.wait_ge(probs_done, ONE + b * NS + max(s - 1, 0))
                    tok = (i % CH) * P
                    for lo in range(0, w, 512):
                        hi = min(lo + 512, w)
                        diag = hi == w
                        last = three(s_ps[:, s % 2, lo:hi], lambda f: qbuf[:, unit % 2, f, h, tok:tok + P],
                                     lambda f: kbuf[:, kv % 2, f, lo:hi], True, not diag)
                    last = pe.matmul(s_ps[:, s % 2, w - P:w], identb_sb[:], causal_sb[:], start=False, stop=True)
                    last.then_inc(scores_done, 1)

                def turn(n, j):
                    if j == 0:
                        pe.wait_ge(probs_done, ONE + b * NS + (n + 1) * G)
                    bank_free("turn", n, j)
                    into = bank("turn", n, j)
                    for h in range(G):
                        last = pe.transpose(into[:, h * P:(h + 1) * P], probs[:, n % 2, h, j * P:(j + 1) * P], ident_sb[:])
                    last.then_inc(pt_filled, 1)

                def values(n, j):
                    a, kv = pt_index(n, j), n // T
                    if j == 0:
                        pe.wait_ge(olo_done, ONE + b * NTILE + n)
                        pe.wait_ge(vlo_done, b * UNITS + n // CH + 1)
                    pe.wait_ge(pt_emptied, ONE + b * NPT + a + 1)
                    three(o_ps[:, :], lambda f: vbuf[:, kv % 2, f, j, :], lambda f: pt[:, a % 2, f, :],
                          j == 0, j == n % T).then_inc(pv_done, 1)

                def project_out(n, half):
                    bank_free("out", n, half)
                    into = bank("out", n, half)
                    pe.wait_ge(olo_done, ONE + b * NTILE + n + 1)
                    for q in range(G // 2):
                        h = half * (G // 2) + q
                        last = three(into[:, q * D:(q + 1) * D], lambda f: o_r[:, f, h * P:(h + 1) * P],
                                     lambda f: wo_part(n // T % 2, f, h), True, True)
                    last.then_inc(out_filled, 1)

                pe.wait_ge(pt_emptied, ONE + b * NPT)
                pe.wait_ge(sum_done, ONE + b * NTILE * G)
                for t in range(T):
                    pe.wait_ge(z_done, b * T + t + 1)
                    bank_free("norm", t)
                    for k in range(KD):
                        last = pe.transpose(bank("norm", t)[:, k * P:(k + 1) * P], z[:, t % 2, k * P:(k + 1) * P], ident_sb[:])
                    last.then_inc(pt_filled, 1)
                for p in PROJ:
                    project(p, 0)
                for h in range(G):
                    scores(0, h)
                for n in range(NTILE):
                    for step, *which in tile_order(n):
                        if step == "turn":
                            turn(n, *which)
                        elif step == "scores":
                            scores(n + 1, *which)
                        elif step == "project":
                            project(*which)
                        elif step == "out":
                            project_out(*which)
                        elif step == "values":
                            values(n, *which)
                for _, *which in LAST_OUT:
                    project_out(*which)

        @block.scalar
        def _(act):
            for started in (raw_done, probs_done):
                act.sem_inc(started, ONE)
            with act.Fori(0, B) as b:
                def empty_proj(p, unit):
                    act.wait_ge(proj_filled, b * NPROJ + proj_index(p, unit) + 1)
                    kv, c = divmod(unit, T // CH)
                    if p == "V":
                        act.copy(vbuf[:, kv % 2, 0, c * CH:(c + 1) * CH, :].rearrange("p t d -> p (t d)"),
                                 bank("project", p, unit)).then_inc(vhi_done, 1)
                    else:
                        r = rot_index(p, unit)
                        act.wait_ge(rot_done, ONE + b * NROT + max(r - 1, 0))
                        act.copy(raw[:, r % 2, :], bank("project", p, unit)).then_inc(raw_done, 1)

                def rot_high(p, unit):
                    if p == "V":
                        return
                    r = rot_index(p, unit)
                    act.wait_ge(rot_done, ONE + b * NROT + r + 1)
                    act.copy(rot_dest(p, unit, 0), rot[:, r % 2, :]).then_inc(rothi_done, 1)

                def exps(n, h):
                    s, w = n * G + h, (n % T + 1) * P
                    act.wait_ge(max_done, b * NS + s + 1)
                    act.wait_ge(linv_done, ONE + b * NTILE + max(n - 1, 0))
                    act.activation(probs[:, n % 2, h, 0:w], s_ps[:, s % 2, 0:w], ACT.Exp, bias=negmax[:, s % 4:s % 4 + 1],
                                   scale=1.0, accum_out=lsum[:, n % 2, h:h + 1]).then_inc(probs_done, 1)

                def turned_high(n, j):
                    a = pt_index(n, j)
                    act.wait_ge(pt_filled, ONE + b * NPT + a + 1)
                    act.wait_ge(pv_done, ONE + b * NPV + max(a - T - 1, 0))
                    act.copy(pt[:, a % 2, 0, :], bank("turn", n, j)).then_inc(pthi_done, 1)

                def out_high(n):
                    act.wait_ge(pv_done, ONE + b * NPV + pt_index(n, n % T) - T + 1)
                    if n:
                        act.wait_ge(out_filled, b * 2 * NTILE + 2 * n)
                    act.copy(o_r[:, 0, :], o_ps[:, :]).then_inc(ohi_done, 1)

                for t in range(T):
                    act.wait_ge(pt_emptied, ONE + b * NPT + t + 1)
                    act.copy(ht[:, 0, :, t * P:(t + 1) * P], hf[:, t % 2]).then_inc(hhi_done, 1)
                act.wait_ge(hlo_done, ONE + b * T + T)
                for q, p in enumerate(PROJ):
                    empty_proj(p, 0)
                    if q:
                        rot_high(PROJ[q - 1], 0)
                rot_high(PROJ[-1], 0)
                for h in range(G):
                    exps(0, h)
                for n in range(NTILE):
                    open_heads = []
                    for step, *which in tile_order(n):
                        if step == "split out":
                            out_high(*which)
                        elif step == "turn":
                            turned_high(n, *which)
                        elif step == "rotate":
                            rot_high(*which)
                        elif step == "scores":
                            if len(open_heads) == 2:
                                exps(n + 1, open_heads.pop(0))
                            open_heads.append(which[0])
                            continue
                        if step in ("turn", "project"):
                            while open_heads:
                                exps(n + 1, open_heads.pop(0))
                        if step == "project":
                            empty_proj(*which)
                    while open_heads:
                        exps(n + 1, open_heads.pop(0))
                out_high(NTILE - 1)

        @block.vector
        def _(dve):
            for started in (pt_emptied, linv_done, olo_done, rot_done, sum_done):
                dve.sem_inc(started, ONE)
            with dve.Fori(0, B) as b:
                def rot_cos(p, unit):
                    if p == "V":
                        kv, c = divmod(unit, T // CH)
                        dve.wait_ge(vhi_done, b * UNITS + unit + 1)
                        dve.tensor_tensor(vbuf[:, kv % 2, 1, c * CH:(c + 1) * CH, :].rearrange("p t d -> p (t d)"),
                                          bank("project", p, unit),
                                          f32(vbuf[:, kv % 2, 0, c * CH:(c + 1) * CH, :].rearrange("p t d -> p (t d)")),
                                          ALU.subtract).then_inc(vlo_done, 1)
                        return
                    r, c = rot_index(p, unit), unit % (T // CH)
                    dve.wait_ge(raw_done, ONE + b * NROT + r + 1)
                    dve.wait_ge(rotlo_done, ONE + b * NROT + max(r - 1, 0))
                    dve.tensor_tensor(rot[:, r % 2, :], raw[:, r % 2, :], cos_sb[:, c * CW:(c + 1) * CW],
                                      ALU.mult).then_inc(cos_done, 1)

                def rot_sum(p, unit):
                    if p == "V":
                        return
                    r = rot_index(p, unit)
                    dve.wait_ge(cos_done, b * NROT + r + 1)
                    dve.wait_ge(sin_done, b * NROT + r + 1)
                    dve.tensor_tensor(rot[:, r % 2, :], rot[:, r % 2, :], swapped[:, r % 2, :],
                                      ALU.add).then_inc(rot_done, 1)

                def row_max(n, h):
                    s, w = n * G + h, (n % T + 1) * P
                    dve.wait_ge(scores_done, b * NS + s + 1)
                    dve.tensor_reduce(negmax[:, s % 4:s % 4 + 1], s_ps[:, s % 2, 0:w], AX_X, ALU.max,
                                      negate=True).then_inc(max_done, 1)

                def turned_low(n, j):
                    a = pt_index(n, j)
                    dve.wait_ge(pthi_done, b * NPV + a - T + 1)
                    dve.tensor_tensor(pt[:, a % 2, 1, :], bank("turn", n, j), f32(pt[:, a % 2, 0, :]),
                                      ALU.subtract).then_inc(pt_emptied, 1)

                def invert_sums(n):
                    dve.wait_ge(probs_done, ONE + b * NS + (n + 1) * G)
                    dve.reciprocal(linv[:, n % 2, :], lsum[:, n % 2, :]).then_inc(linv_done, 1)

                def out_low(n):
                    dve.wait_ge(ohi_done, b * NTILE + n + 1)
                    dve.tensor_tensor(o_r[:, 1, :], o_ps[:, :], f32(o_r[:, 0, :]), ALU.subtract).then_inc(olo_done, 1)

                def sum_out(n, half):
                    dve.wait_ge(out_filled, b * 2 * NTILE + 2 * n + half + 1)
                    dve.wait_ge(rrow_done, b * NTILE + n + 1)
                    for q in range(G // 2):
                        h, y = half * (G // 2) + q, bank("out", n, half)[:, q * D:(q + 1) * D]
                        t, r = ysum[:, n % T, :], rrow[:, n % 2, half * (G // 2) + q:half * (G // 2) + q + 1]
                        if n < T and h == 0:
                            dve.wait_ge(acc_done, ONE + b * T)
                            dve.tensor_scalar(t, y, r, None, ALU.mult).then_inc(sum_done, 1)
                        else:
                            dve.wait_ge(sum_done, ONE + b * NTILE * G + n * G + h)
                            dve.scalar_tensor_tensor(out=t, in0=y, scalar=r, in1=t, op0=ALU.mult, op1=ALU.add).then_inc(sum_done, 1)

                dve.wait_ge(x_loaded, b * 16 + 16)
                for t in range(T):
                    dve.bn_stats(stats[:, t, :], xacc[:, t, :]).then_inc(stats_done, 1)
                dve.wait_ge(stats_done, b * T + T)
                dve.memset(mark[:], 0.0)
                for t in range(T):
                    dve.bn_aggr(mv[:, t, :], stats[:, t, :]).then_inc(mean_done, 1)
                dve.wait_ge(rstd_done, b + 1)

                def shift(t):
                    dve.wait_ge(pt_filled, ONE + b * NPT + t + 1)
                    dve.wait_ge(hlo_done, ONE + b * T + max(t - 1, 0))
                    for k in range(KD):
                        last = dve.tensor_scalar(hf[:, t % 2, k, :], bank("norm", t)[:, k * P:(k + 1) * P],
                                                 modp[:, 1, k, bass.ds(b, 1)], modp[:, 0, k, bass.ds(b, 1)],
                                                 ALU.mult, ALU.add)
                    last.then_inc(pt_emptied, 1)

                for t in range(T):
                    dve.wait_ge(pt_filled, ONE + b * NPT + max(t - 1, 0))
                    dve.tensor_scalar(z[:, t % 2, :], xacc[:, t, :], mv[:, t, 0:1], rstd[:, 1, t:t + 1],
                                      ALU.subtract, ALU.mult).then_inc(z_done, 1)
                    if t:
                        shift(t - 1)
                shift(T - 1)
                for q, p in enumerate(PROJ):
                    rot_cos(p, 0)
                    if q:
                        rot_sum(PROJ[q - 1], 0)
                rot_sum(PROJ[-1], 0)
                for h in range(G):
                    row_max(0, h)
                for n in range(NTILE):
                    for step, *which in tile_order(n):
                        if step == "split out":
                            out_low(*which)
                        elif step == "turn":
                            turned_low(n, *which)
                            if which[0] == 0:
                                invert_sums(n)
                        elif step == "rotate":
                            rot_sum(*which)
                        elif step == "scores":
                            row_max(n + 1, *which)
                        elif step == "project":
                            rot_cos(*which)
                        elif step == "out":
                            sum_out(*which)
                out_low(NTILE - 1)
                for _, *which in LAST_OUT:
                    sum_out(*which)

        @block.gpsimd
        def _(pool):
            for started in (acc_done, hlo_done, rotlo_done):
                pool.sem_inc(started, ONE)
            with pool.Fori(0, B) as b:
                def rot_sin(p, unit):
                    if p == "V":
                        return
                    r, c = rot_index(p, unit), unit % (T // CH)
                    per = NROT // 2 * 32
                    pool.wait_ge(swap_done[r % 2], b * per + 32 * (r // 2 + 1))
                    pool.tensor_tensor(swapped[:, r % 2, :], swapped[:, r % 2, :], sin_sb[:, c * CW:(c + 1) * CW],
                                       ALU.mult).then_inc(sin_done, 1)

                def rot_low(p, unit):
                    if p == "V":
                        return
                    r = rot_index(p, unit)
                    pool.wait_ge(rothi_done, b * NROT + r + 1)
                    pool.tensor_tensor(rot_dest(p, unit, 1), rot[:, r % 2, :], f32(rot_dest(p, unit, 0)),
                                       ALU.subtract).then_inc(rotlo_done, 1)

                def scale_rows(n):
                    kv = n // T
                    pool.wait_ge(linv_done, ONE + b * NTILE + n + 1)
                    pool.wait_ge(sum_done, ONE + b * NTILE * G + max(n - 1, 0) * G)
                    pool.tensor_tensor(rrow[:, n % 2, :], linv[:, n % 2, :], hs_sb[:, kv * G:(kv + 1) * G],
                                       ALU.mult).then_inc(rrow_done, 1)

                def add_out(n):
                    t = n % T
                    pool.wait_ge(sum_done, ONE + b * NTILE * G + (n + 1) * G)
                    pool.sem_inc(gate_go, 1)
                    pool.tensor_tensor(ysum[:, t, :], ysum[:, t, :], ga[:, bass.ds(b, 1), :].rearrange("p o d -> p (o d)"),
                                       ALU.mult).then_inc(gated, 1)
                    pool.wait_ge(gated, b * T + t + 1)
                    pool.tensor_tensor(xacc[:, t, :], xacc[:, t, :], ysum[:, t, :], ALU.add).then_inc(acc_done, 1)

                pool.wait_ge(x_loaded, b * 16 + 16)
                pool.wait_ge(mean_done, b * T + T)
                pool.tensor_tensor(rstd[:, 0, :], mv[:, :, 1], eps[:], ALU.add).then_inc(var_eps, 1)
                pool.wait_ge(var_eps, b + 1)
                pool.tensor_tensor(rstd[:, 1, :], rstd[:, 0, :], mhalf[:], ALU.pow).then_inc(rstd_done, 1)
                for t in range(T):
                    pool.wait_ge(hhi_done, b * T + t + 1)
                    pool.tensor_tensor(ht[:, 1, :, t * P:(t + 1) * P], hf[:, t % 2], f32(ht[:, 0, :, t * P:(t + 1) * P]),
                                       ALU.subtract).then_inc(hlo_done, 1)
                for q, p in enumerate(PROJ):
                    rot_sin(p, 0)
                    if q:
                        rot_low(PROJ[q - 1], 0)
                rot_low(PROJ[-1], 0)
                for n in range(NTILE):
                    scale_rows(n)
                    for step, *which in tile_order(n):
                        if step == "project":
                            rot_sin(*which)
                        elif step == "rotate":
                            rot_low(*which)
                        elif step == "out" and which[0] >= NTILE - T and which[1] == 1:
                            add_out(which[0])
                add_out(NTILE - 1)


def prepare(nc, ctx, sb, sem, wq, wk, wv, wo, hscale, c, wmod, cos, sin, ident, causal, wsplit,
            probs, wbuf, cos_sb, sin_sb, causal_sb, identb_sb, hs_sb, mhalf, eps, ident_sb, ga, rows_dram, modp,
            xacc, raw, swapped, rot, o_f, ps_a, ps_b):
    flat = probs[:].rearrange("p a h n -> p (a h n)")
    wraw = [flat[:, g * WG:(g + 1) * WG] for g in range(2)]
    wm = flat[:, 2 * WG:2 * WG + KD * 6 * D].rearrange("p (k n) -> p k n", k=KD)
    c_sb = sb("c_sb", [P, KD, B])
    c_act = sb("c_act", [P, 3, KD, B])
    c_wide = xacc[:].rearrange("p t d -> p (t d)")[:, 0:KD * B * P].rearrange("p (k b c) -> p k b c", k=KD, b=B)
    gates = raw[:].rearrange("p s w -> p (s w)")[:, 0:3 * D].rearrange("p (s d) -> p s d", s=3)
    gb = swapped[:].rearrange("p s w -> p (s w)").rearrange("p (b d) -> p b d", b=B)
    shift_row = rot[:].rearrange("p s w -> p (s w)").rearrange("p (b d) -> p b d", b=B)
    scale_row = xacc[:].rearrange("p t d -> p (t d)")[:, KD * B * P:].rearrange("p (b d) -> p b d", b=B)

    const_loaded = sem("const_loaded")
    mod_loaded = sem("mod_loaded")
    wraw_loaded = [sem("wraw_loaded0"), sem("wraw_loaded1")]
    whi_done = sem("whi_done")
    wlo_done = sem("wlo_done")
    wsplit_stored = [sem("wsplit_stored0"), sem("wsplit_stored1")]
    exp_done = sem("exp_done")
    silu_steps = sem("silu_steps")
    wide_done = sem("wide_done")
    modp_filled = sem("modp_filled")
    gate_filled = sem("gate_filled")
    gate_steps = sem("gate_steps")
    mhalf_set = sem("mhalf_set")

    block_cm = nc.Block()
    with block_cm as block:
        @block.sync
        def _(sp):
            for k in range(KD):
                for bb in range(B):
                    sp.dma_start(c_sb[:, k, bb:bb + 1], c[bb:bb + 1, k * P:(k + 1) * P].rearrange("b p -> p b")).then_inc(mod_loaded, 16)
            sp.dma_start(wm, wmod.rearrange("(k p) n -> p k n", p=P)).then_inc(mod_loaded, 16)
            sp.dma_start(cos_sb[:], cos).then_inc(const_loaded, 16)
            sp.dma_start(sin_sb[:], sin).then_inc(const_loaded, 16)
            sp.dma_start(ident_sb[:], ident).then_inc(const_loaded, 16)
            sp.dma_start(o_f[:, 0:P], causal).then_inc(const_loaded, 16)
            sp.dma_start(hs_sb[:], hscale.rearrange("a h b c -> a (h b c)").broadcast_to([P, H])).then_inc(const_loaded, 16)
            for kv in range(KV):
                g = kv % 2
                if kv >= 2:
                    sp.wait_ge(wlo_done, kv - 1)
                for k in range(KD):
                    dst = wraw[g][:, k * WQ:(k + 1) * WQ]
                    rows = slice(k * P, (k + 1) * P)
                    sp.dma_start(dst[:, 0:KCOL], wq[rows, kv * KCOL:(kv + 1) * KCOL]).then_inc(wraw_loaded[g], 16)
                    sp.dma_start(dst[:, KCOL:VCOL], wk[rows, kv * DH:(kv + 1) * DH]).then_inc(wraw_loaded[g], 16)
                    sp.dma_start(dst[:, VCOL:WQ], wv[rows, kv * DH:(kv + 1) * DH]).then_inc(wraw_loaded[g], 16)
                sp.dma_start(wraw[g][:, KD * WQ:].rearrange("p (h n) -> p h n", h=G),
                             wo[kv * G * DH:(kv + 1) * G * DH, :].rearrange("(h p) n -> p h n", p=P)).then_inc(wraw_loaded[g], 16)
            for kv in range(KV):
                sp.wait_ge(wlo_done, kv + 1)
                sp.dma_start(wsplit[kv], wbuf[:, kv % 2].rearrange("p s w -> p (s w)").bitcast(F32)).then_inc(wsplit_stored[kv % 2], 16)
            for g in range(2):
                sp.wait_ge(wsplit_stored[g], 32)
            sp.wait_ge(gate_steps, 2 + 10 * B)
            for k, row in enumerate((gb, shift_row, scale_row)):
                sp.dma_start(rows_dram[k:k + 1], row[0:1]).then_inc(const_loaded, 16)
            sp.wait_ge(const_loaded, 16 * 8)

        @block.scalar
        def _(act):
            act.wait_ge(mod_loaded, 16 * (KD * B + 1))
            act.activation(c_act[:, 0], c_sb[:], ACT.Exp, scale=-1.0).then_inc(exp_done, 1)
            for kv in range(KV):
                act.wait_ge(wraw_loaded[kv % 2], 16 * (3 * KD + 1) * (kv // 2 + 1))
                if kv >= 2:
                    act.wait_ge(wsplit_stored[kv % 2], 16)
                act.copy(wbuf[:, kv % 2, 0, :], wraw[kv % 2]).then_inc(whi_done, 1)

        @block.vector
        def _(dve):
            dve.memset(mhalf[:], -0.5)
            dve.memset(eps[:], EPS).then_inc(mhalf_set, 1)
            dve.wait_ge(exp_done, 1)
            dve.tensor_scalar(c_act[:, 1], c_act[:, 0], 1.0, None, ALU.add).then_inc(silu_steps, 1)
            dve.wait_ge(silu_steps, 1)
            dve.reciprocal(c_act[:, 2], c_act[:, 1]).then_inc(silu_steps, 1)
            dve.wait_ge(silu_steps, 2)
            dve.tensor_tensor(c_act[:, 0], c_act[:, 2], c_sb[:], ALU.mult).then_inc(silu_steps, 1)
            dve.wait_ge(silu_steps, 3)
            for k in range(KD):
                last = dve.tensor_copy(c_wide[:, k], c_act[:, 0, k, :].rearrange("p (b o) -> p b o", o=1).broadcast_to([P, B, P]))
            last.then_inc(wide_done, 1)
            dve.wait_ge(modp_filled, 1)
            last = dve.tensor_copy(modp[:].rearrange("p s k b -> p (s k b)"), ps_a[:, 0:6 * KD * B])
            last.then_inc(gate_steps, 1)
            dve.wait_ge(gate_steps, 1)
            for sec in (1, 4):
                last = dve.tensor_scalar(modp[:, sec], modp[:, sec], 1.0, None, ALU.add)
            last.then_inc(gate_steps, 1)
            steps = 2
            for bb in range(B):
                for half, dest in enumerate((ga, gb)):
                    n = 2 * bb + half
                    src = ps_b[:, half * D:(half + 1) * D]
                    dve.wait_ge(gate_filled, n + 1)
                    dve.tensor_scalar(gates[:, 0], src, 0.0, 2.0, ALU.is_ge, ALU.mult).then_inc(gate_steps, 1)
                    dve.wait_ge(gate_steps, steps + 1)
                    dve.tensor_scalar(gates[:, 2], gates[:, 0], -1.0, None, ALU.add).then_inc(gate_steps, 1)
                    dve.wait_ge(gate_steps, steps + 2)
                    dve.tensor_tensor(gates[:, 1], src, gates[:, 2], ALU.mult).then_inc(gate_steps, 1)
                    dve.wait_ge(gate_steps, steps + 3)
                    dve.scalar_tensor_tensor(out=dest[:, bb, :], in0=gates[:, 1], scalar=0.25, in1=gates[:, 2],
                                             op0=ALU.max, op1=ALU.mult).then_inc(gate_steps, 1)
                    dve.wait_ge(gate_steps, steps + 4)
                    steps += 4
            for bb in range(B):
                dve.wait_ge(gate_filled, 2 * B + bb + 1)
                dve.tensor_copy(shift_row[:, bb, :], ps_b[:, 0:D]).then_inc(gate_steps, 1)
                dve.tensor_scalar(scale_row[:, bb, :], ps_b[:, D:2 * D], 1.0, None, ALU.add).then_inc(gate_steps, 1)
            for kv in range(KV):
                dve.wait_ge(whi_done, kv + 1)
                dve.tensor_tensor(wbuf[:, kv % 2, 1, :], wraw[kv % 2], wbuf[:, kv % 2, 0, :].bitcast(F32),
                                  ALU.subtract).then_inc(wlo_done, 1)

        @block.gpsimd
        def _(pool):
            pool.wait_ge(const_loaded, 16 * 5)
            pool.tensor_copy(causal_sb[:], o_f[:, 0:P])
            pool.tensor_copy(identb_sb[:], ident_sb[:]).then_inc(mhalf_set, 1)
            pool.wait_ge(mhalf_set, 2)

        @block.tensor
        def _(pe):
            pe.wait_ge(silu_steps, 3)
            pe.wait_ge(mod_loaded, 16 * (KD * B + 1))
            for sec in range(6):
                for half in range(KD):
                    col = (sec * KD + half) * B
                    for k in range(KD):
                        last = pe.matmul(ps_a[:, col:col + B], wm[:, k, sec * D + half * P:sec * D + (half + 1) * P],
                                         c_act[:, 0, k, :], start=(k == 0), stop=(k == KD - 1))
            last.then_inc(modp_filled, 1)
            pe.wait_ge(wide_done, 1)
            for bb in range(B):
                for half, sec in enumerate((2, 5)):
                    if bb or half:
                        pe.wait_ge(gate_steps, 2 + 4 * (2 * bb + half))
                    for k in range(KD):
                        last = pe.matmul(ps_b[:, half * D:(half + 1) * D], c_wide[:, k, bb, :],
                                         wm[:, k, sec * D:(sec + 1) * D], start=(k == 0), stop=(k == KD - 1))
                    last.then_inc(gate_filled, 1)
            for bb in range(B):
                pe.wait_ge(gate_steps, 2 + 8 * B + 2 * bb)
                for half, sec in enumerate((3, 4)):
                    for k in range(KD):
                        last = pe.matmul(ps_b[:, half * D:(half + 1) * D], c_wide[:, k, bb, :],
                                         wm[:, k, sec * D:(sec + 1) * D], start=(k == 0), stop=(k == KD - 1))
                last.then_inc(gate_filled, 1)


E, TOPK, FI = 32, 4, 96
NTOK = B * N
NSLOT_TILES = NTOK * TOPK // P + E
FU = 8
STORE_LAG = FU - 1


def route(nc, x1, rows_dram, rw, gw, uw, dw, idtab, h2, ydram, out, tri, iota_e, ebase, iota_m, tokens, ident_sb):
    with ExitStack() as ctx:
        def sb(name, shape, dt=F32):
            return ctx.enter_context(nc.sbuf_tensor(name, shape, dt))

        def sem(name):
            return ctx.enter_context(nc.semaphore(name))

        def bank(name, dt=F32):
            return ctx.enter_context(nc.psum_tensor(name, [P, 512], dt))

        banks = [bank(f"bank{i}") for i in range(8)]
        wgu = sb("wgu", [P, KD, E, 2 * FI])
        wd = sb("wd", [P, E, D])
        w4_all = sb("w4_all", [P, B * T + FU, TOPK])
        hot_all = sb("hot_all", [P, B * T, TOPK, E], BF16)
        rank_all = sb("rank_all", [P, B * T, E])
        totals = sb("totals", [P, E])
        etab = sb("etab", [P, NSLOT_TILES], mybir.dt.int32)
        offtab = sb("offtab", [P, NSLOT_TILES], mybir.dt.int32)
        pos_all = sb("pos_all", [P, B * T + FU, TOPK], U32)

        transposed_weights(nc, banks, gw, uw, dw, wgu, wd, ident_sb)
        route_tokens(nc, banks, x1, rows_dram, rw, idtab, h2, tri, iota_e, ebase, tokens, ident_sb,
                     w4_all, hot_all, rank_all, totals)
        place_tiles(nc, iota_m, hot_all, rank_all, totals, w4_all, etab, offtab, pos_all)
        experts(nc, banks, idtab, h2, ydram, wgu, wd, etab, offtab, ident_sb)
        combine(nc, x1, rows_dram, ydram, out, w4_all, pos_all)


def transposed_weights(nc, banks, gw, uw, dw, wgu, wd, ident_sb):
    EG = 4
    with ExitStack() as ctx:
        sb = lambda name, shape: ctx.enter_context(nc.sbuf_tensor(name, shape, F32))
        sem = lambda name: ctx.enter_context(nc.semaphore(name))
        graw = sb("graw", [P, 2, 2, EG, D])
        draw = sb("draw", [P, 2, EG, KD, FI])
        raw_loaded = [sem("raw_loaded0"), sem("raw_loaded1")]
        turned = sem("turned")
        turn_copied = sem("turn_copied")
        down_copied = sem("down_copied")
        steps = E // EG
        block = ctx.enter_context(nc.Block())

        @block.sync
        def _(sp):
            for g in range(steps):
                if g >= 2:
                    sp.wait_ge(turned, 6 * (g - 1))
                for k, w in enumerate((gw, uw)):
                    sp.dma_start(graw[0:FI, g % 2, k], w[g * EG:(g + 1) * EG].rearrange("e i d -> i e d")).then_inc(raw_loaded[g % 2], 16)
                for e in range(EG):
                    sp.dma_start(draw[:, g % 2, e], dw[g * EG + e].rearrange("(k p) i -> p k i", p=P)).then_inc(raw_loaded[g % 2], 16)

        @block.tensor
        def _(pe):
            for g in range(steps):
                pe.wait_ge(raw_loaded[g % 2], 16 * (2 + EG) * (g // 2 + 1))
                for e in range(EG):
                    if g:
                        pe.wait_ge(turn_copied, EG * (g - 1) + e + 1)
                    for k in range(KD):
                        for w in range(2):
                            last = pe.transpose(banks[e][:, (2 * k + w) * FI:(2 * k + w + 1) * FI],
                                                graw[0:FI, g % 2, w, e, k * P:(k + 1) * P], ident_sb[0:FI, 0:FI])
                    last.then_inc(turned, 1)
                for q in range(EG // 2):
                    if g:
                        pe.wait_ge(down_copied, (EG // 2) * (g - 1) + q + 1)
                    for e in range(2):
                        for k in range(KD):
                            last = pe.transpose(banks[4 + q][0:FI, (2 * e + k) * P:(2 * e + k + 1) * P],
                                                draw[:, g % 2, 2 * q + e, k, :], ident_sb[:])
                    last.then_inc(turned, 1)

        @block.vector
        def _(dve):
            for g in range(steps):
                for e in range(EG):
                    dve.wait_ge(turned, 6 * g + e + 1)
                    dve.tensor_copy(wgu[:, :, g * EG + e, :], banks[e][:, 0:4 * FI].rearrange("p (k c) -> p k c", k=KD)).then_inc(turn_copied, 1)

        @block.scalar
        def _(act):
            for g in range(steps):
                for q in range(EG // 2):
                    act.wait_ge(turned, 6 * g + EG + q + 1)
                    act.copy(wd[0:FI, g * EG + 2 * q:g * EG + 2 * q + 2, :].rearrange("p e d -> p (e d)"),
                             banks[4 + q][0:FI, :]).then_inc(down_copied, 1)


def route_tokens(nc, banks, x1, rows_dram, rw, idtab, h2, tri, iota_e, ebase, tokens, ident_sb,
                 w4_all, hot_all, rank_all, totals):
    with ExitStack() as ctx:
        sb = lambda name, shape, dt=F32: ctx.enter_context(nc.sbuf_tensor(name, shape, dt))
        sem = lambda name: ctx.enter_context(nc.semaphore(name))
        xb = sb("xb", [P, T, D])
        hb = sb("hb", [P, T, D])
        hbt = sb("hbt", [P, T, KD, P])
        mod = sb("mod", [P, 2, D])
        rwr = sb("rwr", [P, D])
        rwt = sb("rwt", [P, KD, E])
        st = sb("st", [P, T, 6])
        mv = sb("mv2", [P, T, 2])
        rstd = sb("rstd2", [P, 2, T])
        mhalf = sb("mhalf2", [P, T])
        eps = sb("eps2", [P, T])
        mark = sb("mark2", [P, 4])
        logits = sb("logits", [P, T, E])
        top = sb("top", [P, T, 8])
        top_at = sb("top_at", [P, T, 8], U32)
        at_f = sb("at_f", [P, T, TOPK])
        diff = sb("diff", [P, T, TOPK])
        e4 = sb("e4", [P, T, TOPK])
        esum = sb("esum", [P, 2, T])
        hot = sb("hot", [P, T, TOPK, E])
        mask = sb("mask", [P, T, E], BF16)
        runsum = sb("runsum", [P, E], BF16)
        batch_sum = sb("batch_sum", [P, E])
        rank = sb("rank", [P, T, E])
        slot = sb("slot", [P, T, E])
        slots = sb("slots", [P, T, TOPK, E])
        slot_f = sb("slot_f", [P, T, TOPK])
        slot_u = sb("slot_u", [P, T, TOPK], U32)
        tok = sb("tok", [P, B * T], U32)
        tokb = sb("tokb", [P, T], U32)
        tri_sb = sb("tri_sb", [P, P], BF16)
        tri_f = sb("tri_f", [P, P])
        ones = sb("ones", [P, P], BF16)
        iota_sb = sb("iota_sb", [P, E])
        ebase_sb = sb("ebase_sb", [P, E])
        zero = sb("zero", [P, NTOK * E // P], U32)

        names = """const2 zeroed tab_set in_loaded h2_stored rw_turned rwt_done stats2 mean2 var2 rstd2_done norm2 scaled2
                   h2_done turned2 turn2_copied logits_filled logits_copied top_done at_done diff_done atf_done hot_done
                   mask_done hotall_done bsum_done e4_done esum_done einv_done w4_done rank_filled rank_copied rankall_done
                   slot_done slots_done slotf_done slotu_done tokb_done scatter_go scattered runsum_done totals_filled""".split()
        s = {name: sem("q_" + name) for name in names}
        block = ctx.enter_context(nc.Block())

        @block.sync
        def _(sp):
            sp.dma_start(rwr[0:E, :], rw).then_inc(s["const2"], 16)
            sp.dma_start(tri_f[:], tri).then_inc(s["const2"], 16)
            sp.dma_start(iota_sb[:], iota_e).then_inc(s["const2"], 16)
            sp.dma_start(ebase_sb[:], ebase).then_inc(s["const2"], 16)
            sp.dma_start(tok[:], tokens).then_inc(s["const2"], 16)
            sp.wait_ge(s["zeroed"], 1)
            sp.dma_start(idtab.rearrange("(p n) o -> p (n o)", p=P), zero[:]).then_inc(s["tab_set"], 16)
            sp.sem_inc(s["h2_stored"], ONE)
            with sp.Fori(0, B) as b:
                sp.wait_ge(s["h2_stored"], ONE + b * 16)
                sp.dma_start(xb[:], x1[bass.ds(b, 1), :, :].rearrange("o (t p) d -> p (o t) d", p=P)).then_inc(s["in_loaded"], 16)
                for k in range(2):
                    sp.dma_start(mod[:, k, :], rows_dram[k + 1:k + 2, bass.ds(b, 1), :].rearrange("a b d -> a (b d)").broadcast_to([P, D])).then_inc(s["in_loaded"], 16)
                sp.wait_ge(s["h2_done"], b + 1)
                sp.dma_start(h2[bass.ds(b, 1), :, :].rearrange("o (t p) d -> p (o t) d", p=P), hb[:]).then_inc(s["h2_stored"], 16)
            sp.wait_ge(s["h2_stored"], ONE + 16 * B)
            sp.wait_ge(s["tab_set"], 16)

        @block.vector
        def _(dve):
            dve.memset(mhalf[:], -0.5)
            dve.memset(eps[:], EPS)
            dve.memset(ones[:], 1.0)
            dve.memset(zero[:], 0)
            dve.memset(runsum[:], 0.0).then_inc(s["zeroed"], 1)
            dve.wait_ge(s["rw_turned"], 1)
            dve.tensor_copy(rwt[:].rearrange("p k e -> p (k e)"), banks[7][:, 0:KD * E]).then_inc(s["rwt_done"], 1)
            dve.wait_ge(s["const2"], 16 * 5)
            dve.tensor_copy(tri_sb[:], tri_f[:]).then_inc(s["runsum_done"], ONE)
            with dve.Fori(0, B) as b:
                tiles = bass.ds(b * T, T)
                dve.wait_ge(s["in_loaded"], b * 48 + 48)
                dve.memset(mark[:, 0:1], 0.0)
                for t in range(T):
                    last = dve.bn_stats(st[:, t, :], xb[:, t, :])
                last.then_inc(s["stats2"], 1)
                dve.wait_ge(s["stats2"], b + 1)
                dve.memset(mark[:, 1:2], 0.0)
                for t in range(T):
                    last = dve.bn_aggr(mv[:, t, :], st[:, t, :])
                last.then_inc(s["mean2"], 1)
                dve.wait_ge(s["rstd2_done"], b + 1)
                for t in range(T):
                    last = dve.tensor_scalar(xb[:, t, :], xb[:, t, :], mv[:, t, 0:1], rstd[:, 1, t:t + 1], ALU.subtract, ALU.mult)
                last.then_inc(s["norm2"], 1)
                dve.wait_ge(s["norm2"], b + 1)
                dve.tensor_tensor(hb[:], xb[:], mod[:, 1:2, :].broadcast_to([P, T, D]), ALU.mult).then_inc(s["scaled2"], 1)
                dve.wait_ge(s["scaled2"], b + 1)
                dve.tensor_tensor(hb[:], hb[:], mod[:, 0:1, :].broadcast_to([P, T, D]), ALU.add).then_inc(s["h2_done"], 1)
                dve.wait_ge(s["logits_filled"], b + 1)
                dve.tensor_copy(logits[:].rearrange("p t e -> p (t e)"), banks[4][:, 0:T * E]).then_inc(s["logits_copied"], 1)
                dve.wait_ge(s["logits_copied"], b + 1)
                dve.memset(mark[:, 2:3], 0.0)
                for t in range(T):
                    last = dve.max(top[:, t, :], logits[:, t, :])
                last.then_inc(s["top_done"], 1)
                dve.wait_ge(s["top_done"], b + 1)
                dve.tensor_tensor(diff[:], top[:, :, 0:TOPK], top[:, :, 0:1].broadcast_to([P, T, TOPK]), ALU.subtract).then_inc(s["diff_done"], 1)
                for t in range(T):
                    last = dve.max_index(top_at[:, t, :], top[:, t, :], logits[:, t, :])
                last.then_inc(s["at_done"], 1)
                dve.wait_ge(s["at_done"], b + 1)
                dve.tensor_copy(at_f[:], top_at[:, :, 0:TOPK]).then_inc(s["atf_done"], 1)
                dve.wait_ge(s["atf_done"], b + 1)
                for j in range(TOPK):
                    last = dve.tensor_tensor(hot[:, :, j, :], at_f[:, :, j:j + 1].broadcast_to([P, T, E]),
                                             iota_sb[:].rearrange("p (o e) -> p o e", o=1).broadcast_to([P, T, E]), ALU.is_equal)
                last.then_inc(s["hot_done"], 1)
                dve.wait_ge(s["hot_done"], b + 1)
                dve.tensor_reduce(mask[:], hot[:].rearrange("p t j e -> p t e j"), AX_X, ALU.max).then_inc(s["mask_done"], 1)
                dve.tensor_copy(hot_all[:, tiles].rearrange("p t j e -> p (t j e)"), hot[:].rearrange("p t j e -> p (t j e)")).then_inc(s["hotall_done"], 1)
                dve.wait_ge(s["mask_done"], b + 1)
                dve.tensor_reduce(batch_sum[:], mask[:].rearrange("p t e -> p e t"), AX_X, ALU.add).then_inc(s["bsum_done"], 1)
                dve.wait_ge(s["e4_done"], b + 1)
                dve.tensor_reduce(esum[:, 0, :], e4[:], AX_X, ALU.add).then_inc(s["esum_done"], 1)
                dve.wait_ge(s["esum_done"], b + 1)
                dve.reciprocal(esum[:, 1, :], esum[:, 0, :]).then_inc(s["einv_done"], 1)
                dve.wait_ge(s["einv_done"], b + 1)
                dve.tensor_tensor(w4_all[:, tiles], e4[:], esum[:, 1, :].rearrange("p (t o) -> p t o", o=1).broadcast_to([P, T, TOPK]),
                                  ALU.mult).then_inc(s["w4_done"], 1)
                dve.wait_ge(s["rank_filled"], b + 1)
                dve.tensor_copy(rank[:].rearrange("p t e -> p (t e)"), banks[5][:, 0:T * E]).then_inc(s["rank_copied"], 1)
                dve.wait_ge(s["rank_copied"], b + 1)
                dve.tensor_copy(rank_all[:, tiles].rearrange("p t e -> p (t e)"), rank[:].rearrange("p t e -> p (t e)")).then_inc(s["rankall_done"], 1)
                dve.tensor_tensor(slot[:], rank[:], ebase_sb[:].rearrange("p (o e) -> p o e", o=1).broadcast_to([P, T, E]),
                                  ALU.add).then_inc(s["slot_done"], 1)
                dve.wait_ge(s["slot_done"], b + 1)
                for j in range(TOPK):
                    last = dve.tensor_tensor(slots[:, :, j, :], hot[:, :, j, :], slot[:], ALU.mult)
                last.then_inc(s["slots_done"], 1)
                dve.wait_ge(s["slots_done"], b + 1)
                dve.tensor_reduce(slot_f[:], slots[:], AX_X, ALU.add).then_inc(s["slotf_done"], 1)
                dve.wait_ge(s["slotf_done"], b + 1)
                dve.tensor_copy(slot_u[:], slot_f[:]).then_inc(s["slotu_done"], 1)
                dve.tensor_tensor(runsum[:], runsum[:], batch_sum[:], ALU.add).then_inc(s["runsum_done"], 1)
            dve.wait_ge(s["totals_filled"], 1)
            dve.tensor_copy(totals[:], banks[6][:, 0:E]).then_inc(s["totals_filled"], 1)
            dve.wait_ge(s["totals_filled"], 2)

        @block.scalar
        def _(act):
            with act.Fori(0, B) as b:
                for q in range(T // 2):
                    act.wait_ge(s["turned2"], b * (T // 2) + q + 1)
                    act.copy(hbt[:, 2 * q:2 * q + 2].rearrange("p t k c -> p (t k c)"), banks[q][:]).then_inc(s["turn2_copied"], 1)
                act.wait_ge(s["diff_done"], b + 1)
                act.activation(e4[:], diff[:], ACT.Exp).then_inc(s["e4_done"], 1)

        @block.tensor
        def _(pe):
            pe.wait_ge(s["const2"], 16 * 5)
            for k in range(KD):
                last = pe.transpose(banks[7][:, k * E:(k + 1) * E], rwr[0:E, k * P:(k + 1) * P], ident_sb[0:E, 0:E])
            last.then_inc(s["rw_turned"], 1)
            pe.wait_ge(s["rwt_done"], 1)
            pe.wait_ge(s["zeroed"], 1)
            with pe.Fori(0, B) as b:
                pe.wait_ge(s["h2_done"], b + 1)
                for q in range(T // 2):
                    for t in (2 * q, 2 * q + 1):
                        for k in range(KD):
                            c = ((t % 2) * KD + k) * P
                            last = pe.transpose(banks[q][:, c:c + P], hb[:, t, k * P:(k + 1) * P], ident_sb[:])
                    last.then_inc(s["turned2"], 1)
                pe.wait_ge(s["turn2_copied"], (b + 1) * (T // 2))
                for t in range(T):
                    for k in range(KD):
                        last = pe.matmul(banks[4][:, t * E:(t + 1) * E], hbt[:, t, k, :], rwt[:, k, :], start=(k == 0), stop=(k == KD - 1))
                last.then_inc(s["logits_filled"], 1)
                pe.wait_ge(s["runsum_done"], b + ONE)
                pe.wait_ge(s["mask_done"], b + 1)
                for t in range(T):
                    out = banks[5][:, t * E:(t + 1) * E]
                    pe.matmul(out, ones[:], runsum[:], start=True, stop=False)
                    for before in range(t):
                        pe.matmul(out, ones[:], mask[:, before, :], start=False, stop=False)
                    last = pe.matmul(out, tri_sb[:], mask[:, t, :], start=False, stop=True)
                last.then_inc(s["rank_filled"], 1)
            pe.wait_ge(s["runsum_done"], B + ONE)
            pe.matmul(banks[6][:, 0:E], ones[:], runsum[:], start=True, stop=True).then_inc(s["totals_filled"], 1)

        @block.gpsimd
        def _(pool):
            pool.wait_ge(s["tab_set"], 16)
            pool.wait_ge(s["zeroed"], 1)
            pool.wait_ge(s["const2"], 16 * 5)
            with pool.Fori(0, B) as b:
                pool.wait_ge(s["mean2"], b + 1)
                pool.tensor_tensor(rstd[:, 0, :], mv[:, :, 1], eps[:], ALU.add).then_inc(s["var2"], 1)
                pool.wait_ge(s["var2"], b + 1)
                pool.tensor_tensor(rstd[:, 1, :], rstd[:, 0, :], mhalf[:], ALU.pow).then_inc(s["rstd2_done"], 1)
                pool.tensor_copy(tokb[:], tok[:, bass.ds(b * T, T)]).then_inc(s["tokb_done"], 1)
                pool.wait_ge(s["tokb_done"], b + 1)
                pool.wait_ge(s["slotu_done"], b + 1)
                pool.sem_inc(s["scatter_go"], 1)
                for t in range(T):
                    for j in range(TOPK):
                        pool.indirect_dma_start(idtab, bass.IndirectOffsetOnAxis(ap=slot_u[:, t, j:j + 1], axis=0),
                                                tokb[:, t:t + 1], None).then_inc(s["scattered"], 16)
                pool.wait_ge(s["scattered"], (b + 1) * 16 * T * TOPK)


def place_tiles(nc, iota_m, hot_all, rank_all, totals, w4_all, etab, offtab, pos_all):
    with ExitStack() as ctx:
        sb = lambda name, shape, dt=F32: ctx.enter_context(nc.sbuf_tensor(name, shape, dt))
        M = NSLOT_TILES
        padded = sb("padded", [P, E])
        padded_i = sb("padded_i", [P, 2, E], mybir.dt.int32)
        ntiles = sb("ntiles", [P, E])
        ones = sb("ones_e", [P, E])
        upto = sb("upto", [P, E])
        base = sb("base", [P, 2, E])
        place = sb("place", [P, B * T, E])
        places = sb("places", [P, B * T, TOPK, E])
        pos_f = sb("pos_f", [P, B * T, TOPK])
        passed = sb("passed", [P, M, E])
        passed_n = sb("passed_n", [P, M, E])
        tile_e = sb("tile_e", [P, 3, M])
        off_f = sb("off_f", [P, 4, M])
        iota_sb = sb("iota_m_sb", [P, M])
        loaded = ctx.enter_context(nc.semaphore("iota_loaded"))
        step_done = ctx.enter_context(nc.semaphore("placing_step_done"))
        block = ctx.enter_context(nc.Block())

        @block.sync
        def _(sp):
            sp.dma_start(iota_sb[:], iota_m).then_inc(loaded, 16)

        @block.vector
        def _(dve):
            count = [0]

            def step(ins):
                count[0] += 1
                ins.then_inc(step_done, 1)
                dve.wait_ge(step_done, count[0])

            wide = lambda ap, n: ap.rearrange("p (o e) -> p o e", o=1).broadcast_to([P, n, E])
            dve.wait_ge(loaded, 16)
            step(dve.memset(ones[:], 1.0))
            step(dve.tensor_scalar(padded[:], totals[:], float(P - 1), None, ALU.add))
            step(dve.tensor_copy(padded_i[:, 0], padded[:]))
            step(dve.tensor_scalar(padded_i[:, 1], padded_i[:, 0], 7, None, ALU.arith_shift_right))
            step(dve.tensor_copy(ntiles[:], padded_i[:, 1]))
            step(dve.tensor_tensor_scan(upto[:], ones[:], ntiles[:], 0.0, ALU.mult, ALU.add))
            step(dve.tensor_tensor(base[:, 0], upto[:], ntiles[:], ALU.subtract))
            step(dve.tensor_scalar(base[:, 1], base[:, 0], float(P), None, ALU.mult))
            step(dve.tensor_tensor(place[:], rank_all[:], wide(base[:, 1], B * T), ALU.add))
            for j in range(TOPK):
                last = dve.tensor_tensor(places[:, :, j, :], hot_all[:, :, j, :], place[:], ALU.mult)
            step(last)
            step(dve.tensor_reduce(pos_f[:], places[:], AX_X, ALU.add))
            step(dve.tensor_copy(pos_all[:, 0:B * T], pos_f[:]))
            step(dve.memset(pos_all[:, B * T:], 0))
            step(dve.memset(w4_all[:, B * T:], 0.0))
            step(dve.tensor_tensor(passed[:], wide(upto[:], M), iota_sb[:].rearrange("p (m o) -> p m o", o=1).broadcast_to([P, M, E]), ALU.is_le))
            step(dve.tensor_tensor(passed_n[:], passed[:], wide(ntiles[:], M), ALU.mult))
            step(dve.tensor_reduce(tile_e[:, 0], passed[:], AX_X, ALU.add))
            step(dve.tensor_reduce(off_f[:, 0], passed_n[:], AX_X, ALU.add))
            step(dve.tensor_scalar(tile_e[:, 1], tile_e[:, 0], float(E - 1), None, ALU.min))
            step(dve.tensor_copy(etab[:], tile_e[:, 1]))
            step(dve.tensor_tensor(off_f[:, 1], iota_sb[:], off_f[:, 0], ALU.subtract))
            step(dve.tensor_scalar(off_f[:, 2], off_f[:, 1], float(P), None, ALU.mult))
            step(dve.scalar_tensor_tensor(out=off_f[:, 3], in0=tile_e[:, 1], scalar=float(NTOK), in1=off_f[:, 2], op0=ALU.mult, op1=ALU.add))
            step(dve.tensor_scalar(tile_e[:, 2], off_f[:, 3], float(NTOK * E - P), None, ALU.min))
            step(dve.tensor_copy(offtab[:], tile_e[:, 2]))


def experts(nc, banks, idtab, h2, ydram, wgu, wd, etab, offtab, ident_sb):
    with ExitStack() as ctx:
        sb = lambda name, shape, dt=F32: ctx.enter_context(nc.sbuf_tensor(name, shape, dt))
        sem = lambda name: ctx.enter_context(nc.semaphore(name))
        ids = [sb(f"ids{u}", [P, 1], U32) for u in range(FU)]
        xg = [sb(f"xg{u}", [P, D]) for u in range(FU)]
        xt = sb("xt", [P, FU, KD, P])
        sig = sb("sig", [P, FU, FI])
        act_out = sb("act_out", [P, FU, FI])
        at = sb("at", [P, FU, P])
        y = sb("y", [P, FU, D])
        id_loaded = [sem(f"id_loaded{u}") for u in range(FU)]
        gathered = [sem(f"gathered{u}") for u in range(FU)]
        y_stored = [sem(f"y_stored{u}") for u in range(FU)]
        gather_go = sem("gather_go")
        sp_go = sem("sp_go")
        x_turned = sem("x_turned")
        x_copied = sem("x_copied")
        gu_done = sem("gu_done")
        silu_done = sem("silu_done")
        prod_done = sem("prod_done")
        p_turned = sem("p_turned")
        p_copied = sem("p_copied")
        y_done = sem("yt_done")
        y_copied = sem("y_copied")
        M = NSLOT_TILES
        block = ctx.enter_context(nc.Block())
        h2_rows = h2.rearrange("b n d -> (b n) d")
        x_ps = banks[0:2]
        gu_ps = banks[2:4]
        p_ps = banks[4:6]
        y_ps = banks[6:8]

        def stepped(eng, step, lag=0):
            for m in range(2 * FU):
                step(m, m % FU, True)
            with eng.Fori(2, M // FU) as g:
                for u in range(FU):
                    step(g * FU + u, u, False)
            for m in range(M, M + lag):
                step(m, m % FU, True)

        @block.sync
        def _(sp):
            def step(m, u, edge):
                if not edge or m < M:
                    off = sp.value_load(offtab[0:1, bass.ds(m, 1)], min_val=0, max_val=NTOK * E - P)
                    if not edge or m >= FU:
                        sp.wait_ge(gathered[u], (m - FU - u) * (16 // FU) + 16)
                        sp.sem_inc(sp_go, 1)
                    sp.dma_start(ids[u][:], idtab[bass.ds(off, P), :]).then_inc(id_loaded[u], 16)
                if not edge or m >= STORE_LAG:
                    q, v = m - STORE_LAG, (u - STORE_LAG) % FU
                    sp.wait_ge(y_copied, q + 1)
                    sp.sem_inc(sp_go, 1)
                    sp.dma_start(ydram[bass.ds(q * P, P), :], y[:, v, :]).then_inc(y_stored[v], 16)
            stepped(sp, step, STORE_LAG)
            for u in range(FU):
                sp.wait_ge(y_stored[u], 16 * (M // FU))

        @block.gpsimd
        def _(pool):
            def step(m, u, edge):
                pool.wait_ge(id_loaded[u], (m - u) * (16 // FU) + 16)
                if not edge or m >= FU:
                    pool.wait_ge(x_turned, m - FU + 1)
                pool.sem_inc(gather_go, 1)
                pool.indirect_dma_start(xg[u][:], None, h2_rows, bass.IndirectOffsetOnAxis(ap=ids[u][:], axis=0)).then_inc(gathered[u], 16)
            stepped(pool, step)

        @block.tensor
        def _(pe):
            def step(m, u, edge):
                if not edge or m < M:
                    pe.wait_ge(gathered[u], (m - u) * (16 // FU) + 16)
                    if not edge or m >= 2:
                        pe.wait_ge(x_copied, m - 1)
                    for k in range(KD):
                        last = pe.transpose(x_ps[u % 2][:, k * P:(k + 1) * P], xg[u][:, k * P:(k + 1) * P], ident_sb[:])
                    last.then_inc(x_turned, 1)
                if not edge or 1 <= m < M + 1:
                    q, v = m - 1, (u - 1) % FU
                    e = pe.value_load(etab[0:1, bass.ds(q, 1)], min_val=0, max_val=E - 1)
                    pe.wait_ge(x_copied, q + 1)
                    if not edge or q >= 2:
                        pe.wait_ge(prod_done, q - 1)
                    for k in range(KD):
                        last = pe.matmul(gu_ps[v % 2][:, 0:2 * FI], xt[:, v, k, :], wgu[:, k, bass.ds(e, 1), :].rearrange("p o c -> p (o c)"),
                                         start=(k == 0), stop=(k == KD - 1))
                    last.then_inc(gu_done, 1)
                if not edge or 2 <= m < M + 2:
                    q, v = m - 2, (u - 2) % FU
                    pe.wait_ge(prod_done, q + 1)
                    if not edge or q >= 2:
                        pe.wait_ge(p_copied, q - 1)
                    pe.transpose(p_ps[v % 2][0:FI, 0:P], act_out[:, v, :], ident_sb[:]).then_inc(p_turned, 1)
                if not edge or 3 <= m < M + 3:
                    q, v = m - 3, (u - 3) % FU
                    e = pe.value_load(etab[0:1, bass.ds(q, 1)], min_val=0, max_val=E - 1)
                    pe.wait_ge(p_copied, q + 1)
                    if not edge or q >= 2:
                        pe.wait_ge(y_copied, q - 1)
                    pe.matmul(y_ps[v % 2][:, 0:D], at[0:FI, v, :], wd[0:FI, bass.ds(e, 1), :].rearrange("p o c -> p (o c)"),
                              start=True, stop=True).then_inc(y_done, 1)
            stepped(pe, step, 3)

        @block.scalar
        def _(act):
            def step(m, u, edge):
                if not edge or m < M:
                    act.wait_ge(x_turned, m + 1)
                    if not edge or m >= FU:
                        act.wait_ge(gu_done, m - FU + 1)
                    act.copy(xt[:, u].rearrange("p k t -> p (k t)"), x_ps[u % 2][:, 0:D]).then_inc(x_copied, 1)
                if not edge or 1 <= m < M + 1:
                    q, v = m - 1, (u - 1) % FU
                    act.wait_ge(gu_done, q + 1)
                    act.activation(sig[:, v, :], gu_ps[v % 2][:, 0:FI], ACT.Silu).then_inc(silu_done, 1)
                if not edge or 2 <= m < M + 2:
                    q, v = m - 2, (u - 2) % FU
                    act.wait_ge(p_turned, q + 1)
                    if not edge or q >= FU:
                        act.wait_ge(y_done, q - FU + 1)
                    act.copy(at[0:FI, v, :], p_ps[v % 2][0:FI, 0:P]).then_inc(p_copied, 1)
            stepped(act, step, 2)

        @block.vector
        def _(dve):
            def step(m, u, edge):
                if not edge or 1 <= m < M + 1:
                    q, v = m - 1, (u - 1) % FU
                    dve.wait_ge(silu_done, q + 1)
                    if not edge or q >= FU:
                        dve.wait_ge(p_turned, q - FU + 1)
                    dve.tensor_tensor(act_out[:, v, :], gu_ps[v % 2][:, FI:2 * FI], sig[:, v, :], ALU.mult).then_inc(prod_done, 1)
                if not edge or 3 <= m < M + 3:
                    q, v = m - 3, (u - 3) % FU
                    dve.wait_ge(y_done, q + 1)
                    if not edge or q >= FU:
                        dve.wait_ge(y_stored[v], (m - 3 - v) * (16 // FU))
                    dve.tensor_copy(y[:, v, :], y_ps[v % 2][:, 0:D]).then_inc(y_copied, 1)
            stepped(dve, step, 3)


def combine(nc, x1, rows_dram, ydram, out, w4_all, pos_all):
    with ExitStack() as ctx:
        sb = lambda name, shape, dt=F32: ctx.enter_context(nc.sbuf_tensor(name, shape, dt))
        sem = lambda name: ctx.enter_context(nc.semaphore(name))
        CU = 4
        x = [sb(f"cx{u}", [P, D]) for u in range(CU)]
        yg = [[sb(f"yg{u}_{j}", [P, D]) for j in range(TOPK)] for u in range(CU)]
        acc = sb("cacc", [P, CU, D])
        gb = sb("gb", [P, B, D])
        pos = [sb(f"pos{u}", [P, TOPK], U32) for u in range(CU)]
        w4 = sb("w4", [P, CU, TOPK])
        gb_loaded = sem("gb_loaded")
        x_loaded = [sem(f"cx_loaded{u}") for u in range(CU)]
        y_gathered = [sem(f"y_gathered{u}") for u in range(CU)]
        stored = [sem(f"out_stored{u}") for u in range(CU)]
        pos_done = sem("pos_done")
        w4_done = sem("w4c_done")
        summed = sem("summed")
        added = sem("added")
        gather_go = sem("gather_go2")
        block = ctx.enter_context(nc.Block())
        x_rows, out_rows = (a.rearrange("b n d -> (b n) d") for a in (x1, out))

        @block.sync
        def _(sp):
            sp.dma_start(gb[:].rearrange("p b d -> p (b d)"), rows_dram[0:1].rearrange("a b d -> a (b d)").broadcast_to([P, B * D])).then_inc(gb_loaded, 16)
            for u in range(CU):
                sp.sem_inc(stored[u], ONE)
            with sp.Fori(0, B) as b:
                for i in range(0, T, CU):
                    for u in range(CU):
                        sp.wait_ge(stored[u], ONE + b * (16 * T // CU) + 16 * (i // CU))
                        sp.dma_start(x[u][:], x_rows[bass.ds((b * T + i + u) * P, P), :]).then_inc(x_loaded[u], 16)
                    for u in range(CU):
                        sp.wait_ge(added, b * T + i + u + 1)
                        sp.dma_start(out_rows[bass.ds((b * T + i + u) * P, P), :], x[u][:]).then_inc(stored[u], 16)
            for u in range(CU):
                sp.wait_ge(stored[u], ONE + B * (16 * T // CU))

        @block.gpsimd
        def _(pool):
            with pool.Fori(0, B) as b:
                for i in range(T):
                    u = i % CU
                    pool.wait_ge(pos_done, b * T + i + 1)
                    pool.sem_inc(gather_go, 1)
                    for j in range(TOPK):
                        pool.indirect_dma_start(yg[u][j][:], None, ydram, bass.IndirectOffsetOnAxis(ap=pos[u][:, j:j + 1], axis=0)).then_inc(y_gathered[u], 16)

        @block.vector
        def _(dve):
            dve.wait_ge(gb_loaded, 16)

            def positions(t, u):
                dve.tensor_copy(w4[:, u, :], w4_all[:, bass.ds(t, 1), :].rearrange("p o j -> p (o j)")).then_inc(w4_done, 1)
                dve.tensor_copy(pos[u][:], pos_all[:, bass.ds(t, 1), :].rearrange("p o j -> p (o j)")).then_inc(pos_done, 1)

            for u in range(CU):
                positions(u, u)
            with dve.Fori(0, B) as b:
                for i in range(T):
                    u, t, n = i % CU, b * T + i, i * (TOPK + 1)
                    per = T * (TOPK + 1)
                    dve.wait_ge(w4_done, t + 1)
                    dve.wait_ge(y_gathered[u], b * (16 * TOPK * T // CU) + 16 * TOPK * (i // CU + 1))
                    dve.tensor_scalar(acc[:, u, :], yg[u][0][:], w4[:, u, 0:1], None, ALU.mult).then_inc(summed, 1)
                    for j in range(1, TOPK):
                        dve.wait_ge(summed, b * per + n + j)
                        dve.scalar_tensor_tensor(out=acc[:, u, :], in0=yg[u][j][:], scalar=w4[:, u, j:j + 1], in1=acc[:, u, :],
                                                 op0=ALU.mult, op1=ALU.add).then_inc(summed, 1)
                    dve.wait_ge(summed, b * per + n + TOPK)
                    dve.tensor_tensor(acc[:, u, :], acc[:, u, :], gb[:, bass.ds(b, 1), :].rearrange("p o d -> p (o d)"),
                                      ALU.mult).then_inc(summed, 1)
                    dve.wait_ge(summed, b * per + n + TOPK + 1)
                    dve.wait_ge(x_loaded[u], b * (16 * T // CU) + 16 * (i // CU + 1))
                    dve.tensor_tensor(x[u][:], x[u][:], acc[:, u, :], ALU.add).then_inc(added, 1)
                    positions(t + CU, u)


def build(nc, x, wq, wk, wv, wo, hscale, rw, gw, uw, dw, c, wmod, cos, sin, ident, causal, tri, iota_e, ebase, iota_m, tokens, out):
    dram = lambda name, shape, dt=F32: nc.dram_tensor(name, shape, dt).ap()
    wsplit = dram("wsplit", [KV, P, 2 * WG])
    rows = dram("rows", [3, B, D])
    x1 = dram("x1", [B, N, D])
    h2 = dram("h2", [B, N, D])
    idtab = dram("idtab", [NTOK * E, 1], U32)
    ydram = dram("ydram", [NSLOT_TILES * P, D])
    with ExitStack() as ctx:
        modp = ctx.enter_context(nc.sbuf_tensor("modp", [P, 6, KD, B], F32))
        ident_sb = ctx.enter_context(nc.sbuf_tensor("ident_sb", [P, P], F32))
        attention(nc, x, wq, wk, wv, wo, hscale, c, wmod, cos, sin, ident, causal, rows, modp, wsplit, x1, ident_sb)
        route(nc, x1, rows, rw, gw, uw, dw, idtab, h2, ydram, out, tri, iota_e, ebase, iota_m, tokens, ident_sb)


_INS = ['L0_attn_x', 'L0_attn_Wq', 'L0_attn_Wk', 'L0_attn_Wv', 'L0_attn_Wo', 'L0_attn_head_scale', 'L0_ffn_router_w',
        'L0_ffn_gate_w', 'L0_ffn_up_w', 'L0_ffn_down_w', 'L0_c', 'L0_wmod']


def constants():
    import numpy as np
    inv = (np.float32(1.0) / np.power(np.float32(10000.0), np.arange(0, DH, 2, dtype=np.float32) / np.float32(DH))).astype(np.float32)
    freqs = np.arange(N, dtype=np.float32)[:, None] * inv[None, :]
    emb = np.concatenate((freqs, freqs), axis=-1).T
    root = float(DH) ** -0.25
    sign = np.where(np.arange(DH) < DH // 2, -1.0, 1.0)[:, None]
    cos = (np.cos(emb.astype(np.float64)) * root).astype(np.float32)
    sin = (np.sin(emb.astype(np.float64)) * sign * root).astype(np.float32)
    causal = np.where(np.arange(P)[None, :] <= np.arange(P)[:, None], 0.0, -3e38).astype(np.float32)
    rows = lambda a: np.ascontiguousarray(np.broadcast_to(np.asarray(a, np.float32)[None, :], (P, len(a))))
    return {"cos": cos, "sin": sin, "ident": np.eye(P, dtype=np.float32), "causal": causal,
            "tri": np.triu(np.ones((P, P), np.float32), 1), "iota_e": rows(np.arange(E)),
            "ebase": rows(np.arange(E) * NTOK), "iota_m": rows(np.arange(NSLOT_TILES)),
            "tokens": (np.arange(B * T)[None, :] * P + np.arange(P)[:, None]).astype(np.uint32)}


def kernel(**inputs):
    import numpy as _np
    import concourse.bacc as _bacc
    from concourse import mybir as _mybir
    from concourse.bass_utils import run_bass_kernel_spmd as _run

    nc = _bacc.Bacc("TRN2", target_bir_lowering=False, num_devices=1)
    arrays, args = {}, []
    given = {name: _np.ascontiguousarray(inputs[name]) for name in _INS}
    given.update(constants())
    for name, a in given.items():
        arrays[f"in_{name}_dram"] = a
        args.append(nc.dram_tensor(f"in_{name}_dram", a.shape, _mybir.dt.from_np(a.dtype), kind="ExternalInput").ap())
    args.append(nc.dram_tensor("out_0_dram", (B, N, D), _mybir.dt.float32, kind="ExternalOutput").ap())
    build(nc, *args)
    r = _run(nc, [arrays], core_ids=[0])
    return r.results[0]["out_0_dram"]
```

```python
from contextlib import ExitStack

import concourse.bass as bass
from concourse import mybir

ALU = mybir.AluOpType
ACT = mybir.ActivationFunctionType
AX_X = mybir.AxisListType.X
F32 = mybir.dt.float32
F32R = mybir.dt.float32r
BF16 = mybir.dt.bfloat16
U32 = mybir.dt.uint32

P = 128
B, N, D = 4, 1024, 256
H, KV, DH = 16, 4, 128
G = H // KV
T = N // P
KD = D // P
CH = 4
CW = CH * P
NTILE = KV * T
UNITS = KV * (T // CH)
WQ = (G + 2) * DH
WG = KD * WQ + G * D
KCOL, VCOL = G * DH, (G + 1) * DH
EPS = 1e-5
ONE = 1

PROJ = ["K", "V", "Q0", "Q1", "Q2", "Q3"]


def projected_in(n):
    if n // CH + 1 >= UNITS or n % CH == CH - 1:
        return []
    return PROJ[2 * (n % CH):2 * (n % CH) + 2]


def scores_at(n, j):
    nj = n % T + 1
    return [h for h in range(G) if h * max(nj - 1, 1) // G == j] if n + 1 < NTILE else []


def tile_order(n):
    nj, proj, unit, order = n % T + 1, projected_in(n), n // CH + 1, []
    before = projected_in(n - 1) if n else []
    late = n > 0 and not proj
    if n:
        order.append(("split out", n - 1))
    for j in range(nj):
        order.append(("turn", j))
        if j == 0 and before and (n - 1) % T + 1 < 3:
            order.append(("rotate", before[0], (n - 1) // CH + 1))
        if j == min(1, nj - 1) and before:
            order.append(("rotate", before[1], (n - 1) // CH + 1))
        order += [("scores", h) for h in scores_at(n, j)]
        if j == 0 and proj:
            order.append(("project", proj[0], unit))
        if n and j == min(1, nj - 1):
            order.append(("out", n - 1, 0))
        if n and j == min(2, nj - 1) and not late:
            order.append(("out", n - 1, 1))
        if j == nj - 1 and nj >= 3 and proj:
            order.append(("rotate", proj[0], unit))
        if j:
            order.append(("values", j - 1))
    if proj:
        order.append(("project", proj[1], unit))
    if late:
        order.append(("out", n - 1, 1))
    return order + [("values", nj - 1)]


LAST_OUT = [("out", NTILE - 1, 0), ("out", NTILE - 1, 1)]
NRING = 3


def ring_fills():
    fills = [("norm", t) for t in range(T)] + [("project", p, 0) for p in PROJ]
    for n in range(NTILE):
        for step in tile_order(n):
            if step[0] == "turn":
                fills.append(("turn", n, step[1]))
            elif step[0] in ("project", "out"):
                fills.append(step)
    return fills + LAST_OUT


FILLS = ring_fills()
FILL = {what: k for k, what in enumerate(FILLS)}
NROT = UNITS * (G + 1)
NPROJ = UNITS * len(PROJ)
NPT = T + KV * T * (T + 1) // 2
NPV = NPT - T
NS = NTILE * G


def rot_index(p, unit):
    return unit * (G + 1) + (0 if p == "K" else 1 + int(p[1]))


def proj_index(p, unit):
    return unit * len(PROJ) + PROJ.index(p)


def pt_index(n, j):
    kv, i = divmod(n, T)
    return T + kv * T * (T + 1) // 2 + i * (i + 1) // 2 + j


def attention(nc, x, wq, wk, wv, wo, hscale, c, wmod, cos, sin, ident, causal, rows_dram, modp, wsplit, x1, ident_sb):
    with ExitStack() as ctx:
        def sb(name, shape, dt=F32):
            return ctx.enter_context(nc.sbuf_tensor(name, shape, dt))

        def sem(name):
            return ctx.enter_context(nc.semaphore(name))

        wbuf = sb("wbuf", [P, 2, 2, WG], F32R)
        kbuf = sb("kbuf", [P, 2, 2, N], F32R)
        vbuf = sb("vbuf", [P, 2, 2, T, DH], F32R)
        qbuf = sb("qbuf", [P, 2, 2, G, CW], F32R)
        ht = sb("ht", [P, 2, KD, N], F32R)
        probs = sb("probs", [P, 2, G, N])
        pt = sb("pt", [P, 2, 2, G * P], F32R)
        cos_sb = sb("cos_sb", [P, N])
        sin_sb = sb("sin_sb", [P, N])
        raw = sb("raw", [P, 2, CW])
        swapped = sb("swapped", [P, 2, CW])
        rot = sb("rot", [P, 2, CW])
        o_r = sb("o_r", [P, 2, G * P], F32R)
        xacc = sb("xacc", [P, T, D])
        ysum = sb("ysum", [P, T, D])
        z = raw[:, 0, :].rearrange("p (s d) -> p s d", s=2)
        hf = raw[:, 1, :].rearrange("p (s k t) -> p s k t", s=2, k=KD)
        ga = sb("ga", [P, B, D])
        causal_sb = sb("causal_sb", [P, P], BF16)
        identb_sb = sb("identb_sb", [P, P], BF16)
        hs_sb = sb("hs_sb", [P, H])
        stats = sb("stats", [P, T, 6])
        mv = sb("mv", [P, T, 2])
        rstd = sb("rstd", [P, 2, T])
        mhalf = sb("mhalf", [P, T])
        eps = sb("eps", [P, T])
        mark = sb("mark", [P, 1])
        negmax = sb("negmax", [P, 4])
        lsum = sb("lsum", [P, 2, G])
        linv = sb("linv", [P, 2, G])
        rrow = sb("rrow", [P, 2, G])

        s_ps = ctx.enter_context(nc.psum_tensor("s_ps", [P, 2, N], F32))
        ring = ctx.enter_context(nc.psum_tensor("ring", [P, NRING, 512], F32))
        o_ps = ctx.enter_context(nc.psum_tensor("o_ps", [P, 512], F32))

        f32 = lambda ap: ap.bitcast(F32)
        wsplit_stored = [sem("wsplit_stored0"), sem("wsplit_stored1")]
        prepare(nc, ctx, sb, sem, wq, wk, wv, wo, hscale, c, wmod, cos, sin, ident, causal, wsplit,
                probs, wbuf, cos_sb, sin_sb, causal_sb, identb_sb, hs_sb, mhalf, eps, ident_sb, ga, rows_dram, modp,
                xacc, raw, swapped, rot, ysum, s_ps, ring, o_ps, wsplit_stored)

        w_loaded = [sem("w_loaded0"), sem("w_loaded1")]
        x_loaded = [sem("x_loaded0"), sem("x_loaded1")]
        x1_stored = [sem("x1_stored0"), sem("x1_stored1")]
        stats_done = sem("stats_done")
        mean_done = sem("mean_done")
        var_eps = sem("var_eps")
        rstd_done = sem("rstd_done")
        z_done = sem("z_done")
        pt_filled = sem("pt_filled")
        pt_emptied = sem("pt_emptied")
        pthi_done = sem("pthi_done")
        hhi_done = sem("hhi_done")
        hlo_done = sem("hlo_done")
        proj_filled = sem("proj_filled")
        raw_done = sem("raw_done")
        vlo_done = sem("vlo_done")
        out_filled = sem("out_filled")
        sum_done = sem("sum_done")
        swap_done = [sem("swap_done0"), sem("swap_done1")]
        cos_done = sem("cos_done")
        sin_done = sem("sin_done")
        rot_done = sem("rot_done")
        rothi_done = sem("rothi_done")
        rotlo_done = sem("rotlo_done")
        vhi_done = sem("vhi_done")
        scores_done = sem("scores_done")
        max_done = sem("max_done")
        probs_done = sem("probs_done")
        pv_done = sem("pv_done")
        linv_done = sem("linv_done")
        rrow_done = sem("rrow_done")
        ohi_done = sem("ohi_done")
        olo_done = sem("olo_done")
        gate_go = sem("gate_go")
        gated = sem("gated")
        acc_done = sem("acc_done")

        def wqkv(par, half, k, col, width):
            return wbuf[:, par, half, k * WQ + col:k * WQ + col + width]

        def wo_part(par, half, h):
            return wbuf[:, par, half, KD * WQ + h * D:KD * WQ + (h + 1) * D]

        def bank(*what):
            return ring[:, FILL[what] % NRING]

        def tiles_of(rows, b, g):
            return rows[bass.ds(b, 1), g * CW:(g + 1) * CW, :].rearrange("o (t p) d -> p (o t) d", p=P)

        def rot_dest(p, unit, half):
            kv, c = divmod(unit, T // CH)
            if p == "K":
                return kbuf[:, kv % 2, half, c * CW:(c + 1) * CW]
            return qbuf[:, unit % 2, half, int(p[1]), :]

        block = ctx.enter_context(nc.Block())

        @block.sync
        def _(sp):
            for g in range(2):
                sp.sem_inc(x1_stored[g], ONE)
            for g in range(2):
                sp.sem_inc(w_loaded[g], 16)

            def batch(b, first):
                for g in range(2):
                    sp.wait_ge(x1_stored[g], ONE + b * 16)
                    sp.dma_start(xacc[:, g * CH:(g + 1) * CH], tiles_of(x, b, g)).then_inc(x_loaded[g], 16)
                if first:
                    for g in range(2):
                        sp.dma_start(wsplit[g], wbuf[:, g].rearrange("p s w -> p (s w)").bitcast(F32)).then_inc(wsplit_stored[g], 16)

                def swap(p, unit):
                    r = rot_index(p, unit)
                    sp.wait_ge(raw_done, ONE + b * NROT + r + 1)
                    sp.dma_start(swapped[0:64, r % 2, :], raw[64:128, r % 2, :]).then_inc(swap_done[r % 2], 16)
                    sp.dma_start(swapped[64:128, r % 2, :], raw[0:64, r % 2, :]).then_inc(swap_done[r % 2], 16)

                def reload(kv, done):
                    sp.wait_ge(out_filled, b * 2 * NTILE + 2 * done)
                    sp.wait_ge(wsplit_stored[kv % 2], 32)
                    sp.dma_start(wbuf[:, kv % 2].rearrange("p s w -> p (s w)").bitcast(F32),
                                 wsplit[(kv + 2) % KV]).then_inc(w_loaded[kv % 2], 16)

                if not first:
                    reload(KV - 1, 0)
                for p in PROJ:
                    if p != "V":
                        swap(p, 0)
                for n in range(NTILE):
                    for p in projected_in(n):
                        if p != "V":
                            swap(p, n // CH + 1)
                    if n and n % T == 0:
                        reload(n // T - 1, n)
                for g in range(2):
                    sp.wait_ge(acc_done, ONE + b * T + (g + 1) * CH)
                    sp.dma_start(tiles_of(x1, b, g), xacc[:, g * CH:(g + 1) * CH]).then_inc(x1_stored[g], 16)

            batch(0, True)
            with sp.Fori(1, B) as b:
                batch(b, False)
            for g in range(2):
                sp.wait_ge(x1_stored[g], ONE + 16 * B)
            for g in range(2):
                sp.wait_ge(w_loaded[g], 16 * (1 + 2 * B - g))

        @block.tensor
        def _(pe):
            for started in (pv_done, pt_filled):
                pe.sem_inc(started, ONE)

            def three(out, a, w, start, stop):
                pe.matmul(out, a(0), w(0), start=start, stop=False)
                pe.matmul(out, a(0), w(1), start=False, stop=False)
                return pe.matmul(out, a(1), w(0), start=False, stop=stop)

            with pe.Fori(0, B) as b:
                def bank_free(*what):
                    k = FILL[what] - NRING
                    if k < 0:
                        return
                    kind, *which = FILLS[k]
                    if kind == "norm":
                        pe.wait_ge(pt_emptied, ONE + b * NPT + which[0] + 1)
                    elif kind == "turn":
                        pe.wait_ge(pt_emptied, ONE + b * NPT + pt_index(*which) + 1)
                    elif kind == "out":
                        pe.wait_ge(sum_done, ONE + b * NTILE * G + which[0] * G + (which[1] + 1) * G // 2)
                    elif which[0] == "V":
                        pe.wait_ge(vlo_done, b * UNITS + which[1] + 1)
                    else:
                        pe.wait_ge(raw_done, ONE + b * NROT + rot_index(*which) + 1)

                def project(p, unit):
                    kv, c = divmod(unit, T // CH)
                    into = bank("project", p, unit)
                    bank_free("project", p, unit)
                    pe.wait_ge(w_loaded[kv % 2], b * 32 + 16 * (kv // 2 + 1))
                    pe.wait_ge(hlo_done, ONE + b * T + CH * (c + 1))
                    if p == "V":
                        for t in range(CH):
                            tok = (c * CH + t) * P
                            for k in range(KD):
                                last = three(into[:, t * DH:(t + 1) * DH], lambda s: ht[:, s, k, tok:tok + P],
                                             lambda s: wqkv(kv % 2, s, k, VCOL, DH), k == 0, k == KD - 1)
                    else:
                        col = KCOL if p == "K" else int(p[1]) * DH
                        for k in range(KD):
                            last = three(into, lambda s: wqkv(kv % 2, s, k, col, DH),
                                         lambda s: ht[:, s, k, c * CW:(c + 1) * CW], k == 0, k == KD - 1)
                    last.then_inc(proj_filled, 1)

                def scores(n, h):
                    kv, i = divmod(n, T)
                    s, w, unit = n * G + h, (i + 1) * P, n // CH
                    pe.wait_ge(rotlo_done, ONE + b * NROT + unit * (G + 1) + h + 2)
                    pe.wait_ge(probs_done, ONE + b * NS + max(s - 1, 0))
                    tok = (i % CH) * P
                    for lo in range(0, w, 512):
                        hi = min(lo + 512, w)
                        diag = hi == w
                        last = three(s_ps[:, s % 2, lo:hi], lambda f: qbuf[:, unit % 2, f, h, tok:tok + P],
                                     lambda f: kbuf[:, kv % 2, f, lo:hi], True, not diag)
                    last = pe.matmul(s_ps[:, s % 2, w - P:w], identb_sb[:], causal_sb[:], start=False, stop=True)
                    last.then_inc(scores_done, 1)

                def turn(n, j):
                    if j == 0:
                        pe.wait_ge(probs_done, ONE + b * NS + (n + 1) * G)
                    bank_free("turn", n, j)
                    into = bank("turn", n, j)
                    for h in range(G):
                        last = pe.transpose(into[:, h * P:(h + 1) * P], probs[:, n % 2, h, j * P:(j + 1) * P], ident_sb[:])
                    last.then_inc(pt_filled, 1)

                def values(n, j):
                    a, kv = pt_index(n, j), n // T
                    if j == 0:
                        pe.wait_ge(olo_done, ONE + b * NTILE + n)
                        pe.wait_ge(vlo_done, b * UNITS + n // CH + 1)
                    pe.wait_ge(pt_emptied, ONE + b * NPT + a + 1)
                    three(o_ps[:, :], lambda f: vbuf[:, kv % 2, f, j, :], lambda f: pt[:, a % 2, f, :],
                          j == 0, j == n % T).then_inc(pv_done, 1)

                def project_out(n, half):
                    bank_free("out", n, half)
                    into = bank("out", n, half)
                    pe.wait_ge(olo_done, ONE + b * NTILE + n + 1)
                    for q in range(G // 2):
                        h = half * (G // 2) + q
                        last = three(into[:, q * D:(q + 1) * D], lambda f: o_r[:, f, h * P:(h + 1) * P],
                                     lambda f: wo_part(n // T % 2, f, h), True, True)
                    last.then_inc(out_filled, 1)

                pe.wait_ge(pt_emptied, ONE + b * NPT)
                pe.wait_ge(sum_done, ONE + b * NTILE * G)
                for t in range(T):
                    pe.wait_ge(z_done, b * T + t + 1)
                    bank_free("norm", t)
                    for k in range(KD):
                        last = pe.transpose(bank("norm", t)[:, k * P:(k + 1) * P], z[:, t % 2, k * P:(k + 1) * P], ident_sb[:])
                    last.then_inc(pt_filled, 1)
                for p in PROJ:
                    project(p, 0)
                for h in range(G):
                    scores(0, h)
                for n in range(NTILE):
                    for step, *which in tile_order(n):
                        if step == "turn":
                            turn(n, *which)
                        elif step == "scores":
                            scores(n + 1, *which)
                        elif step == "project":
                            project(*which)
                        elif step == "out":
                            project_out(*which)
                        elif step == "values":
                            values(n, *which)
                for _, *which in LAST_OUT:
                    project_out(*which)

        @block.scalar
        def _(act):
            for started in (raw_done, probs_done):
                act.sem_inc(started, ONE)
            with act.Fori(0, B) as b:
                def empty_proj(p, unit):
                    act.wait_ge(proj_filled, b * NPROJ + proj_index(p, unit) + 1)
                    kv, c = divmod(unit, T // CH)
                    if p == "V":
                        act.copy(vbuf[:, kv % 2, 0, c * CH:(c + 1) * CH, :].rearrange("p t d -> p (t d)"),
                                 bank("project", p, unit)).then_inc(vhi_done, 1)
                    else:
                        r = rot_index(p, unit)
                        act.wait_ge(rot_done, ONE + b * NROT + max(r - 1, 0))
                        act.copy(raw[:, r % 2, :], bank("project", p, unit)).then_inc(raw_done, 1)

                def rot_high(p, unit):
                    if p == "V":
                        return
                    r = rot_index(p, unit)
                    act.wait_ge(rot_done, ONE + b * NROT + r + 1)
                    act.copy(rot_dest(p, unit, 0), rot[:, r % 2, :]).then_inc(rothi_done, 1)

                def exps(n, h):
                    s, w = n * G + h, (n % T + 1) * P
                    act.wait_ge(max_done, b * NS + s + 1)
                    act.wait_ge(linv_done, ONE + b * NTILE + max(n - 1, 0))
                    act.activation(probs[:, n % 2, h, 0:w], s_ps[:, s % 2, 0:w], ACT.Exp, bias=negmax[:, s % 4:s % 4 + 1],
                                   scale=1.0, accum_out=lsum[:, n % 2, h:h + 1]).then_inc(probs_done, 1)

                def turned_high(n, j):
                    a = pt_index(n, j)
                    act.wait_ge(pt_filled, ONE + b * NPT + a + 1)
                    act.wait_ge(pv_done, ONE + b * NPV + max(a - T - 1, 0))
                    act.copy(pt[:, a % 2, 0, :], bank("turn", n, j)).then_inc(pthi_done, 1)

                def out_high(n):
                    act.wait_ge(pv_done, ONE + b * NPV + pt_index(n, n % T) - T + 1)
                    if n:
                        act.wait_ge(out_filled, b * 2 * NTILE + 2 * n)
                    act.copy(o_r[:, 0, :], o_ps[:, :]).then_inc(ohi_done, 1)

                for t in range(T):
                    act.wait_ge(pt_emptied, ONE + b * NPT + t + 1)
                    act.copy(ht[:, 0, :, t * P:(t + 1) * P], hf[:, t % 2]).then_inc(hhi_done, 1)
                act.wait_ge(hlo_done, ONE + b * T + T)
                for q, p in enumerate(PROJ):
                    empty_proj(p, 0)
                    if q:
                        rot_high(PROJ[q - 1], 0)
                rot_high(PROJ[-1], 0)
                for h in range(G):
                    exps(0, h)
                for n in range(NTILE):
                    open_heads = []
                    for step, *which in tile_order(n):
                        if step == "split out":
                            out_high(*which)
                        elif step == "turn":
                            turned_high(n, *which)
                        elif step == "rotate":
                            rot_high(*which)
                        elif step == "scores":
                            if len(open_heads) == 2:
                                exps(n + 1, open_heads.pop(0))
                            open_heads.append(which[0])
                            continue
                        if step in ("turn", "project"):
                            while open_heads:
                                exps(n + 1, open_heads.pop(0))
                        if step == "project":
                            empty_proj(*which)
                    while open_heads:
                        exps(n + 1, open_heads.pop(0))
                out_high(NTILE - 1)

        @block.vector
        def _(dve):
            for started in (pt_emptied, linv_done, olo_done, rot_done, sum_done):
                dve.sem_inc(started, ONE)
            with dve.Fori(0, B) as b:
                def rot_cos(p, unit):
                    if p == "V":
                        kv, c = divmod(unit, T // CH)
                        dve.wait_ge(vhi_done, b * UNITS + unit + 1)
                        dve.tensor_tensor(vbuf[:, kv % 2, 1, c * CH:(c + 1) * CH, :].rearrange("p t d -> p (t d)"),
                                          bank("project", p, unit),
                                          f32(vbuf[:, kv % 2, 0, c * CH:(c + 1) * CH, :].rearrange("p t d -> p (t d)")),
                                          ALU.subtract).then_inc(vlo_done, 1)
                        return
                    r, c = rot_index(p, unit), unit % (T // CH)
                    dve.wait_ge(raw_done, ONE + b * NROT + r + 1)
                    dve.wait_ge(rotlo_done, ONE + b * NROT + max(r - 1, 0))
                    dve.tensor_tensor(rot[:, r % 2, :], raw[:, r % 2, :], cos_sb[:, c * CW:(c + 1) * CW],
                                      ALU.mult).then_inc(cos_done, 1)

                def rot_sum(p, unit):
                    if p == "V":
                        return
                    r = rot_index(p, unit)
                    dve.wait_ge(cos_done, b * NROT + r + 1)
                    dve.wait_ge(sin_done, b * NROT + r + 1)
                    dve.tensor_tensor(rot[:, r % 2, :], rot[:, r % 2, :], swapped[:, r % 2, :],
                                      ALU.add).then_inc(rot_done, 1)

                def row_max(n, h):
                    s, w = n * G + h, (n % T + 1) * P
                    dve.wait_ge(scores_done, b * NS + s + 1)
                    dve.tensor_reduce(negmax[:, s % 4:s % 4 + 1], s_ps[:, s % 2, 0:w], AX_X, ALU.max,
                                      negate=True).then_inc(max_done, 1)

                def turned_low(n, j):
                    a = pt_index(n, j)
                    dve.wait_ge(pthi_done, b * NPV + a - T + 1)
                    dve.tensor_tensor(pt[:, a % 2, 1, :], bank("turn", n, j), f32(pt[:, a % 2, 0, :]),
                                      ALU.subtract).then_inc(pt_emptied, 1)

                def invert_sums(n):
                    dve.wait_ge(probs_done, ONE + b * NS + (n + 1) * G)
                    dve.reciprocal(linv[:, n % 2, :], lsum[:, n % 2, :]).then_inc(linv_done, 1)

                def out_low(n):
                    dve.wait_ge(ohi_done, b * NTILE + n + 1)
                    dve.tensor_tensor(o_r[:, 1, :], o_ps[:, :], f32(o_r[:, 0, :]), ALU.subtract).then_inc(olo_done, 1)

                def sum_out(n, half):
                    dve.wait_ge(out_filled, b * 2 * NTILE + 2 * n + half + 1)
                    dve.wait_ge(rrow_done, b * NTILE + n + 1)
                    for q in range(G // 2):
                        h, y = half * (G // 2) + q, bank("out", n, half)[:, q * D:(q + 1) * D]
                        t, r = ysum[:, n % T, :], rrow[:, n % 2, half * (G // 2) + q:half * (G // 2) + q + 1]
                        if n < T and h == 0:
                            dve.wait_ge(acc_done, ONE + b * T)
                            dve.tensor_scalar(t, y, r, None, ALU.mult).then_inc(sum_done, 1)
                        else:
                            dve.wait_ge(sum_done, ONE + b * NTILE * G + n * G + h)
                            dve.scalar_tensor_tensor(out=t, in0=y, scalar=r, in1=t, op0=ALU.mult, op1=ALU.add).then_inc(sum_done, 1)

                for t in range(T):
                    if t % CH == 0:
                        dve.wait_ge(x_loaded[t // CH], b * 16 + 16)
                    dve.bn_stats(stats[:, t, :], xacc[:, t, :]).then_inc(stats_done, 1)
                dve.wait_ge(stats_done, b * T + T)
                dve.memset(mark[:], 0.0)
                for t in range(T):
                    dve.bn_aggr(mv[:, t, :], stats[:, t, :]).then_inc(mean_done, 1)
                dve.wait_ge(rstd_done, b + 1)

                def shift(t):
                    dve.wait_ge(pt_filled, ONE + b * NPT + t + 1)
                    dve.wait_ge(hlo_done, ONE + b * T + max(t - 1, 0))
                    for k in range(KD):
                        last = dve.tensor_scalar(hf[:, t % 2, k, :], bank("norm", t)[:, k * P:(k + 1) * P],
                                                 modp[:, 1, k, bass.ds(b, 1)], modp[:, 0, k, bass.ds(b, 1)],
                                                 ALU.mult, ALU.add)
                    last.then_inc(pt_emptied, 1)

                for t in range(T):
                    dve.wait_ge(pt_filled, ONE + b * NPT + max(t - 1, 0))
                    dve.tensor_scalar(z[:, t % 2, :], xacc[:, t, :], mv[:, t, 0:1], rstd[:, 1, t:t + 1],
                                      ALU.subtract, ALU.mult).then_inc(z_done, 1)
                    if t:
                        shift(t - 1)
                shift(T - 1)
                for q, p in enumerate(PROJ):
                    rot_cos(p, 0)
                    if q:
                        rot_sum(PROJ[q - 1], 0)
                rot_sum(PROJ[-1], 0)
                for h in range(G):
                    row_max(0, h)
                for n in range(NTILE):
                    for step, *which in tile_order(n):
                        if step == "split out":
                            out_low(*which)
                        elif step == "turn":
                            turned_low(n, *which)
                            if which[0] == 0:
                                invert_sums(n)
                        elif step == "rotate":
                            rot_sum(*which)
                        elif step == "scores":
                            row_max(n + 1, *which)
                        elif step == "project":
                            rot_cos(*which)
                        elif step == "out":
                            sum_out(*which)
                out_low(NTILE - 1)
                for _, *which in LAST_OUT:
                    sum_out(*which)

        @block.gpsimd
        def _(pool):
            for started in (acc_done, hlo_done, rotlo_done):
                pool.sem_inc(started, ONE)
            with pool.Fori(0, B) as b:
                def rot_sin(p, unit):
                    if p == "V":
                        return
                    r, c = rot_index(p, unit), unit % (T // CH)
                    per = NROT // 2 * 32
                    pool.wait_ge(swap_done[r % 2], b * per + 32 * (r // 2 + 1))
                    pool.tensor_tensor(swapped[:, r % 2, :], swapped[:, r % 2, :], sin_sb[:, c * CW:(c + 1) * CW],
                                       ALU.mult).then_inc(sin_done, 1)

                def rot_low(p, unit):
                    if p == "V":
                        return
                    r = rot_index(p, unit)
                    pool.wait_ge(rothi_done, b * NROT + r + 1)
                    pool.tensor_tensor(rot_dest(p, unit, 1), rot[:, r % 2, :], f32(rot_dest(p, unit, 0)),
                                       ALU.subtract).then_inc(rotlo_done, 1)

                def scale_rows(n):
                    kv = n // T
                    pool.wait_ge(linv_done, ONE + b * NTILE + n + 1)
                    pool.wait_ge(sum_done, ONE + b * NTILE * G + max(n - 1, 0) * G)
                    pool.tensor_tensor(rrow[:, n % 2, :], linv[:, n % 2, :], hs_sb[:, kv * G:(kv + 1) * G],
                                       ALU.mult).then_inc(rrow_done, 1)

                def add_out(n):
                    t = n % T
                    pool.wait_ge(sum_done, ONE + b * NTILE * G + (n + 1) * G)
                    pool.sem_inc(gate_go, 1)
                    pool.tensor_tensor(ysum[:, t, :], ysum[:, t, :], ga[:, bass.ds(b, 1), :].rearrange("p o d -> p (o d)"),
                                       ALU.mult).then_inc(gated, 1)
                    pool.wait_ge(gated, b * T + t + 1)
                    pool.tensor_tensor(xacc[:, t, :], xacc[:, t, :], ysum[:, t, :], ALU.add).then_inc(acc_done, 1)

                pool.wait_ge(mean_done, b * T + T)
                pool.tensor_tensor(rstd[:, 0, :], mv[:, :, 1], eps[:], ALU.add).then_inc(var_eps, 1)
                pool.wait_ge(var_eps, b + 1)
                pool.tensor_tensor(rstd[:, 1, :], rstd[:, 0, :], mhalf[:], ALU.pow).then_inc(rstd_done, 1)
                for t in range(T):
                    pool.wait_ge(hhi_done, b * T + t + 1)
                    pool.tensor_tensor(ht[:, 1, :, t * P:(t + 1) * P], hf[:, t % 2], f32(ht[:, 0, :, t * P:(t + 1) * P]),
                                       ALU.subtract).then_inc(hlo_done, 1)
                for q, p in enumerate(PROJ):
                    rot_sin(p, 0)
                    if q:
                        rot_low(PROJ[q - 1], 0)
                rot_low(PROJ[-1], 0)
                for n in range(NTILE):
                    scale_rows(n)
                    for step, *which in tile_order(n):
                        if step == "project":
                            rot_sin(*which)
                        elif step == "rotate":
                            rot_low(*which)
                        elif step == "out" and which[0] >= NTILE - T and which[1] == 1:
                            add_out(which[0])
                add_out(NTILE - 1)


def prepare(nc, ctx, sb, sem, wq, wk, wv, wo, hscale, c, wmod, cos, sin, ident, causal, wsplit,
            probs, wbuf, cos_sb, sin_sb, causal_sb, identb_sb, hs_sb, mhalf, eps, ident_sb, ga, rows_dram, modp,
            xacc, raw, swapped, rot, ysum, s_ps, ring, o_ps, wsplit_stored):
    flat = probs[:].rearrange("p a h n -> p (a h n)")
    wraw = [flat[:, g * WG:(g + 1) * WG] for g in range(2)]
    wm = flat[:, 2 * WG:2 * WG + KD * 6 * D].rearrange("p (k n) -> p k n", k=KD)
    c_sb = sb("c_sb", [P, KD, B])
    c_act = sb("c_act", [P, 3, KD, B])
    c_wide = xacc[:].rearrange("p t d -> p (t d)")[:, 0:KD * B * P].rearrange("p (k b c) -> p k b c", k=KD, b=B)
    signs = [raw[:].rearrange("p s w -> p (s w)")] + [ysum[:].rearrange("p t d -> p (t d)")[:, k * B * D:(k + 1) * B * D] for k in range(2)]
    causal_f = rot[:, 0, 0:P]
    modp_ps = ring[:, 0, 0:6 * KD * B]
    rows_ps = [ring[:, 1], ring[:, 2], o_ps, ring[:, 0]]
    order = [2, 3, 0, 1]
    gb = swapped[:].rearrange("p s w -> p (s w)").rearrange("p (b d) -> p b d", b=B)
    shift_row = rot[:].rearrange("p s w -> p (s w)").rearrange("p (b d) -> p b d", b=B)
    scale_row = xacc[:].rearrange("p t d -> p (t d)")[:, KD * B * P:].rearrange("p (b d) -> p b d", b=B)

    const_loaded = sem("const_loaded")
    mod_loaded = sem("mod_loaded")
    wraw_loaded = [sem("wraw_loaded0"), sem("wraw_loaded1")]
    whi_done = sem("whi_done")
    wlo_done = sem("wlo_done")
    exp_done = sem("exp_done")
    silu_steps = sem("silu_steps")
    wide_done = sem("wide_done")
    modp_filled = sem("modp_filled")
    gate_filled = sem("gate_filled")
    gate_steps = sem("gate_steps")
    mhalf_set = sem("mhalf_set")

    block_cm = nc.Block()
    with block_cm as block:
        @block.sync
        def _(sp):
            for k in range(KD):
                for bb in range(B):
                    sp.dma_start(c_sb[:, k, bb:bb + 1], c[bb:bb + 1, k * P:(k + 1) * P].rearrange("b p -> p b")).then_inc(mod_loaded, 16)
            sp.dma_start(wm, wmod.rearrange("(k p) n -> p k n", p=P)).then_inc(mod_loaded, 16)
            sp.dma_start(cos_sb[:], cos).then_inc(const_loaded, 16)
            sp.dma_start(sin_sb[:], sin).then_inc(const_loaded, 16)
            sp.dma_start(ident_sb[:], ident).then_inc(const_loaded, 16)
            sp.dma_start(causal_f, causal).then_inc(const_loaded, 16)
            sp.dma_start(hs_sb[:], hscale.rearrange("a h b c -> a (h b c)").broadcast_to([P, H])).then_inc(const_loaded, 16)

            def load_group(n):
                kv = order[n]
                g = kv % 2
                if n >= 2:
                    sp.wait_ge(wlo_done, n - 1)
                for k in range(KD):
                    dst = wraw[g][:, k * WQ:(k + 1) * WQ]
                    rows = slice(k * P, (k + 1) * P)
                    sp.dma_start(dst[:, 0:KCOL], wq[rows, kv * KCOL:(kv + 1) * KCOL]).then_inc(wraw_loaded[g], 16)
                    sp.dma_start(dst[:, KCOL:VCOL], wk[rows, kv * DH:(kv + 1) * DH]).then_inc(wraw_loaded[g], 16)
                    sp.dma_start(dst[:, VCOL:WQ], wv[rows, kv * DH:(kv + 1) * DH]).then_inc(wraw_loaded[g], 16)
                sp.dma_start(wraw[g][:, KD * WQ:].rearrange("p (h n) -> p h n", h=G),
                             wo[kv * G * DH:(kv + 1) * G * DH, :].rearrange("(h p) n -> p h n", p=P)).then_inc(wraw_loaded[g], 16)

            def store_group(n):
                sp.wait_ge(wlo_done, n + 1)
                sp.dma_start(wsplit[order[n]], wbuf[:, order[n] % 2].rearrange("p s w -> p (s w)").bitcast(F32)).then_inc(wsplit_stored[order[n] % 2], 16)

            load_group(0)
            load_group(1)
            store_group(0)
            load_group(2)
            store_group(1)
            load_group(3)
            sp.wait_ge(gate_steps, 10 + 2 * B)
            for k, row in enumerate((gb, shift_row, scale_row)):
                sp.dma_start(rows_dram[k:k + 1], row[0:1]).then_inc(const_loaded, 16)
            sp.wait_ge(const_loaded, 16 * 8)

        @block.scalar
        def _(act):
            act.wait_ge(mod_loaded, 16 * (KD * B + 1))
            act.activation(c_act[:, 0], c_sb[:], ACT.Exp, scale=-1.0).then_inc(exp_done, 1)
            for n, kv in enumerate(order):
                act.wait_ge(wraw_loaded[kv % 2], 16 * (3 * KD + 1) * (n // 2 + 1))
                if n >= 2:
                    act.wait_ge(wsplit_stored[kv % 2], 16)
                act.copy(wbuf[:, kv % 2, 0, :], wraw[kv % 2]).then_inc(whi_done, 1)

        @block.vector
        def _(dve):
            dve.memset(mhalf[:], -0.5)
            dve.memset(eps[:], EPS).then_inc(mhalf_set, 1)
            dve.wait_ge(exp_done, 1)
            dve.tensor_scalar(c_act[:, 1], c_act[:, 0], 1.0, None, ALU.add).then_inc(silu_steps, 1)
            dve.wait_ge(silu_steps, 1)
            dve.reciprocal(c_act[:, 2], c_act[:, 1]).then_inc(silu_steps, 1)
            dve.wait_ge(silu_steps, 2)
            dve.tensor_tensor(c_act[:, 0], c_act[:, 2], c_sb[:], ALU.mult).then_inc(silu_steps, 1)
            dve.wait_ge(silu_steps, 3)
            for k in range(KD):
                last = dve.tensor_copy(c_wide[:, k], c_act[:, 0, k, :].rearrange("p (b o) -> p b o", o=1).broadcast_to([P, B, P]))
            last.then_inc(wide_done, 1)
            dve.wait_ge(modp_filled, 1)
            last = dve.tensor_copy(modp[:].rearrange("p s k b -> p (s k b)"), modp_ps)
            last.then_inc(gate_steps, 1)
            dve.wait_ge(gate_steps, 1)
            for sec in (1, 4):
                last = dve.tensor_scalar(modp[:, sec], modp[:, sec], 1.0, None, ALU.add)
            last.then_inc(gate_steps, 1)

            def split_low(n):
                kv = order[n]
                dve.wait_ge(whi_done, n + 1)
                dve.tensor_tensor(wbuf[:, kv % 2, 1, :], wraw[kv % 2], wbuf[:, kv % 2, 0, :].bitcast(F32),
                                  ALU.subtract).then_inc(wlo_done, 1)

            split_low(0)
            split_low(1)
            steps = 2
            for half, dest in enumerate((ga, gb)):
                src = s_ps[:, half, :]
                dve.wait_ge(gate_filled, half + 1)
                dve.tensor_scalar(signs[0], src, 0.0, 2.0, ALU.is_ge, ALU.mult).then_inc(gate_steps, 1)
                dve.wait_ge(gate_steps, steps + 1)
                dve.tensor_scalar(signs[2], signs[0], -1.0, None, ALU.add).then_inc(gate_steps, 1)
                dve.wait_ge(gate_steps, steps + 2)
                dve.tensor_tensor(signs[1], src, signs[2], ALU.mult).then_inc(gate_steps, 1)
                dve.wait_ge(gate_steps, steps + 3)
                dve.scalar_tensor_tensor(out=dest[:].rearrange("p b d -> p (b d)") if half == 0 else swapped[:].rearrange("p s w -> p (s w)"),
                                         in0=signs[1], scalar=0.25, in1=signs[2],
                                         op0=ALU.max, op1=ALU.mult).then_inc(gate_steps, 1)
                dve.wait_ge(gate_steps, steps + 4)
                steps += 4
            split_low(2)
            dve.wait_ge(mhalf_set, 2)
            for bb in range(B):
                dve.wait_ge(gate_filled, 3 + bb)
                dve.tensor_copy(shift_row[:, bb, :], rows_ps[bb][:, 0:D]).then_inc(gate_steps, 1)
                dve.tensor_scalar(scale_row[:, bb, :], rows_ps[bb][:, D:2 * D], 1.0, None, ALU.add).then_inc(gate_steps, 1)
            split_low(3)

        @block.gpsimd
        def _(pool):
            pool.wait_ge(const_loaded, 16 * 5)
            pool.tensor_copy(causal_sb[:], causal_f)
            pool.tensor_copy(identb_sb[:], ident_sb[:]).then_inc(mhalf_set, 1)
            pool.wait_ge(mhalf_set, 2)

        @block.tensor
        def _(pe):
            pe.wait_ge(silu_steps, 3)
            pe.wait_ge(mod_loaded, 16 * (KD * B + 1))
            for sec in range(6):
                for half in range(KD):
                    col = (sec * KD + half) * B
                    for k in range(KD):
                        last = pe.matmul(modp_ps[:, col:col + B], wm[:, k, sec * D + half * P:sec * D + (half + 1) * P],
                                         c_act[:, 0, k, :], start=(k == 0), stop=(k == KD - 1))
            last.then_inc(modp_filled, 1)
            pe.wait_ge(wide_done, 1)
            for half, sec in enumerate((2, 5)):
                for bb in range(B):
                    for k in range(KD):
                        last = pe.matmul(s_ps[:, half, bb * D:(bb + 1) * D], c_wide[:, k, bb, :],
                                         wm[:, k, sec * D:(sec + 1) * D], start=(k == 0), stop=(k == KD - 1))
                last.then_inc(gate_filled, 1)
            pe.wait_ge(gate_steps, 1)
            for bb in range(B):
                for k in range(KD):
                    last = pe.matmul(rows_ps[bb][:, :], c_wide[:, k, bb, :], wm[:, k, 3 * D:5 * D], start=(k == 0), stop=(k == KD - 1))
                last.then_inc(gate_filled, 1)


E, TOPK, FI = 32, 4, 96
NTOK = B * N
NSLOT_TILES = NTOK * TOPK // P + E
PACK, EBITS = 4, 5
ID_TILES = NTOK * E // P
FU = 8
LU = 2 * FU
STORE_LAG = 4


def route(nc, x1, rows_dram, rw, gw, uw, dw, idtab, h2, ydram, out, tri, iota_e, ebase, iota_m, tokens, ident_sb):
    with ExitStack() as ctx:
        def sb(name, shape, dt=F32):
            return ctx.enter_context(nc.sbuf_tensor(name, shape, dt))

        def sem(name):
            return ctx.enter_context(nc.semaphore(name))

        def bank(name, dt=F32):
            return ctx.enter_context(nc.psum_tensor(name, [P, 512], dt))

        banks = [bank(f"bank{i}") for i in range(8)]
        wgu = sb("wgu", [P, KD, E, 2 * FI])
        wd = sb("wd", [P, E, D])
        x_all = sb("x_all", [P, B * T, D])
        w4_all = sb("w4_all", [P, B * T + FU, TOPK])
        hot_all = sb("hot_all", [P, B * T, TOPK, E], BF16)
        rank_all = sb("rank_all", [P, B * T, E])
        totals = sb("totals", [P, E])
        etab = sb("etab", [P, NSLOT_TILES // PACK], mybir.dt.int32)
        offtab = sb("offtab", [P, NSLOT_TILES // 2], mybir.dt.int32)
        pos_all = sb("pos_all", [P, B * T + FU, TOPK], U32)

        route_tokens(nc, banks, gw, uw, dw, wgu, wd, x1, x_all, rows_dram, rw, idtab, h2, tri, iota_e, ebase, tokens, ident_sb,
                     w4_all, hot_all, rank_all, totals, iota_m, etab, offtab, pos_all)
        experts(nc, banks, idtab, h2, ydram, wgu, wd, etab, offtab, ident_sb)
        combine(nc, x_all, rows_dram, ydram, out, w4_all, pos_all)


def route_tokens(nc, banks, gw, uw, dw, wgu, wd, x1, x_all, rows_dram, rw, idtab, h2, tri, iota_e, ebase, tokens, ident_sb,
                 w4_all, hot_all, rank_all, totals, iota_m, etab, offtab, pos_all):
    EG = 2
    WFILLS = EG + EG // 2
    with ExitStack() as ctx:
        sb = lambda name, shape, dt=F32: ctx.enter_context(nc.sbuf_tensor(name, shape, dt))
        sem = lambda name: ctx.enter_context(nc.semaphore(name))
        work = sb("work", [P, 3, T * D])
        xb, hb = (work[:, k].rearrange("p (t d) -> p t d", d=D) for k in range(2))
        hbt = work[:, 2].rearrange("p (t k c) -> p t k c", k=KD, c=P)
        mod = sb("mod", [P, 2, D])
        rwr = sb("rwr", [P, D])
        rwt = sb("rwt", [P, KD, E])
        st = sb("st", [P, B * T, 6])
        mv = sb("mv2", [P, B * T, 2])
        rstd = sb("rstd2", [P, 2, B * T])
        mhalf = sb("mhalf2", [P, B * T])
        eps = sb("eps2", [P, B * T])
        mark = sb("mark2", [P, 4])
        logits = sb("logits", [P, T, E])
        top = sb("top", [P, T, 8])
        top_at = sb("top_at", [P, T, 8], U32)
        at_f = sb("at_f", [P, T, TOPK])
        diff = sb("diff", [P, T, TOPK])
        e4 = sb("e4", [P, T, TOPK])
        esum = sb("esum", [P, 2, T])
        hot = sb("hot", [P, T, TOPK, E])
        mask = sb("mask", [P, T, E], BF16)
        runsum = sb("runsum", [P, E], BF16)
        batch_sum = sb("batch_sum", [P, E])
        rank = sb("rank", [P, T, E])
        slot = sb("slot", [P, T, E])
        slots = sb("slots", [P, T, TOPK, E])
        slot_f = sb("slot_f", [P, T, TOPK])
        slot_u = sb("slot_u", [P, T, TOPK], U32)
        tok = sb("tok", [P, B * T], U32)
        tokb = sb("tokb", [P, T], U32)
        tri_sb = sb("tri_sb", [P, P], BF16)
        tri_f = work[:, 2, 0:P]
        ones = sb("ones", [P, P], BF16)
        iota_sb = sb("iota_sb", [P, E])
        ebase_sb = sb("ebase_sb", [P, E])
        M = NSLOT_TILES
        padded = sb("padded", [P, E])
        padded_i = sb("padded_i", [P, 2, E], mybir.dt.int32)
        ntiles = sb("ntiles", [P, E])
        ones_e = sb("ones_e", [P, E])
        upto = sb("upto", [P, E])
        base = sb("base", [P, 2, E])
        place = sb("place", [P, B * T, E])
        places = sb("places", [P, B * T, TOPK, E])
        zero = places[:].rearrange("p t j e -> p (t j e)")[:, 0:NTOK * E // P]
        pos_f = sb("pos_f", [P, B * T, TOPK])
        passed = work[:].rearrange("p k n -> p (k n)")[:, 0:M * E].rearrange("p (m e) -> p m e", e=E)
        tile_e = sb("tile_e", [P, 3, M])
        packed = sb("packed", [P, PACK - 1, M // PACK])
        off_f = sb("off_f", [P, 4, M])
        iota_m_sb = sb("iota_m_sb", [P, M])
        step_done = sem("placing_step_done")
        x_loaded = [sem(f"x_loaded2_{b}") for b in range(B)]
        graw = sb("graw", [P, 2, 2, EG, D])
        draw = sb("draw", [P, 2, EG, KD, FI])
        raw_loaded = [sem("raw_loaded0"), sem("raw_loaded1")]
        turned = sem("turned")
        weight_copied = sem("weight_copied")

        names = """const2 zeroed tab_set mod_loaded2 h2_stored rw_turned rwt_done stats2 mean2 var2 rstd2_done norm2 scaled2
                   h2_done turned2 turn2_copied logits_filled logits_copied top_done at_done diff_done atf_done hot_done
                   mask_done hotall_done bsum_done e4_done esum_done einv_done w4_done rank_filled rank_copied rankall_done
                   slot_done slots_done slotf_done slotu_done slots_free tokb_done scatter_go scattered runsum_done totals_filled""".split()
        s = {name: sem("q_" + name) for name in names}
        block = ctx.enter_context(nc.Block())

        @block.sync
        def _(sp):
            for b in range(B):
                sp.dma_start(x_all[:, b * T:(b + 1) * T], x1[b:b + 1].rearrange("o (t p) d -> p (o t) d", p=P)).then_inc(x_loaded[b], 16)
            sp.dma_start(rwr[0:E, :], rw).then_inc(s["const2"], 16)
            sp.dma_start(tri_f, tri).then_inc(s["const2"], 16)
            sp.dma_start(iota_sb[:], iota_e).then_inc(s["const2"], 16)
            sp.dma_start(ebase_sb[:], ebase).then_inc(s["const2"], 16)
            sp.dma_start(tok[:], tokens).then_inc(s["const2"], 16)
            sp.dma_start(iota_m_sb[:], iota_m).then_inc(s["const2"], 16)
            sp.wait_ge(s["zeroed"], 1)
            sp.dma_start(idtab.rearrange("(p n) o -> p (n o)", p=P), zero.bitcast(U32)).then_inc(s["tab_set"], 16)
            sp.sem_inc(s["h2_stored"], ONE)

            def load_weights(g):
                for k, w in enumerate((gw, uw)):
                    sp.dma_start(graw[0:FI, g % 2, k], w[g * EG:(g + 1) * EG].rearrange("e i d -> i e d")).then_inc(raw_loaded[g % 2], 16)
                for e in range(EG):
                    sp.dma_start(draw[:, g % 2, e], dw[g * EG + e].rearrange("(k p) i -> p k i", p=P)).then_inc(raw_loaded[g % 2], 16)

            for g in range(2):
                load_weights(g)
            with sp.Fori(0, B) as b:
                sp.wait_ge(s["h2_stored"], ONE + b * 16)
                for k in range(2):
                    sp.dma_start(mod[:, k, :], rows_dram[k + 1:k + 2, bass.ds(b, 1), :].rearrange("a b d -> a (b d)").broadcast_to([P, D])).then_inc(s["mod_loaded2"], 16)
                sp.wait_ge(s["h2_done"], b + 1)
                sp.dma_start(h2[bass.ds(b, 1), :, :].rearrange("o (t p) d -> p (o t) d", p=P), hb).then_inc(s["h2_stored"], 16)
            for g in range(2, E // EG):
                sp.wait_ge(turned, WFILLS * (g - 1))
                load_weights(g)
            sp.wait_ge(s["h2_stored"], ONE + 16 * B)
            sp.wait_ge(s["tab_set"], 16)

        @block.vector
        def _(dve):
            dve.memset(mhalf[:], -0.5)
            dve.memset(eps[:], EPS)
            dve.memset(ones[:], 1.0)
            dve.memset(zero, 0.0)
            dve.memset(runsum[:], 0.0).then_inc(s["zeroed"], 1)
            dve.wait_ge(s["rw_turned"], 1)
            dve.tensor_copy(rwt[:].rearrange("p k e -> p (k e)"), banks[7][:, 0:KD * E]).then_inc(s["rwt_done"], 1)
            dve.wait_ge(s["const2"], 16 * 6)
            dve.tensor_copy(tri_sb[:], tri_f).then_inc(s["runsum_done"], ONE)
            for t in range(B * T):
                if t % T == 0:
                    dve.wait_ge(x_loaded[t // T], 16)
                dve.bn_stats(st[:, t, :], x_all[:, t, :]).then_inc(s["stats2"], 1)
                if t % T == T - 1:
                    for q in range(t + 1 - T, t + 1):
                        dve.wait_ge(s["stats2"], q + 1)
                        last = dve.bn_aggr(mv[:, q, :], st[:, q, :])
                    last.then_inc(s["mean2"], 1)
            dve.wait_ge(s["rstd2_done"], B)
            with dve.Fori(0, B) as b:
                tiles = bass.ds(b * T, T)
                dve.wait_ge(s["mod_loaded2"], b * 32 + 32)
                for t in range(T):
                    at = bass.ds(b * T + t, 1)
                    last = dve.tensor_scalar(xb[:, t, :], x_all[:, at, :].rearrange("p o d -> p (o d)"), mv[:, at, 0:1].rearrange("p o c -> p (o c)"),
                                             rstd[:, 1, at], ALU.subtract, ALU.mult)
                last.then_inc(s["norm2"], 1)
                dve.wait_ge(s["norm2"], b + 1)
                dve.wait_ge(s["h2_stored"], ONE + b * 16)
                dve.tensor_tensor(hb, xb, mod[:, 1:2, :].broadcast_to([P, T, D]), ALU.mult).then_inc(s["scaled2"], 1)
                dve.wait_ge(s["scaled2"], b + 1)
                dve.tensor_tensor(hb, hb, mod[:, 0:1, :].broadcast_to([P, T, D]), ALU.add).then_inc(s["h2_done"], 1)
                dve.wait_ge(s["logits_filled"], b + 1)
                dve.tensor_copy(logits[:].rearrange("p t e -> p (t e)"), banks[4][:, 0:T * E]).then_inc(s["logits_copied"], 1)
                dve.wait_ge(s["logits_copied"], b + 1)
                dve.memset(mark[:, 2:3], 0.0)
                for t in range(T):
                    last = dve.max(top[:, t, :], logits[:, t, :])
                last.then_inc(s["top_done"], 1)
                dve.wait_ge(s["top_done"], b + 1)
                dve.tensor_tensor(diff[:], top[:, :, 0:TOPK], top[:, :, 0:1].broadcast_to([P, T, TOPK]), ALU.subtract).then_inc(s["diff_done"], 1)
                for t in range(T):
                    last = dve.max_index(top_at[:, t, :], top[:, t, :], logits[:, t, :])
                last.then_inc(s["at_done"], 1)
                dve.wait_ge(s["at_done"], b + 1)
                dve.tensor_copy(at_f[:], top_at[:, :, 0:TOPK]).then_inc(s["atf_done"], 1)
                dve.wait_ge(s["atf_done"], b + 1)
                for j in range(TOPK):
                    last = dve.tensor_tensor(hot[:, :, j, :], at_f[:, :, j:j + 1].broadcast_to([P, T, E]),
                                             iota_sb[:].rearrange("p (o e) -> p o e", o=1).broadcast_to([P, T, E]), ALU.is_equal)
                last.then_inc(s["hot_done"], 1)
                dve.wait_ge(s["hot_done"], b + 1)
                dve.tensor_reduce(mask[:], hot[:].rearrange("p t j e -> p t e j"), AX_X, ALU.max).then_inc(s["mask_done"], 1)
                dve.tensor_copy(hot_all[:, tiles].rearrange("p t j e -> p (t j e)"), hot[:].rearrange("p t j e -> p (t j e)")).then_inc(s["hotall_done"], 1)
                dve.wait_ge(s["mask_done"], b + 1)
                dve.tensor_reduce(batch_sum[:], mask[:].rearrange("p t e -> p e t"), AX_X, ALU.add).then_inc(s["bsum_done"], 1)
                dve.wait_ge(s["e4_done"], b + 1)
                dve.tensor_reduce(esum[:, 0, :], e4[:], AX_X, ALU.add).then_inc(s["esum_done"], 1)
                dve.wait_ge(s["esum_done"], b + 1)
                dve.reciprocal(esum[:, 1, :], esum[:, 0, :]).then_inc(s["einv_done"], 1)
                dve.wait_ge(s["einv_done"], b + 1)
                dve.tensor_tensor(w4_all[:, tiles], e4[:], esum[:, 1, :].rearrange("p (t o) -> p t o", o=1).broadcast_to([P, T, TOPK]),
                                  ALU.mult).then_inc(s["w4_done"], 1)
                dve.wait_ge(s["rank_filled"], b + 1)
                dve.tensor_copy(rank[:].rearrange("p t e -> p (t e)"), banks[5][:, 0:T * E]).then_inc(s["rank_copied"], 1)
                dve.wait_ge(s["rank_copied"], b + 1)
                dve.tensor_copy(rank_all[:, tiles].rearrange("p t e -> p (t e)"), rank[:].rearrange("p t e -> p (t e)")).then_inc(s["rankall_done"], 1)
                dve.tensor_tensor(slot[:], rank[:], ebase_sb[:].rearrange("p (o e) -> p o e", o=1).broadcast_to([P, T, E]),
                                  ALU.add).then_inc(s["slot_done"], 1)
                dve.wait_ge(s["slot_done"], b + 1)
                for j in range(TOPK):
                    last = dve.tensor_tensor(slots[:, :, j, :], hot[:, :, j, :], slot[:], ALU.mult)
                last.then_inc(s["slots_done"], 1)
                dve.wait_ge(s["slots_done"], b + 1)
                dve.tensor_reduce(slot_f[:], slots[:], AX_X, ALU.add).then_inc(s["slotf_done"], 1)
                dve.wait_ge(s["slotf_done"], b + 1)
                dve.wait_ge(s["slots_free"], ONE + b)
                dve.tensor_copy(slot_u[:], slot_f[:]).then_inc(s["slotu_done"], 1)
                dve.wait_ge(s["bsum_done"], b + 1)
                dve.tensor_tensor(runsum[:], runsum[:], batch_sum[:], ALU.add).then_inc(s["runsum_done"], 1)
            dve.wait_ge(s["totals_filled"], 1)
            dve.tensor_copy(totals[:], banks[7][:, 0:E]).then_inc(s["totals_filled"], 1)
            dve.wait_ge(s["totals_filled"], 2)
            dve.wait_ge(s["h2_stored"], ONE + 16 * B)
            dve.wait_ge(s["logits_filled"], B)
            dve.wait_ge(s["tab_set"], 16)
            dve.wait_ge(s["hotall_done"], B)
            dve.wait_ge(s["rankall_done"], B)

            count = [0]

            def step(ins):
                count[0] += 1
                ins.then_inc(step_done, 1)
                dve.wait_ge(step_done, count[0])

            wide = lambda ap, n: ap.rearrange("p (o e) -> p o e", o=1).broadcast_to([P, n, E])
            step(dve.memset(ones_e[:], 1.0))
            step(dve.tensor_scalar(padded[:], totals[:], float(P - 1), None, ALU.add))
            step(dve.tensor_copy(padded_i[:, 0], padded[:]))
            step(dve.tensor_scalar(padded_i[:, 1], padded_i[:, 0], 7, None, ALU.arith_shift_right))
            step(dve.tensor_copy(ntiles[:], padded_i[:, 1]))
            step(dve.tensor_tensor_scan(upto[:], ones_e[:], ntiles[:], 0.0, ALU.mult, ALU.add))
            step(dve.tensor_tensor(base[:, 0], upto[:], ntiles[:], ALU.subtract))
            step(dve.tensor_scalar(base[:, 1], base[:, 0], float(P), None, ALU.mult))
            step(dve.tensor_tensor(place[:], rank_all[:], wide(base[:, 1], B * T), ALU.add))
            for j in range(TOPK):
                last = dve.tensor_tensor(places[:, :, j, :], hot_all[:, :, j, :], place[:], ALU.mult)
            step(last)
            step(dve.tensor_reduce(pos_f[:], places[:], AX_X, ALU.add))
            step(dve.tensor_copy(pos_all[:, 0:B * T], pos_f[:]))
            step(dve.memset(pos_all[:, B * T:], 0))
            step(dve.memset(w4_all[:, B * T:], 0.0))
            step(dve.tensor_tensor(passed, wide(upto[:], M), iota_m_sb[:].rearrange("p (m o) -> p m o", o=1).broadcast_to([P, M, E]), ALU.is_le))
            step(dve.tensor_reduce(tile_e[:, 0], passed, AX_X, ALU.add))
            step(dve.tensor_tensor(passed, passed, wide(ntiles[:], M), ALU.mult))
            step(dve.tensor_reduce(off_f[:, 0], passed, AX_X, ALU.add))
            step(dve.tensor_scalar(tile_e[:, 1], tile_e[:, 0], float(E - 1), None, ALU.min))
            e_of = lambda k: tile_e[:, 1].rearrange("p (w k) -> p w k", k=PACK)[:, :, k]
            for k in range(PACK - 1):
                high = e_of(PACK - 1) if k == 0 else packed[:, k - 1]
                step(dve.scalar_tensor_tensor(out=packed[:, k], in0=high, scalar=float(1 << EBITS), in1=e_of(PACK - 2 - k), op0=ALU.mult, op1=ALU.add))
            step(dve.tensor_copy(etab[:], packed[:, PACK - 2]))
            step(dve.tensor_tensor(off_f[:, 1], iota_m_sb[:], off_f[:, 0], ALU.subtract))
            step(dve.scalar_tensor_tensor(out=off_f[:, 3], in0=tile_e[:, 1], scalar=float(NTOK // P), in1=off_f[:, 1], op0=ALU.mult, op1=ALU.add))
            step(dve.tensor_scalar(tile_e[:, 2], off_f[:, 3], float(ID_TILES - 1), None, ALU.min))
            pairs = tile_e[:, 2].rearrange("p (w k) -> p w k", k=2)
            step(dve.scalar_tensor_tensor(out=off_f[:, 2, 0:M // 2], in0=pairs[:, :, 1], scalar=float(ID_TILES), in1=pairs[:, :, 0], op0=ALU.mult, op1=ALU.add))
            step(dve.tensor_copy(offtab[:], off_f[:, 2, 0:M // 2]))

        @block.scalar
        def _(act):
            with act.Fori(0, B) as b:
                for q in range(T // 2):
                    act.wait_ge(s["turned2"], b * (T // 2) + q + 1)
                    act.copy(hbt[:, 2 * q:2 * q + 2].rearrange("p t k c -> p (t k c)"), banks[q][:]).then_inc(s["turn2_copied"], 1)
                act.wait_ge(s["diff_done"], b + 1)
                act.activation(e4[:], diff[:], ACT.Exp).then_inc(s["e4_done"], 1)
            for g in range(E // EG):
                for i in range(WFILLS):
                    filled = banks[g % 2 * WFILLS + i]
                    act.wait_ge(turned, WFILLS * g + i + 1)
                    if i < EG:
                        act.copy(wgu[:, :, g * EG + i, :], filled[:, 0:4 * FI].rearrange("p (k c) -> p k c", k=KD)).then_inc(weight_copied, 1)
                    else:
                        e = g * EG + 2 * (i - EG)
                        act.copy(wd[0:FI, e:e + 2, :].rearrange("p e d -> p (e d)"), filled[0:FI, :]).then_inc(weight_copied, 1)

        @block.tensor
        def _(pe):
            pe.wait_ge(s["const2"], 16 * 6)
            for k in range(KD):
                last = pe.transpose(banks[7][:, k * E:(k + 1) * E], rwr[0:E, k * P:(k + 1) * P], ident_sb[0:E, 0:E])
            last.then_inc(s["rw_turned"], 1)
            pe.wait_ge(s["rwt_done"], 1)
            pe.wait_ge(s["zeroed"], 1)
            with pe.Fori(0, B) as b:
                pe.wait_ge(s["h2_done"], b + 1)
                for q in range(T // 2):
                    for t in (2 * q, 2 * q + 1):
                        for k in range(KD):
                            c = ((t % 2) * KD + k) * P
                            last = pe.transpose(banks[q][:, c:c + P], hb[:, t, k * P:(k + 1) * P], ident_sb[:])
                    last.then_inc(s["turned2"], 1)
                pe.wait_ge(s["turn2_copied"], (b + 1) * (T // 2))
                for t in range(T):
                    for k in range(KD):
                        last = pe.matmul(banks[4][:, t * E:(t + 1) * E], hbt[:, t, k, :], rwt[:, k, :], start=(k == 0), stop=(k == KD - 1))
                last.then_inc(s["logits_filled"], 1)
                pe.wait_ge(s["runsum_done"], b + ONE)
                pe.wait_ge(s["mask_done"], b + 1)
                for t in range(T):
                    out = banks[5][:, t * E:(t + 1) * E]
                    pe.matmul(out, ones[:], runsum[:], start=True, stop=False)
                    for before in range(t):
                        pe.matmul(out, ones[:], mask[:, before, :], start=False, stop=False)
                    last = pe.matmul(out, tri_sb[:], mask[:, t, :], start=False, stop=True)
                last.then_inc(s["rank_filled"], 1)
            pe.wait_ge(s["runsum_done"], B + ONE)
            pe.matmul(banks[7][:, 0:E], ones[:], runsum[:], start=True, stop=True).then_inc(s["totals_filled"], 1)

            pe.wait_ge(s["logits_copied"], B)
            pe.wait_ge(s["rank_copied"], B)
            pe.wait_ge(s["turn2_copied"], B * (T // 2))
            for g in range(E // EG):
                pe.wait_ge(raw_loaded[g % 2], 16 * (2 + EG) * (g // 2 + 1))
                for i in range(WFILLS):
                    into = banks[g % 2 * WFILLS + i]
                    if g >= 2:
                        pe.wait_ge(weight_copied, WFILLS * (g - 2) + i + 1)
                    for k in range(KD):
                        for w in range(2):
                            if i < EG:
                                last = pe.transpose(into[:, (2 * k + w) * FI:(2 * k + w + 1) * FI],
                                                    graw[0:FI, g % 2, w, i, k * P:(k + 1) * P], ident_sb[0:FI, 0:FI])
                            else:
                                last = pe.transpose(into[0:FI, (2 * w + k) * P:(2 * w + k + 1) * P],
                                                    draw[:, g % 2, 2 * (i - EG) + w, k, :], ident_sb[:])
                    last.then_inc(turned, 1)

        @block.gpsimd
        def _(pool):
            pool.wait_ge(s["tab_set"], 16)
            pool.wait_ge(s["zeroed"], 1)
            pool.wait_ge(s["const2"], 16 * 6)
            for b in range(B):
                some = slice(b * T, (b + 1) * T)
                pool.wait_ge(s["mean2"], b + 1)
                pool.tensor_tensor(rstd[:, 0, some], mv[:, some, 1], eps[:, some], ALU.add).then_inc(s["var2"], 1)
                pool.wait_ge(s["var2"], b + 1)
                pool.tensor_tensor(rstd[:, 1, some], rstd[:, 0, some], mhalf[:, some], ALU.pow).then_inc(s["rstd2_done"], 1)
            pool.sem_inc(s["slots_free"], ONE)
            with pool.Fori(0, B) as b:
                pool.tensor_copy(tokb[:], tok[:, bass.ds(b * T, T)]).then_inc(s["tokb_done"], 1)
                pool.wait_ge(s["tokb_done"], b + 1)
                pool.wait_ge(s["slotu_done"], b + 1)
                pool.sem_inc(s["scatter_go"], 1)
                for t in range(T):
                    for j in range(TOPK):
                        pool.indirect_dma_start(idtab, bass.IndirectOffsetOnAxis(ap=slot_u[:, t, j:j + 1], axis=0),
                                                tokb[:, t:t + 1], None).then_inc(s["scattered"], 16)
                pool.wait_ge(s["scattered"], (b + 1) * 16 * T * TOPK)
                pool.sem_inc(s["slots_free"], 1)


def experts(nc, banks, idtab, h2, ydram, wgu, wd, etab, offtab, ident_sb):
    with ExitStack() as ctx:
        sb = lambda name, shape, dt=F32: ctx.enter_context(nc.sbuf_tensor(name, shape, dt))
        sem = lambda name: ctx.enter_context(nc.semaphore(name))
        ids = [sb(f"ids{u}", [P, 1], U32) for u in range(FU)]
        xg = [sb(f"xg{u}", [P, D]) for u in range(FU)]
        xt = sb("xt", [P, FU, KD, P])
        sig = sb("sig", [P, FU, FI])
        act_out = sb("act_out", [P, FU, FI])
        at = sb("at", [P, FU, P])
        y = sb("y", [P, FU, D])
        id_loaded = [sem(f"id_loaded{u}") for u in range(FU)]
        gathered = [sem(f"gathered{u}") for u in range(FU)]
        y_stored = [sem(f"y_stored{u}") for u in range(FU // 2)]
        gather_go = sem("gather_go")
        sp_go = sem("sp_go")
        store_go = sem("store_go")
        x_turned = sem("x_turned")
        x_copied = sem("x_copied")
        gu_done = sem("gu_done")
        silu_done = sem("silu_done")
        prod_done = sem("prod_done")
        p_turned = sem("p_turned")
        p_copied = sem("p_copied")
        y_done = sem("yt_done")
        y_copied = sem("y_copied")
        M = NSLOT_TILES
        block = ctx.enter_context(nc.Block())
        h2_rows = h2.rearrange("b n d -> (b n) d")
        x_ps = banks[0:2]
        gu_ps = banks[2:4]
        p_ps = banks[4:6]
        y_ps = banks[6:8]

        def stepped(eng, step, lag=0):
            for m in range(LU):
                step(m, m % FU, True)
            with eng.Fori(1, M // LU) as g:
                for k in range(LU):
                    step(g * LU + k, k % FU, False)
            for m in range(M, M + lag):
                step(m, m % FU, True)

        @block.sync
        def _(sp):
            pair = [None]

            def step(m, u, edge):
                if not edge or m < M:
                    if u % 2 == 0:
                        at = m // 2 if edge else (m - u) // 2 + u // 2
                        pair[0] = sp.value_load(offtab[0:1, bass.ds(at, 1)], min_val=0, max_val=ID_TILES * ID_TILES - 1)
                        off = pair[0] & (ID_TILES - 1)
                    else:
                        off = (pair[0] >> ID_TILES.bit_length() - 1) & (ID_TILES - 1)
                    if not edge or m >= FU:
                        sp.wait_ge(gathered[u], (m - FU - u) * (16 // FU) + 16)
                        sp.sem_inc(sp_go, 1)
                    sp.dma_start(ids[u][:], idtab[bass.ds(off * P, P), :]).then_inc(id_loaded[u], 16)
            stepped(sp, step)
            for u in range(FU // 2):
                sp.wait_ge(y_stored[u], 16 * (M // FU))

        @block.gpsimd
        def _(pool):
            def step(m, u, edge):
                pool.wait_ge(id_loaded[u], (m - u) * (16 // FU) + 16)
                if not edge or m >= FU:
                    pool.wait_ge(x_turned, m - FU + 1)
                pool.sem_inc(gather_go, 1)
                pool.indirect_dma_start(xg[u][:], None, h2_rows, bass.IndirectOffsetOnAxis(ap=ids[u][:], axis=0)).then_inc(gathered[u], 16)
            stepped(pool, step)

        @block.tensor
        def _(pe):
            words = {}

            def expert(m, u, back, edge):
                word, k = divmod((m if edge else u) - back, PACK)
                if (edge, word) not in words:
                    at = word if edge else (m - u) // PACK + word
                    words[edge, word] = pe.value_load(etab[0:1, bass.ds(at, 1)], min_val=0, max_val=(1 << EBITS * PACK) - 1)
                return (words[edge, word] >> EBITS * k) & (E - 1)

            def step(m, u, edge):
                if (m if edge else u) == 0:
                    words.clear()
                if not edge or m < M:
                    pe.wait_ge(gathered[u], (m - u) * (16 // FU) + 16)
                    if not edge or m >= 2:
                        pe.wait_ge(x_copied, m - 1)
                    for k in range(KD):
                        last = pe.transpose(x_ps[u % 2][:, k * P:(k + 1) * P], xg[u][:, k * P:(k + 1) * P], ident_sb[:])
                    last.then_inc(x_turned, 1)
                if not edge or 1 <= m < M + 1:
                    q, v = m - 1, (u - 1) % FU
                    e = expert(m, u, 1, edge)
                    pe.wait_ge(x_copied, q + 1)
                    if not edge or q >= 2:
                        pe.wait_ge(prod_done, q - 1)
                    for k in range(KD):
                        last = pe.matmul(gu_ps[v % 2][:, 0:2 * FI], xt[:, v, k, :], wgu[:, k, bass.ds(e, 1), :].rearrange("p o c -> p (o c)"),
                                         start=(k == 0), stop=(k == KD - 1))
                    last.then_inc(gu_done, 1)
                if not edge or 2 <= m < M + 2:
                    q, v = m - 2, (u - 2) % FU
                    pe.wait_ge(prod_done, q + 1)
                    if not edge or q >= 2:
                        pe.wait_ge(p_copied, q - 1)
                    pe.transpose(p_ps[v % 2][0:FI, 0:P], act_out[:, v, :], ident_sb[:]).then_inc(p_turned, 1)
                if not edge or 3 <= m < M + 3:
                    q, v = m - 3, (u - 3) % FU
                    e = expert(m, u, 3, edge)
                    pe.wait_ge(p_copied, q + 1)
                    if not edge or q >= 2:
                        pe.wait_ge(y_copied, q - 1)
                    pe.matmul(y_ps[v % 2][:, 0:D], at[0:FI, v, :], wd[0:FI, bass.ds(e, 1), :].rearrange("p o c -> p (o c)"),
                              start=True, stop=True).then_inc(y_done, 1)
            stepped(pe, step, 3)

        @block.scalar
        def _(act):
            def step(m, u, edge):
                if not edge or m < M:
                    act.wait_ge(x_turned, m + 1)
                    if not edge or m >= FU:
                        act.wait_ge(gu_done, m - FU + 1)
                    act.copy(xt[:, u].rearrange("p k t -> p (k t)"), x_ps[u % 2][:, 0:D]).then_inc(x_copied, 1)
                if not edge or 1 <= m < M + 1:
                    q, v = m - 1, (u - 1) % FU
                    act.wait_ge(gu_done, q + 1)
                    act.activation(sig[:, v, :], gu_ps[v % 2][:, 0:FI], ACT.Silu).then_inc(silu_done, 1)
                if not edge or 2 <= m < M + 2:
                    q, v = m - 2, (u - 2) % FU
                    act.wait_ge(p_turned, q + 1)
                    if not edge or q >= FU:
                        act.wait_ge(y_done, q - FU + 1)
                    act.copy(at[0:FI, v, :], p_ps[v % 2][0:FI, 0:P]).then_inc(p_copied, 1)
                if (not edge or STORE_LAG <= m < M + STORE_LAG) and (u - STORE_LAG) % 2 == 1:
                    q, v = m - STORE_LAG, (u - STORE_LAG) % FU
                    act.wait_ge(y_copied, q + 1)
                    act.sem_inc(store_go, 1)
                    act.dma_start(ydram[bass.ds((q - 1) * P, 2 * P), :].rearrange("(t p) d -> p t d", p=P),
                                  y[:, v - 1:v + 1, :]).then_inc(y_stored[v // 2], 16)
            stepped(act, step, STORE_LAG)

        @block.vector
        def _(dve):
            def step(m, u, edge):
                if not edge or 1 <= m < M + 1:
                    q, v = m - 1, (u - 1) % FU
                    dve.wait_ge(silu_done, q + 1)
                    if not edge or q >= FU:
                        dve.wait_ge(p_turned, q - FU + 1)
                    dve.tensor_tensor(act_out[:, v, :], gu_ps[v % 2][:, FI:2 * FI], sig[:, v, :], ALU.mult).then_inc(prod_done, 1)
                if not edge or 3 <= m < M + 3:
                    q, v = m - 3, (u - 3) % FU
                    dve.wait_ge(y_done, q + 1)
                    if not edge or q >= FU:
                        dve.wait_ge(y_stored[v // 2], (m - 3 - v) * (16 // FU))
                    dve.tensor_copy(y[:, v, :], y_ps[v % 2][:, 0:D]).then_inc(y_copied, 1)
            stepped(dve, step, 3)


def combine(nc, x_all, rows_dram, ydram, out, w4_all, pos_all):
    with ExitStack() as ctx:
        sb = lambda name, shape, dt=F32: ctx.enter_context(nc.sbuf_tensor(name, shape, dt))
        sem = lambda name: ctx.enter_context(nc.semaphore(name))
        CU = 4
        yg = [[sb(f"yg{u}_{j}", [P, D]) for j in range(TOPK)] for u in range(CU)]
        acc = sb("cacc", [P, CU, D])
        gb = sb("gb", [P, B, D])
        pos = [sb(f"pos{u}", [P, TOPK], U32) for u in range(CU)]
        w4 = sb("w4", [P, CU, TOPK])
        gb_loaded = sem("gb_loaded")
        y_gathered = [sem(f"y_gathered{u}") for u in range(CU)]
        stored = sem("out_stored")
        pos_done = sem("pos_done")
        w4_done = sem("w4c_done")
        summed = sem("summed")
        added = sem("added")
        gather_go = sem("gather_go2")
        block = ctx.enter_context(nc.Block())

        @block.sync
        def _(sp):
            sp.dma_start(gb[:].rearrange("p b d -> p (b d)"), rows_dram[0:1].rearrange("a b d -> a (b d)").broadcast_to([P, B * D])).then_inc(gb_loaded, 16)
            with sp.Fori(0, B) as b:
                for i in range(0, T, CU):
                    sp.wait_ge(added, b * T + i + CU)
                    sp.dma_start(out[bass.ds(b, 1), i * P:(i + CU) * P, :].rearrange("o (t p) d -> p (o t) d", p=P),
                                 x_all[:, bass.ds(b * T + i, CU), :]).then_inc(stored, 16)
            sp.wait_ge(stored, 16 * B * T // CU)

        @block.gpsimd
        def _(pool):
            with pool.Fori(0, B) as b:
                for i in range(T):
                    u = i % CU
                    pool.wait_ge(pos_done, b * T + i + 1)
                    pool.sem_inc(gather_go, 1)
                    for j in range(TOPK):
                        pool.indirect_dma_start(yg[u][j][:], None, ydram, bass.IndirectOffsetOnAxis(ap=pos[u][:, j:j + 1], axis=0)).then_inc(y_gathered[u], 16)

        @block.vector
        def _(dve):
            dve.wait_ge(gb_loaded, 16)

            def positions(t, u):
                dve.tensor_copy(w4[:, u, :], w4_all[:, bass.ds(t, 1), :].rearrange("p o j -> p (o j)")).then_inc(w4_done, 1)
                dve.tensor_copy(pos[u][:], pos_all[:, bass.ds(t, 1), :].rearrange("p o j -> p (o j)")).then_inc(pos_done, 1)

            for u in range(CU):
                positions(u, u)
            with dve.Fori(0, B) as b:
                for i in range(T):
                    u, t, n = i % CU, b * T + i, i * (TOPK + 1)
                    per = T * (TOPK + 1)
                    dve.wait_ge(w4_done, t + 1)
                    dve.wait_ge(y_gathered[u], b * (16 * TOPK * T // CU) + 16 * TOPK * (i // CU + 1))
                    dve.tensor_scalar(acc[:, u, :], yg[u][0][:], w4[:, u, 0:1], None, ALU.mult).then_inc(summed, 1)
                    for j in range(1, TOPK):
                        dve.wait_ge(summed, b * per + n + j)
                        dve.scalar_tensor_tensor(out=acc[:, u, :], in0=yg[u][j][:], scalar=w4[:, u, j:j + 1], in1=acc[:, u, :],
                                                 op0=ALU.mult, op1=ALU.add).then_inc(summed, 1)
                    dve.wait_ge(summed, b * per + n + TOPK)
                    dve.tensor_tensor(acc[:, u, :], acc[:, u, :], gb[:, bass.ds(b, 1), :].rearrange("p o d -> p (o d)"),
                                      ALU.mult).then_inc(summed, 1)
                    dve.wait_ge(summed, b * per + n + TOPK + 1)
                    x = x_all[:, bass.ds(t, 1), :].rearrange("p o d -> p (o d)")
                    dve.tensor_tensor(x, x, acc[:, u, :], ALU.add).then_inc(added, 1)
                    positions(t + CU, u)


def build(nc, x, wq, wk, wv, wo, hscale, rw, gw, uw, dw, c, wmod, cos, sin, ident, causal, tri, iota_e, ebase, iota_m, tokens, out):
    dram = lambda name, shape, dt=F32: nc.dram_tensor(name, shape, dt).ap()
    wsplit = dram("wsplit", [KV, P, 2 * WG])
    rows = dram("rows", [3, B, D])
    x1 = dram("x1", [B, N, D])
    h2 = dram("h2", [B, N, D])
    idtab = dram("idtab", [NTOK * E, 1], U32)
    ydram = dram("ydram", [NSLOT_TILES * P, D])
    with ExitStack() as ctx:
        modp = ctx.enter_context(nc.sbuf_tensor("modp", [P, 6, KD, B], F32))
        ident_sb = ctx.enter_context(nc.sbuf_tensor("ident_sb", [P, P], F32))
        attention(nc, x, wq, wk, wv, wo, hscale, c, wmod, cos, sin, ident, causal, rows, modp, wsplit, x1, ident_sb)
        route(nc, x1, rows, rw, gw, uw, dw, idtab, h2, ydram, out, tri, iota_e, ebase, iota_m, tokens, ident_sb)


_INS = ['L0_attn_x', 'L0_attn_Wq', 'L0_attn_Wk', 'L0_attn_Wv', 'L0_attn_Wo', 'L0_attn_head_scale', 'L0_ffn_router_w',
        'L0_ffn_gate_w', 'L0_ffn_up_w', 'L0_ffn_down_w', 'L0_c', 'L0_wmod']


def constants():
    import numpy as np
    inv = (np.float32(1.0) / np.power(np.float32(10000.0), np.arange(0, DH, 2, dtype=np.float32) / np.float32(DH))).astype(np.float32)
    freqs = np.arange(N, dtype=np.float32)[:, None] * inv[None, :]
    emb = np.concatenate((freqs, freqs), axis=-1).T
    root = float(DH) ** -0.25
    sign = np.where(np.arange(DH) < DH // 2, -1.0, 1.0)[:, None]
    cos = (np.cos(emb.astype(np.float64)) * root).astype(np.float32)
    sin = (np.sin(emb.astype(np.float64)) * sign * root).astype(np.float32)
    causal = np.where(np.arange(P)[None, :] <= np.arange(P)[:, None], 0.0, -3e38).astype(np.float32)
    rows = lambda a: np.ascontiguousarray(np.broadcast_to(np.asarray(a, np.float32)[None, :], (P, len(a))))
    return {"cos": cos, "sin": sin, "ident": np.eye(P, dtype=np.float32), "causal": causal,
            "tri": np.triu(np.ones((P, P), np.float32), 1), "iota_e": rows(np.arange(E)),
            "ebase": rows(np.arange(E) * NTOK), "iota_m": rows(np.arange(NSLOT_TILES)),
            "tokens": (np.arange(B * T)[None, :] * P + np.arange(P)[:, None]).astype(np.uint32)}


def kernel(**inputs):
    import numpy as _np
    import concourse.bacc as _bacc
    from concourse import mybir as _mybir
    from concourse.bass_utils import run_bass_kernel_spmd as _run

    nc = _bacc.Bacc("TRN2", target_bir_lowering=False, num_devices=1)
    arrays, args = {}, []
    given = {name: _np.ascontiguousarray(inputs[name]) for name in _INS}
    given.update(constants())
    for name, a in given.items():
        arrays[f"in_{name}_dram"] = a
        args.append(nc.dram_tensor(f"in_{name}_dram", a.shape, _mybir.dt.from_np(a.dtype), kind="ExternalInput").ap())
    args.append(nc.dram_tensor("out_0_dram", (B, N, D), _mybir.dt.float32, kind="ExternalOutput").ap())
    build(nc, *args)
    r = _run(nc, [arrays], core_ids=[0])
    return r.results[0]["out_0_dram"]
```
